# Optimizing a Trainium2 kernel written in Bass

```python
import numpy as np
import jax
import jax.numpy as jnp

def _softmax(x, axis=-1):
    return jax.nn.softmax(x, axis=axis)
def _gelu(x):
    return jax.nn.gelu(x, approximate=True)
def _silu(x):
    return jax.nn.silu(x)
def _sigmoid(x):
    return jax.nn.sigmoid(x)
def _layernorm(x, axis=-1, eps=1e-5):
    m = jnp.mean(x, axis=axis, keepdims=True)
    v = jnp.var(x, axis=axis, keepdims=True)
    return (x - m) / jnp.sqrt(v + eps)
def _scatter_add(tgt, idx, src, axis=0):
    return tgt.at[idx].add(src)
def _segment_sum(src, seg, n):
    return jax.ops.segment_sum(src, seg, n)

kernel_name = 'mk_conv_seq_d4_conv_nchw192_c4b22f'

def setup_inputs(seed: int = 0):
    np.random.seed(seed)
    _w = jnp.asarray
    def _rec_inputs():
        import jax
        import jax.numpy as jnp
        _gk = jax.random.key(seed)
        x = -0.0001538 + 1 * jax.random.normal(jax.random.fold_in(_gk, 1), (8, 192, 64, 64), jnp.float32)
        return x
    x = _rec_inputs()
    def _L0_conv_setup():
        import jax, jax.numpy as jnp
        import numpy as np
        from jax import lax
        EPS = 1e-05
        D_STATE = 16

        def layernorm_cf(x, g, b):
            mu = jnp.mean(x, axis=1, keepdims=True)
            v = jnp.var(x, axis=1, keepdims=True)
            return (x - mu) / jnp.sqrt(v + EPS) * g[None, :, None, None] + b[None, :, None, None]

        def conv1x1(x, w, b):
            return jnp.einsum('oc,bchw->bohw', w, x) + b[None, :, None, None]

        def dwconv3(x, w, b):
            y = lax.conv_general_dilated(x, w, (1, 1), 'SAME', dimension_numbers=('NCHW', 'OIHW', 'NCHW'), feature_group_count=x.shape[1])
            return y + b[None, :, None, None]

        def ss2d(x, x_proj_w, dt_proj_w, dt_proj_b, A_log, Dp):
            Bn, C, H, W = x.shape
            L = H * W
            R = dt_proj_w.shape[2]
            N = A_log.shape[2]
            x_hw = x.reshape(Bn, C, L)
            x_wh = jnp.swapaxes(x, 2, 3).reshape(Bn, C, L)
            xs = jnp.stack([x_hw, x_wh, x_hw[..., ::-1], x_wh[..., ::-1]], axis=1)
            x_dbl = jnp.einsum('kdc,bkcl->bkdl', x_proj_w, xs)
            dts, Bs, Cs = (x_dbl[:, :, :R], x_dbl[:, :, R:R + N], x_dbl[:, :, R + N:])
            dt = jax.nn.softplus(jnp.einsum('kcr,bkrl->bkcl', dt_proj_w, dts) + dt_proj_b[None, :, :, None])
            A = -jnp.exp(A_log)
            dt_l = jnp.moveaxis(dt, 3, 0)
            Bs_l = jnp.moveaxis(Bs, 3, 0)
            Cs_l = jnp.moveaxis(Cs, 3, 0)
            xs_l = jnp.moveaxis(xs, 3, 0)
            h0 = jnp.zeros((Bn, 4, C, N), x.dtype)

            def step(h, inp):
                dt_t, B_t, C_t, x_t = inp
                h = h * jnp.exp(dt_t[..., None] * A[None]) + (dt_t * x_t)[..., None] * B_t[:, :, None, :]
                return (h, jnp.einsum('bkcn,bkn->bkc', h, C_t))
            _, ys = lax.scan(step, h0, (dt_l, Bs_l, Cs_l, xs_l))
            ys = jnp.moveaxis(ys, 0, 3) + Dp[None, :, :, None] * xs
            y0 = ys[:, 0]
            y1 = jnp.swapaxes(ys[:, 1].reshape(Bn, C, W, H), 2, 3).reshape(Bn, C, L)
            y2 = ys[:, 2][..., ::-1]
            y3 = jnp.swapaxes(ys[:, 3][..., ::-1].reshape(Bn, C, W, H), 2, 3).reshape(Bn, C, L)
            return (y0 + y1 + y2 + y3).reshape(Bn, C, H, W)

        def channel_attn(y, w1, b1, w2, b2):
            p = jnp.mean(y, axis=(2, 3))
            s = jax.nn.sigmoid(jnp.einsum('oc,bc->bo', w2, jax.nn.relu(jnp.einsum('oc,bc->bo', w1, p) + b1)) + b2)
            return y * s[:, :, None, None]
        key = jax.random.key(seed)
        ks = jax.random.split(key, 20)
        B, C, H, W = (8, 192, 64, 64)
        N, R, K = (D_STATE, C // 16, 4)
        Cr = C // 16
        f = jnp.float32
        inp = {'x': jax.random.normal(ks[0], (B, C, H, W), f), 'ln_g': jnp.ones((C,), f), 'ln_b': jnp.zeros((C,), f), 'p1_w': jax.random.normal(ks[1], (C, C), f) * 0.02, 'p1_b': jnp.zeros((C,), f), 'p2in_w': jax.random.normal(ks[2], (C, C), f) * 0.02, 'p2in_b': jnp.zeros((C,), f), 'dw_w': jax.random.normal(ks[3], (C, 1, 3, 3), f) * 0.1, 'dw_b': jnp.zeros((C,), f), 'x_proj_w': jax.random.normal(ks[4], (K, R + 2 * N, C), f) * 0.02, 'dt_proj_w': jax.random.normal(ks[5], (K, C, R), f) * 0.1, 'dt_proj_b': jax.random.normal(ks[6], (K, C), f) * 0.1, 'A_log': jnp.log(jnp.tile(jnp.arange(1, N + 1, dtype=f), (K, C, 1))), 'Dp': jnp.ones((K, C), f), 'on_g': jnp.ones((C,), f), 'on_b': jnp.zeros((C,), f), 'ca_w1': jax.random.normal(ks[7], (Cr, C), f) * 0.05, 'ca_b1': jnp.zeros((Cr,), f), 'ca_w2': jax.random.normal(ks[8], (C, Cr), f) * 0.05, 'ca_b2': jnp.zeros((C,), f), 'block_idx': 0}
        return inp
    _L0_conv_all = _L0_conv_setup()
    _L0_conv_in = {k: v for k, v in _L0_conv_all.items() if k in ('ln_g', 'ln_b', 'p1_w', 'p1_b', 'p2in_w', 'p2in_b', 'dw_w', 'dw_b', 'x_proj_w', 'dt_proj_w', 'dt_proj_b', 'A_log', 'Dp', 'on_g', 'on_b', 'ca_w1', 'ca_b1', 'ca_w2', 'ca_b2', )}
    del _L0_conv_all

    def _L1_conv_setup():
        import jax, jax.numpy as jnp
        import numpy as np
        B, C, H, W = (4, 192, 128, 128)
        K = 4
        DSTATE = 8
        DTRANK = max(8, C // 16)
        EPS = 1e-05

        def _ln(x, w, b):
            mu = jnp.mean(x, axis=-1, keepdims=True)
            var = jnp.var(x, axis=-1, keepdims=True)
            return (x - mu) * jax.lax.rsqrt(var + EPS) * w + b
        key = jax.random.key(seed)
        ks = jax.random.split(key, 16)
        s_in = 1.0 / np.sqrt(C)
        inp = {'x': jax.random.normal(ks[0], (B, C, H, W), jnp.float32), 'norm_w': 1.0 + 0.02 * jax.random.normal(ks[1], (C,), jnp.float32), 'norm_b': 0.02 * jax.random.normal(ks[2], (C,), jnp.float32), 'w_in': s_in * jax.random.normal(ks[3], (2 * C, C), jnp.float32), 'ssm_in_w': s_in * jax.random.normal(ks[4], (2 * C, C), jnp.float32), 'x_proj_w': s_in * jax.random.normal(ks[5], (K, DTRANK + 2 * DSTATE, C), jnp.float32), 'dt_w': 1.0 / np.sqrt(DTRANK) * jax.random.normal(ks[6], (K, C, DTRANK), jnp.float32), 'dt_b': 0.1 * jax.random.normal(ks[7], (K, C), jnp.float32), 'A_logs': jnp.log(jnp.broadcast_to(jnp.arange(1, DSTATE + 1, dtype=jnp.float32), (K * C, DSTATE))), 'Ds': jnp.ones((K * C,), jnp.float32), 'out_norm_w': 1.0 + 0.02 * jax.random.normal(ks[8], (C,), jnp.float32), 'out_norm_b': 0.02 * jax.random.normal(ks[9], (C,), jnp.float32), 'ssm_out_w': s_in * jax.random.normal(ks[10], (C, C), jnp.float32), 'w_out': s_in * jax.random.normal(ks[11], (C, C), jnp.float32)}
        return inp
    _L1_conv_all = _L1_conv_setup()
    _L1_conv_in = {k: v for k, v in _L1_conv_all.items() if k in ('norm_w', 'norm_b', 'w_in', 'ssm_in_w', 'x_proj_w', 'dt_w', 'dt_b', 'A_logs', 'Ds', 'out_norm_w', 'out_norm_b', 'ssm_out_w', 'w_out', )}
    del _L1_conv_all

    def _L2_conv_setup():
        import jax, jax.numpy as jnp
        import numpy as np
        B_SZ, D_IN, H_SZ, W_SZ = (8, 192, 64, 64)
        N_ST, R_DT, K_GRP = (16, 6, 4)
        LN_EPS = 1e-05

        def _ss2d(x, x_proj_weight, dt_projs_weight, dt_projs_bias, A_logs, Ds, ln_g, ln_b):
            B, D, H, W = x.shape
            L = H * W
            K = x_proj_weight.shape[0]
            N = A_logs.shape[1]
            R = dt_projs_weight.shape[2]
            x0 = x.reshape(B, D, L)
            x1 = x.transpose(0, 1, 3, 2).reshape(B, D, L)
            xs = jnp.stack([x0, x1, x0[..., ::-1], x1[..., ::-1]], axis=1)
            x_dbl = jnp.einsum('bkdl,kcd->bkcl', xs, x_proj_weight)
            dts, Bs, Cs = jnp.split(x_dbl, [R, R + N], axis=2)
            dts = jnp.einsum('bkrl,kdr->bkdl', dts, dt_projs_weight)
            A = -jnp.exp(A_logs.astype(jnp.float32)).reshape(K, D, N)
            delta = jax.nn.softplus(dts + dt_projs_bias[None, :, :, None])

            def step(h, inp):
                u_t, d_t, B_t, C_t = inp
                h = jnp.exp(d_t[..., None] * A) * h + (d_t * u_t)[..., None] * B_t[:, :, None, :]
                y = jnp.einsum('bkdn,bkn->bkd', h, C_t)
                return (h, y)
            h0 = jnp.zeros((B, K, D, N), dtype=jnp.float32)
            seq = (xs.transpose(3, 0, 1, 2), delta.transpose(3, 0, 1, 2), Bs.transpose(3, 0, 1, 2), Cs.transpose(3, 0, 1, 2))
            _, ys = jax.lax.scan(step, h0, seq)
            ys = ys.transpose(1, 2, 3, 0) + Ds.reshape(K, D)[None, :, :, None] * xs
            ym = ys[:, 0:2] + ys[:, 2:4][..., ::-1]
            y = ym[:, 0] + ym[:, 1].reshape(B, D, W, H).transpose(0, 1, 3, 2).reshape(B, D, L)
            y = y.reshape(B, D, H, W)
            mean = jnp.mean(y, axis=1, keepdims=True)
            var = jnp.var(y, axis=1, keepdims=True)
            return (y - mean) / jnp.sqrt(var + LN_EPS) * ln_g + ln_b
        key = jax.random.key(seed)
        ks = jax.random.split(key, 6)
        x = jax.random.normal(ks[0], (B_SZ, D_IN, H_SZ, W_SZ), dtype=jnp.float32)
        x_proj_weight = jax.random.normal(ks[1], (K_GRP, R_DT + 2 * N_ST, D_IN), dtype=jnp.float32) * 0.02
        dt_projs_weight = jax.random.normal(ks[2], (K_GRP, D_IN, R_DT), dtype=jnp.float32) * R_DT ** (-0.5)
        dt_projs_bias = jax.random.normal(ks[3], (K_GRP, D_IN), dtype=jnp.float32) * 0.1
        A_logs = jnp.log(jnp.tile(jnp.arange(1, N_ST + 1, dtype=jnp.float32), (K_GRP * D_IN, 1)))
        Ds = jnp.ones((K_GRP * D_IN,), dtype=jnp.float32)
        ln_g = jnp.ones((1, D_IN, 1, 1), dtype=jnp.float32)
        ln_b = jnp.zeros((1, D_IN, 1, 1), dtype=jnp.float32)
        return dict(x=x, x_proj_weight=x_proj_weight, dt_projs_weight=dt_projs_weight, dt_projs_bias=dt_projs_bias, A_logs=A_logs, Ds=Ds, ln_g=ln_g, ln_b=ln_b)
    _L2_conv_all = _L2_conv_setup()
    _L2_conv_in = {k: v for k, v in _L2_conv_all.items() if k in ('x_proj_weight', 'dt_projs_weight', 'dt_projs_bias', 'A_logs', 'Ds', 'ln_g', 'ln_b', )}
    del _L2_conv_all

    def _L3_conv_setup():
        import jax, jax.numpy as jnp
        import numpy as np
        from jax import lax
        C_IN = 192
        NUM_WINDOWS = 8
        WINDOWS = [NUM_WINDOWS // 2, NUM_WINDOWS, NUM_WINDOWS + NUM_WINDOWS // 2]
        CB = C_IN // len(WINDOWS)

        def _conv1x1(x, w, b=None):
            y = jnp.einsum('nchw,oc->nohw', x, w)
            if b is not None:
                y = y + b[None, :, None, None]
            return y

        def _se(x, wse1, wse2):
            y = jnp.mean(x, axis=(2, 3))
            y = jax.nn.relu(jnp.einsum('bc,oc->bo', y, wse1))
            y = jax.nn.sigmoid(jnp.einsum('bc,oc->bo', y, wse2))
            return x * y[:, :, None, None]

        def _dwconv3x3(x, w, b):
            y = lax.conv_general_dilated(x, w, window_strides=(1, 1), padding=((1, 1), (1, 1)), feature_group_count=CB, dimension_numbers=('NCHW', 'OIHW', 'NCHW'))
            return y + b[None, :, None, None]
        key = jax.random.key(seed)
        ks = jax.random.split(key, 8)
        N, H, W = (16, 100, 100)
        rn = lambda k, s, sc: jax.random.normal(k, s, jnp.float32) * sc
        return {'x': rn(ks[0], (N, C_IN, H, W), 1.0), 'w1': rn(ks[1], (CB, C_IN), 0.05), 'b1': jnp.zeros((CB,), jnp.float32), 'w2': rn(ks[2], (CB, CB), 0.05), 'b2': jnp.zeros((CB,), jnp.float32), 'w3': rn(ks[3], (C_IN, 3 * CB), 0.05), 'b3': jnp.zeros((C_IN,), jnp.float32), 'wpos': rn(ks[4], (CB, 1, 3, 3), 0.1), 'bpos': jnp.zeros((CB,), jnp.float32), 'wse1': rn(ks[5], (CB // 16, CB), 0.1), 'wse2': rn(ks[6], (CB, CB // 16), 0.1)}
    _L3_conv_all = _L3_conv_setup()
    _L3_conv_in = {k: v for k, v in _L3_conv_all.items() if k in ('w1', 'b1', 'w2', 'b2', 'w3', 'b3', 'wpos', 'bpos', 'wse1', 'wse2', )}
    del _L3_conv_all

    return {
        "x": x,
        "L0_conv_ln_g": _L0_conv_in["ln_g"],
        "L0_conv_ln_b": _L0_conv_in["ln_b"],
        "L0_conv_p1_w": _L0_conv_in["p1_w"],
        "L0_conv_p1_b": _L0_conv_in["p1_b"],
        "L0_conv_p2in_w": _L0_conv_in["p2in_w"],
        "L0_conv_p2in_b": _L0_conv_in["p2in_b"],
        "L0_conv_dw_w": _L0_conv_in["dw_w"],
        "L0_conv_dw_b": _L0_conv_in["dw_b"],
        "L0_conv_x_proj_w": _L0_conv_in["x_proj_w"],
        "L0_conv_dt_proj_w": _L0_conv_in["dt_proj_w"],
        "L0_conv_dt_proj_b": _L0_conv_in["dt_proj_b"],
        "L0_conv_A_log": _L0_conv_in["A_log"],
        "L0_conv_Dp": _L0_conv_in["Dp"],
        "L0_conv_on_g": _L0_conv_in["on_g"],
        "L0_conv_on_b": _L0_conv_in["on_b"],
        "L0_conv_ca_w1": _L0_conv_in["ca_w1"],
        "L0_conv_ca_b1": _L0_conv_in["ca_b1"],
        "L0_conv_ca_w2": _L0_conv_in["ca_w2"],
        "L0_conv_ca_b2": _L0_conv_in["ca_b2"],
        "L1_conv_norm_w": _L1_conv_in["norm_w"],
        "L1_conv_norm_b": _L1_conv_in["norm_b"],
        "L1_conv_w_in": _L1_conv_in["w_in"],
        "L1_conv_ssm_in_w": _L1_conv_in["ssm_in_w"],
        "L1_conv_x_proj_w": _L1_conv_in["x_proj_w"],
        "L1_conv_dt_w": _L1_conv_in["dt_w"],
        "L1_conv_dt_b": _L1_conv_in["dt_b"],
        "L1_conv_A_logs": _L1_conv_in["A_logs"],
        "L1_conv_Ds": _L1_conv_in["Ds"],
        "L1_conv_out_norm_w": _L1_conv_in["out_norm_w"],
        "L1_conv_out_norm_b": _L1_conv_in["out_norm_b"],
        "L1_conv_ssm_out_w": _L1_conv_in["ssm_out_w"],
        "L1_conv_w_out": _L1_conv_in["w_out"],
        "L2_conv_x_proj_weight": _L2_conv_in["x_proj_weight"],
        "L2_conv_dt_projs_weight": _L2_conv_in["dt_projs_weight"],
        "L2_conv_dt_projs_bias": _L2_conv_in["dt_projs_bias"],
        "L2_conv_A_logs": _L2_conv_in["A_logs"],
        "L2_conv_Ds": _L2_conv_in["Ds"],
        "L2_conv_ln_g": _L2_conv_in["ln_g"],
        "L2_conv_ln_b": _L2_conv_in["ln_b"],
        "L3_conv_w1": _L3_conv_in["w1"],
        "L3_conv_b1": _L3_conv_in["b1"],
        "L3_conv_w2": _L3_conv_in["w2"],
        "L3_conv_b2": _L3_conv_in["b2"],
        "L3_conv_w3": _L3_conv_in["w3"],
        "L3_conv_b3": _L3_conv_in["b3"],
        "L3_conv_wpos": _L3_conv_in["wpos"],
        "L3_conv_bpos": _L3_conv_in["bpos"],
        "L3_conv_wse1": _L3_conv_in["wse1"],
        "L3_conv_wse2": _L3_conv_in["wse2"],
    }

def reference(x, L0_conv_ln_g, L0_conv_ln_b, L0_conv_p1_w, L0_conv_p1_b, L0_conv_p2in_w, L0_conv_p2in_b, L0_conv_dw_w, L0_conv_dw_b, L0_conv_x_proj_w, L0_conv_dt_proj_w, L0_conv_dt_proj_b, L0_conv_A_log, L0_conv_Dp, L0_conv_on_g, L0_conv_on_b, L0_conv_ca_w1, L0_conv_ca_b1, L0_conv_ca_w2, L0_conv_ca_b2, L1_conv_norm_w, L1_conv_norm_b, L1_conv_w_in, L1_conv_ssm_in_w, L1_conv_x_proj_w, L1_conv_dt_w, L1_conv_dt_b, L1_conv_A_logs, L1_conv_Ds, L1_conv_out_norm_w, L1_conv_out_norm_b, L1_conv_ssm_out_w, L1_conv_w_out, L2_conv_x_proj_weight, L2_conv_dt_projs_weight, L2_conv_dt_projs_bias, L2_conv_A_logs, L2_conv_Ds, L2_conv_ln_g, L2_conv_ln_b, L3_conv_w1, L3_conv_b1, L3_conv_w2, L3_conv_b2, L3_conv_w3, L3_conv_b3, L3_conv_wpos, L3_conv_bpos, L3_conv_wse1, L3_conv_wse2):
    import jax
    import jax.numpy as jnp
    def _L0_conv_ref(x, ln_g, ln_b, p1_w, p1_b, p2in_w, p2in_b, dw_w, dw_b, x_proj_w, dt_proj_w, dt_proj_b, A_log, Dp, on_g, on_b, ca_w1, ca_b1, ca_w2, ca_b2, block_idx):
        import jax, jax.numpy as jnp
        import numpy as np
        from jax import lax
        EPS = 1e-05
        D_STATE = 16

        def layernorm_cf(x, g, b):
            mu = jnp.mean(x, axis=1, keepdims=True)
            v = jnp.var(x, axis=1, keepdims=True)
            return (x - mu) / jnp.sqrt(v + EPS) * g[None, :, None, None] + b[None, :, None, None]

        def conv1x1(x, w, b):
            return jnp.einsum('oc,bchw->bohw', w, x) + b[None, :, None, None]

        def dwconv3(x, w, b):
            y = lax.conv_general_dilated(x, w, (1, 1), 'SAME', dimension_numbers=('NCHW', 'OIHW', 'NCHW'), feature_group_count=x.shape[1])
            return y + b[None, :, None, None]

        def ss2d(x, x_proj_w, dt_proj_w, dt_proj_b, A_log, Dp):
            Bn, C, H, W = x.shape
            L = H * W
            R = dt_proj_w.shape[2]
            N = A_log.shape[2]
            x_hw = x.reshape(Bn, C, L)
            x_wh = jnp.swapaxes(x, 2, 3).reshape(Bn, C, L)
            xs = jnp.stack([x_hw, x_wh, x_hw[..., ::-1], x_wh[..., ::-1]], axis=1)
            x_dbl = jnp.einsum('kdc,bkcl->bkdl', x_proj_w, xs)
            dts, Bs, Cs = (x_dbl[:, :, :R], x_dbl[:, :, R:R + N], x_dbl[:, :, R + N:])
            dt = jax.nn.softplus(jnp.einsum('kcr,bkrl->bkcl', dt_proj_w, dts) + dt_proj_b[None, :, :, None])
            A = -jnp.exp(A_log)
            dt_l = jnp.moveaxis(dt, 3, 0)
            Bs_l = jnp.moveaxis(Bs, 3, 0)
            Cs_l = jnp.moveaxis(Cs, 3, 0)
            xs_l = jnp.moveaxis(xs, 3, 0)
            h0 = jnp.zeros((Bn, 4, C, N), x.dtype)

            def step(h, inp):
                dt_t, B_t, C_t, x_t = inp
                h = h * jnp.exp(dt_t[..., None] * A[None]) + (dt_t * x_t)[..., None] * B_t[:, :, None, :]
                return (h, jnp.einsum('bkcn,bkn->bkc', h, C_t))
            _, ys = lax.scan(step, h0, (dt_l, Bs_l, Cs_l, xs_l))
            ys = jnp.moveaxis(ys, 0, 3) + Dp[None, :, :, None] * xs
            y0 = ys[:, 0]
            y1 = jnp.swapaxes(ys[:, 1].reshape(Bn, C, W, H), 2, 3).reshape(Bn, C, L)
            y2 = ys[:, 2][..., ::-1]
            y3 = jnp.swapaxes(ys[:, 3][..., ::-1].reshape(Bn, C, W, H), 2, 3).reshape(Bn, C, L)
            return (y0 + y1 + y2 + y3).reshape(Bn, C, H, W)

        def channel_attn(y, w1, b1, w2, b2):
            p = jnp.mean(y, axis=(2, 3))
            s = jax.nn.sigmoid(jnp.einsum('oc,bc->bo', w2, jax.nn.relu(jnp.einsum('oc,bc->bo', w1, p) + b1)) + b2)
            return y * s[:, :, None, None]
        h = layernorm_cf(x, ln_g, ln_b)
        a = jax.nn.silu(conv1x1(h, p1_w, p1_b))
        b = jax.nn.silu(dwconv3(conv1x1(h, p2in_w, p2in_b), dw_w, dw_b))
        if block_idx % 2 == 0:
            b = jnp.swapaxes(b, 2, 3)
        else:
            b = b[:, :, ::-1, ::-1]
        b = ss2d(b, x_proj_w, dt_proj_w, dt_proj_b, A_log, Dp)
        if block_idx % 2 == 0:
            b = jnp.swapaxes(b, 2, 3)
        else:
            b = b[:, :, ::-1, ::-1]
        b = layernorm_cf(b, on_g, on_b)
        y = channel_attn(a * b, ca_w1, ca_b1, ca_w2, ca_b2)
        return x + y

    def _L1_conv_ref(x, norm_w, norm_b, w_in, ssm_in_w, x_proj_w, dt_w, dt_b, A_logs, Ds, out_norm_w, out_norm_b, ssm_out_w, w_out):
        import jax, jax.numpy as jnp
        import numpy as np
        B, C, H, W = (4, 192, 128, 128)
        K = 4
        DSTATE = 8
        DTRANK = max(8, C // 16)
        EPS = 1e-05

        def _ln(x, w, b):
            mu = jnp.mean(x, axis=-1, keepdims=True)
            var = jnp.var(x, axis=-1, keepdims=True)
            return (x - mu) * jax.lax.rsqrt(var + EPS) * w + b
        xh = jnp.transpose(x, (0, 2, 3, 1))
        xn = _ln(xh, norm_w, norm_b)
        p = xn @ w_in.T
        x1, x2 = (p[..., :C], p[..., C:])
        u = x1 @ ssm_in_w.T
        xss, z = (u[..., :C], u[..., C:])
        z = jax.nn.silu(z)
        xss = jax.nn.silu(xss)
        xd = jnp.einsum('bhwd,kcd->bhwkc', xss, x_proj_w)
        dtr = xd[..., :DTRANK]
        Bv = xd[..., DTRANK:DTRANK + DSTATE]
        Cv = xd[..., DTRANK + DSTATE:]
        dt = jax.nn.softplus(jnp.einsum('bhwkr,kdr->bhwkd', dtr, dt_w) + dt_b)
        bc = jnp.sum(Bv * Cv, axis=-1)
        gain = jnp.sum(bc[..., None] * dt + Ds.reshape(K, C), axis=-2)
        y = xss * gain
        y = _ln(y, out_norm_w, out_norm_b)
        y = y * z
        s = y @ ssm_out_w.T
        o = s * jax.nn.silu(x2) @ w_out.T
        return x + jnp.transpose(o, (0, 3, 1, 2))

    def _L2_conv_ref(x, x_proj_weight, dt_projs_weight, dt_projs_bias, A_logs, Ds, ln_g, ln_b):
        import jax, jax.numpy as jnp
        import numpy as np
        B_SZ, D_IN, H_SZ, W_SZ = (8, 192, 64, 64)
        N_ST, R_DT, K_GRP = (16, 6, 4)
        LN_EPS = 1e-05

        def _ss2d(x, x_proj_weight, dt_projs_weight, dt_projs_bias, A_logs, Ds, ln_g, ln_b):
            B, D, H, W = x.shape
            L = H * W
            K = x_proj_weight.shape[0]
            N = A_logs.shape[1]
            R = dt_projs_weight.shape[2]
            x0 = x.reshape(B, D, L)
            x1 = x.transpose(0, 1, 3, 2).reshape(B, D, L)
            xs = jnp.stack([x0, x1, x0[..., ::-1], x1[..., ::-1]], axis=1)
            x_dbl = jnp.einsum('bkdl,kcd->bkcl', xs, x_proj_weight)
            dts, Bs, Cs = jnp.split(x_dbl, [R, R + N], axis=2)
            dts = jnp.einsum('bkrl,kdr->bkdl', dts, dt_projs_weight)
            A = -jnp.exp(A_logs.astype(jnp.float32)).reshape(K, D, N)
            delta = jax.nn.softplus(dts + dt_projs_bias[None, :, :, None])

            def step(h, inp):
                u_t, d_t, B_t, C_t = inp
                h = jnp.exp(d_t[..., None] * A) * h + (d_t * u_t)[..., None] * B_t[:, :, None, :]
                y = jnp.einsum('bkdn,bkn->bkd', h, C_t)
                return (h, y)
            h0 = jnp.zeros((B, K, D, N), dtype=jnp.float32)
            seq = (xs.transpose(3, 0, 1, 2), delta.transpose(3, 0, 1, 2), Bs.transpose(3, 0, 1, 2), Cs.transpose(3, 0, 1, 2))
            _, ys = jax.lax.scan(step, h0, seq)
            ys = ys.transpose(1, 2, 3, 0) + Ds.reshape(K, D)[None, :, :, None] * xs
            ym = ys[:, 0:2] + ys[:, 2:4][..., ::-1]
            y = ym[:, 0] + ym[:, 1].reshape(B, D, W, H).transpose(0, 1, 3, 2).reshape(B, D, L)
            y = y.reshape(B, D, H, W)
            mean = jnp.mean(y, axis=1, keepdims=True)
            var = jnp.var(y, axis=1, keepdims=True)
            return (y - mean) / jnp.sqrt(var + LN_EPS) * ln_g + ln_b
        return _ss2d(x, x_proj_weight, dt_projs_weight, dt_projs_bias, A_logs, Ds, ln_g, ln_b)

    def _L3_conv_ref(x, w1, b1, w2, b2, w3, b3, wpos, bpos, wse1, wse2):
        import jax, jax.numpy as jnp
        import numpy as np
        from jax import lax
        C_IN = 192
        NUM_WINDOWS = 8
        WINDOWS = [NUM_WINDOWS // 2, NUM_WINDOWS, NUM_WINDOWS + NUM_WINDOWS // 2]
        CB = C_IN // len(WINDOWS)

        def _conv1x1(x, w, b=None):
            y = jnp.einsum('nchw,oc->nohw', x, w)
            if b is not None:
                y = y + b[None, :, None, None]
            return y

        def _se(x, wse1, wse2):
            y = jnp.mean(x, axis=(2, 3))
            y = jax.nn.relu(jnp.einsum('bc,oc->bo', y, wse1))
            y = jax.nn.sigmoid(jnp.einsum('bc,oc->bo', y, wse2))
            return x * y[:, :, None, None]

        def _dwconv3x3(x, w, b):
            y = lax.conv_general_dilated(x, w, window_strides=(1, 1), padding=((1, 1), (1, 1)), feature_group_count=CB, dimension_numbers=('NCHW', 'OIHW', 'NCHW'))
            return y + b[None, :, None, None]
        xc = _conv1x1(x, w1, b1)
        N, C, H, W = xc.shape
        out_list = []
        for nw in WINDOWS:
            s = H // nw
            k = s + H % nw
            hi = (jnp.arange(nw) * s)[:, None] + jnp.arange(k)[None, :]
            patches = xc[:, :, hi][..., hi]
            u3 = patches.transpose(0, 1, 3, 5, 2, 4).reshape(N, C * k * k, nw * nw)
            u4 = u3.reshape(-1, C, k, k)
            a = _se(_conv1x1(u4, w2, b2), wse1, wse2) + _dwconv3x3(u4, wpos, bpos)
            a3 = a.reshape(N, C * k * k, nw * nw)
            p = a3.reshape(N, C, k, k, nw, nw).transpose(0, 1, 4, 2, 5, 3)
            hidx = hi[:, :, None, None]
            widx = hi[None, None, :, :]
            folded = jnp.zeros((N, C, H, W), xc.dtype).at[:, :, hidx, widx].add(p)
            cnt = jnp.zeros((H, W), xc.dtype).at[hidx, widx].add(jnp.ones((nw, k, nw, k), xc.dtype))
            out_list.append(folded / cnt[None, None, :, :])
        out = _conv1x1(jnp.concatenate(out_list, axis=1) + x, w3, b3)
        return out

    def _gn(v, G=32, eps=1e-5):
        B_, C_, H_, W_ = v.shape
        g = v.reshape(B_, G, C_ // G, H_, W_)
        m = jnp.mean(g, axis=(2, 3, 4), keepdims=True)
        s = jnp.var(g, axis=(2, 3, 4), keepdims=True)
        return ((g - m) / jnp.sqrt(s + eps)).reshape(v.shape)

    def _ln_c(v, eps=1e-6):
        m = jnp.mean(v, axis=1, keepdims=True)
        s = jnp.var(v, axis=1, keepdims=True)
        return (v - m) / jnp.sqrt(s + eps)

    def _ln_t(v, eps=1e-5):
        m = jnp.mean(v, axis=-1, keepdims=True)
        s = jnp.var(v, axis=-1, keepdims=True)
        return (v - m) / jnp.sqrt(s + eps)

    def _to_tokens(v):
        B_, C_, H_, W_ = v.shape
        return v.reshape(B_, C_, H_ * W_).transpose(0, 2, 1)
    def _from_tokens(t, like):
        B_, C_, H_, W_ = like.shape
        return t.transpose(0, 2, 1).reshape(B_, C_, H_, W_)

    x = _L0_conv_ref(x, L0_conv_ln_g, L0_conv_ln_b, L0_conv_p1_w, L0_conv_p1_b, L0_conv_p2in_w, L0_conv_p2in_b, L0_conv_dw_w, L0_conv_dw_b, L0_conv_x_proj_w, L0_conv_dt_proj_w, L0_conv_dt_proj_b, L0_conv_A_log, L0_conv_Dp, L0_conv_on_g, L0_conv_on_b, L0_conv_ca_w1, L0_conv_ca_b1, L0_conv_ca_w2, L0_conv_ca_b2, 0)
    x = _L1_conv_ref(x, L1_conv_norm_w, L1_conv_norm_b, L1_conv_w_in, L1_conv_ssm_in_w, L1_conv_x_proj_w, L1_conv_dt_w, L1_conv_dt_b, L1_conv_A_logs, L1_conv_Ds, L1_conv_out_norm_w, L1_conv_out_norm_b, L1_conv_ssm_out_w, L1_conv_w_out)
    x = _L2_conv_ref(x, L2_conv_x_proj_weight, L2_conv_dt_projs_weight, L2_conv_dt_projs_bias, L2_conv_A_logs, L2_conv_Ds, L2_conv_ln_g, L2_conv_ln_b)
    x = _L3_conv_ref(x, L3_conv_w1, L3_conv_b1, L3_conv_w2, L3_conv_b2, L3_conv_w3, L3_conv_b3, L3_conv_wpos, L3_conv_bpos, L3_conv_wse1, L3_conv_wse2)
    return x


_drawn_inputs = setup_inputs


def setup_inputs(seed=0):
    import zlib

    import numpy as np

    out = dict(_drawn_inputs(seed))
    spreads = {'L0_conv_ln_g': (1.0, 0.6),
     'L0_conv_ln_b': (0.0, 0.8),
     'L0_conv_p1_b': (0.0, 0.1),
     'L0_conv_p2in_b': (0.0, 0.55),
     'L0_conv_dw_b': (0.0, 0.1),
     'L0_conv_Dp': (1.0, 0.6),
     'L0_conv_on_g': (1.0, 0.6),
     'L0_conv_on_b': (0.0, 0.8),
     'L0_conv_ca_b1': (0.0, 0.8),
     'L0_conv_ca_b2': (0.0, 0.8),
     'L1_conv_Ds': (1.0, 0.6),
     'L2_conv_Ds': (1.0, 0.6),
     'L2_conv_ln_g': (1.0, 0.2),
     'L2_conv_ln_b': (0.0, 0.1),
     'L3_conv_b1': (0.0, 0.296),
     'L3_conv_b2': (0.0, 0.1),
     'L3_conv_b3': (0.0, 0.1),
     'L3_conv_bpos': (0.0, 0.1)}
    factors = {'L0_conv_x_proj_w': 8.0,
     'L0_conv_dt_proj_w': 8.0,
     'L0_conv_dt_proj_b': 8.0,
     'L0_conv_A_log': 21.709,
     'L0_conv_ca_w1': 8.0,
     'L0_conv_ca_w2': 8.0,
     'L1_conv_norm_w': 4.624,
     'L1_conv_norm_b': 4.953,
     'L1_conv_dt_b': 5.58,
     'L1_conv_out_norm_w': 8.0,
     'L1_conv_out_norm_b': 8.0,
     'L2_conv_dt_projs_bias': 6.869,
     'L2_conv_A_logs': 3.871,
     'L3_conv_wse1': 8.0,
     'L3_conv_wse2': 8.0}
    for name, (base, spread) in spreads.items():
        noise = np.random.default_rng([zlib.crc32(name.encode()), seed]).standard_normal(out[name].shape)
        drawn = base * np.exp(spread * noise) if base else spread * noise
        out[name] = jnp.asarray(drawn.astype(out[name].dtype))
    for name, factor in factors.items():
        out[name] = (out[name] * factor).astype(out[name].dtype)
    return out
```

```python
from collections import namedtuple
from contextlib import ExitStack

import numpy as np
import concourse.bass as bass
from concourse import mybir

ALU = mybir.AluOpType
ACT = mybir.ActivationFunctionType
AX = mybir.AxisListType
F32 = mybir.dt.float32
BF16 = mybir.dt.bfloat16

NIMG, C, H, W = 8, 192, 64, 64
L = H * W
HC = C // 2
T = 512
NCH = L // T
ROWS = T // W
K = 4
NS = 16
CG = 128 // NS
NG = C // CG
NGH = NG // 2
NQ = C // 32
PADW = W + 2
EPS = 1e-5
SMALL = 0.00390625
CB = 64
WINS = ((4, 16, 16), (8, 8, 8), (12, 5, 9))
DTR1, DS1 = 12, 8


def columns(spec):
    out, at = {}, 0
    for name, n in spec:
        out[name] = (at, at + n)
        at += n
    return out, at


PRE_W, PRE_N = columns([("p1", 2 * C), ("p2", 2 * C), ("g", 2), ("b", 2), ("p1b", 2), ("p2b", 2),
                        ("dw", 18), ("dwb", 2), ("D", 2 * K), ("mean", HC)])
SCAN_W, SCAN_N = columns([("wb", 2 * K * 128), ("wc", 2 * K * 128), ("dtb", 2 * K)])
RANK_N = 2 * K * C
L1_W, L1_N = columns([("win", 2 * C), ("ssmin", 4 * C), ("wx2", 2 * C), ("xb", 2 * 32), ("xc", 2 * 32),
                      ("xd", 2 * K * DTR1), ("dtb", 2 * K), ("D", 2 * K), ("g", 2), ("b", 2),
                      ("og", 2), ("ob", 2), ("so", 2 * C), ("wo", 2 * C), ("mean", HC),
                      ("l0g", 2), ("l0b", 2), ("ca1", 2 * 12)])
L3_W, L3_N = columns([("w1", 2 * 2 * CB), ("w3x", 2 * C), ("b3", 2), ("g", 2), ("b", 2), ("mean", HC)])
L3B_W, L3B_N = columns([("w2", 128), ("se1", 8), ("b2", 1), ("dw", 9), ("dwb", 1), ("w3c", 3 * C), ("b1", 1)])


def semaphores(nc, stack, names):
    names = names.split()
    return namedtuple("Semaphores", names)(*[stack.enter_context(nc.semaphore(n)) for n in names])


def end_phase(nc, sems):
    for s in sems:
        nc.gpsimd.sem_clear(s)
    nc.all_engine_barrier()


class Carver:

    def __init__(self, arena):
        self.arena, self.at = arena, 0

    def take(self, partitions, n):
        a = self.arena[0:partitions, self.at:self.at + n]
        self.at += n
        assert self.at <= self.arena.shape[1], self.at
        return a


def halves(ap, n):
    return ap.rearrange("p (h t) -> p h t", h=2, t=n)


def chunk(ap3, i):
    return ap3[:, :, bass.ds(i * T, T)]


def top_half(ap):
    if len(ap.shape) == 2:
        return ap.bitcast(BF16).rearrange("p (t two) -> p t two", two=2)[:, :, 1]
    return ap.bitcast(BF16).rearrange("p h (t two) -> p h t two", two=2)[:, :, :, 1]


def conv192(pe, ps, banks, w, x, first=True, last=True):
    for j, bank in enumerate(banks):
        for h in range(2):
            m = pe.matmul(ps[0:HC, bank, :], w[:, h, j * HC:(j + 1) * HC], x[:, h, :],
                          start=first and h == 0, stop=last and h == 1)
    return m


LN_SEMS = "ln_mean ln_centered ln_square ln_var ln_std ln_rstd ln_normed ln_out"


def ln_pe(pe, S, i, ps, ones, x, sq):
    for h in range(2):
        m = pe.matmul(ps[0:HC, 0, :], ones, x[:, h, :], start=h == 0, stop=h == 1)
    m.then_inc(S.ln_mean, 1)
    pe.wait_ge(S.ln_square, i + 1)
    for h in range(2):
        m = pe.matmul(ps[0:HC, 1, :], ones, sq[:, h, :], start=h == 0, stop=h == 1)
    m.then_inc(S.ln_var, 1)


def ln_dve(v, S, i, ps, x, xc, rstd, gain):
    v.wait_ge(S.ln_mean, i + 1)
    for h in range(2):
        m = v.tensor_tensor(xc[:, h, :], x[:, h, :], ps[0:HC, 0, :], ALU.subtract)
    m.then_inc(S.ln_centered, 1)
    v.wait_ge(S.ln_std, i + 1)
    v.reciprocal(rstd, rstd).then_inc(S.ln_rstd, 1)
    v.wait_ge(S.ln_rstd, i + 1)
    for h in range(2):
        m = v.scalar_tensor_tensor(xc[:, h, :], xc[:, h, :], gain[:, h:h + 1], rstd, ALU.mult, ALU.mult)
    m.then_inc(S.ln_normed, 1)


def ln_act(act, S, i, ps, xc, sq, rstd, eps, bias, out):
    act.wait_ge(S.ln_centered, i + 1)
    act.activation(sq, xc, ACT.Square).then_inc(S.ln_square, 1)
    act.wait_ge(S.ln_var, i + 1)
    act.activation(rstd, ps[0:HC, 1, :], ACT.Sqrt, bias=eps[0:HC, 0:1]).then_inc(S.ln_std, 1)
    act.wait_ge(S.ln_normed, i + 1)
    for h in range(2):
        m = act.activation(out[:, h, :], xc[:, h, :], ACT.Identity, bias=bias[:, h:h + 1])
    m.then_inc(S.ln_out, 1)


def layer0_before(nc, t, b):
    cv = Carver(t.arena)
    wt = cv.take(HC, PRE_N)
    w = {n: wt[:, a:e] for n, (a, e) in PRE_W.items()}
    p1, p2 = (w[n].rearrange("p (h o) -> p h o", h=2) for n in ("p1", "p2"))
    taps = w["dw"].rearrange("p (h k) -> p h k", h=2)
    pad = cv.take(HC, 2 * PADW * PADW).rearrange("p (h y x) -> p h y x", h=2, y=PADW)
    xc, sq, xn, gate = (halves(cv.take(HC, 2 * T), T) for _ in range(4))
    rstd = cv.take(HC, T)
    dsum = cv.take(HC, 2)
    x, xs, ps = halves(t.ys[0:HC, :], L), halves(t.xs[0:HC, :], L), t.ps
    with ExitStack() as stack:
        S = semaphores(nc, stack, LN_SEMS + " weights image cleared gate_conv branch_conv gate_done gate_stored "
                       "branch_padded taps_summed silu_done dsum_done init_done")
        with nc.Block() as block:
            @block.sync
            def _(sp):
                sp.dma_start(wt, t.inp["pre_w"]).then_inc(S.weights, 16)
                sp.dma_start(x, t.inp["x_in"][b].rearrange("(h p) l -> p h l", h=2)).then_inc(S.image, 16)
                with sp.Fori(0, NCH) as i:
                    sp.wait_ge(S.gate_done, i + 1)
                    sp.dma_start(t.gate_scratch[:, :, bass.ds(i * T, T)], gate).then_inc(S.gate_stored, 16)
                sp.wait_ge(S.gate_stored, 16 * NCH)

            @block.gpsimd
            def _(pool):
                nc.gpsimd.memset(pad, 0.0).then_inc(S.cleared, 1)

            @block.tensor
            def _(pe):
                pe.wait_ge(S.weights, 16)
                pe.wait_ge(S.image, 16)
                with pe.Fori(0, NCH) as i:
                    pe.wait_ge(S.ln_rstd, i)
                    ln_pe(pe, S, i, ps, w["mean"], chunk(x, i), sq)
                    pe.wait_ge(S.ln_out, i + 1)
                    pe.wait_ge(S.gate_done, i)
                    conv192(pe, ps, (2, 3), p1, xn).then_inc(S.gate_conv, 1)
                    pe.wait_ge(S.branch_padded, i)
                    conv192(pe, ps, (4, 5), p2, xn).then_inc(S.branch_conv, 1)

            @block.scalar
            def _(act):
                act.wait_ge(S.cleared, 1)
                with act.Fori(0, NCH) as i:
                    act.wait_ge(S.branch_conv, i)
                    ln_act(act, S, i, ps, xc, sq, rstd, t.eps, w["b"], xn)
                    act.wait_ge(S.gate_conv, i + 1)
                    act.wait_ge(S.gate_stored, 16 * i)
                    for h in range(2):
                        m = act.activation(gate[:, h, :], ps[0:HC, 2 + h, :], ACT.Silu, bias=w["p1b"][:, h:h + 1])
                    m.then_inc(S.gate_done, 1)
                    act.wait_ge(S.branch_conv, i + 1)
                    for h in range(2):
                        m = act.activation(pad[:, h, bass.ds(i * ROWS + 1, ROWS), 1:W + 1],
                                           ps[0:HC, 4 + h, :].rearrange("p (y x) -> p y x", x=W),
                                           ACT.Identity, bias=w["p2b"][:, h:h + 1])
                    m.then_inc(S.branch_padded, 1)
                for h in range(2):
                    act.wait_ge(S.taps_summed, 9 * (h + 1))
                    act.activation(xs[:, h, :], xs[:, h, :], ACT.Silu, bias=w["dwb"][:, h:h + 1])\
                       .then_inc(S.silu_done, 1)

            @block.vector
            def _(v):
                v.wait_ge(S.weights, 16)
                v.wait_ge(S.image, 16)
                v.tensor_reduce(dsum, w["D"].rearrange("p (h k) -> p h k", h=2), AX.X, ALU.add).then_inc(S.dsum_done, 1)
                with v.Fori(0, NCH) as i:
                    v.wait_ge(S.ln_out, i)
                    ln_dve(v, S, i, ps, chunk(x, i), xc, rstd, w["g"])
                v.wait_ge(S.branch_padded, NCH)
                for h in range(2):
                    acc = xs[:, h, :].rearrange("p (y x) -> p y x", x=W)
                    for k in range(9):
                        tap = pad[:, h, k // 3:k // 3 + H, k % 3:k % 3 + W]
                        if k:
                            v.wait_ge(S.taps_summed, 9 * h + k)
                            v.scalar_tensor_tensor(acc, tap, taps[:, h, k:k + 1], acc, ALU.mult, ALU.add)\
                             .then_inc(S.taps_summed, 1)
                        else:
                            v.tensor_scalar(acc, tap, taps[:, h, 0:1], None, ALU.mult).then_inc(S.taps_summed, 1)
                v.wait_ge(S.dsum_done, 1)
                for h in range(2):
                    v.wait_ge(S.silu_done, h + 1)
                    v.tensor_scalar(x[:, h, :], xs[:, h, :], dsum[:, h:h + 1], None, ALU.mult).then_inc(S.init_done, 1)
        end_phase(nc, S)


def as_rows(ap2):
    return ap2.rearrange("p (y x) -> p y x", x=W)


def scan_layer(nc, t, rank, w_scan, w_rank, w_alog, cols):
    NSTEP = K * NCH
    cv = Carver(t.arena)
    wt = cv.take(HC, SCAN_N)
    wb, wc = (wt[:, slice(*SCAN_W[n])].rearrange("p (k h m) -> p k h m", k=K, h=2) for n in ("wb", "wc"))
    dtb = wt[:, slice(*SCAN_W["dtb"])].rearrange("p (h k) -> p h k", h=2)
    wz = cv.take(HC, 2 * K * C).rearrange("p (k h o) -> p k h o", k=K, h=2)
    neg_a = cv.take(128, K * NG)
    hs = cv.take(128, NG * T).rearrange("p (g t) -> p g t", g=NG)
    parts = cv.take(HC, 2 * 3 * 2 * T).rearrange("p (q r h t) -> p q r h t", q=2, r=3, h=2)
    stacks = cv.take(HC, 2 * NQ * T).rearrange("p (q n t) -> p q n t", q=2, n=NQ)
    u = cv.take(128, 3 * T).rearrange("p (n t) -> p n t", n=3)
    hc = cv.take(128, 3 * T).rearrange("p (n t) -> p n t", n=3)
    b_rep, c_rep = cv.take(128, T), cv.take(128, T)
    ranks = hs[0:rank, 0:6, :].rearrange("p g t -> p (g t)")[:, 0:RANK_N]
    ranks = ranks.rearrange("p (w k c) -> p w k c", w=2, k=K)
    xs, ys, ps = halves(t.xs[0:HC, :], L), halves(t.ys[0:HC, :], L), t.ps
    dt, dt1, dt2 = (parts[:, 0, r] for r in range(3))
    dx, dx1, dx2 = (parts[:, 1, r] for r in range(3))
    e_buf, log_buf, relu_buf, poly_buf = dx1, dt, dt2, dx2
    DBANK, XBANK, YBANK, PBANK = 0, 2, 4, 6
    LAG = 3

    def place(s):
        k, i = s // NCH, s % NCH
        return k, i if k < 2 else NCH - 1 - i

    def flip(ap, k):
        return ap if k < 2 else ap[:, ::-1]

    def px(ap2, k, i):
        lines = ap2.rearrange("p (y x) -> p x y", x=W) if cols[k] else as_rows(ap2)
        return lines[:, bass.ds(i * ROWS, ROWS), :]

    def shape(ap2):
        return as_rows(ap2)

    with ExitStack() as stack:
        S = semaphores(nc, stack, "weights a_exp a_ready wz_made wz_ready z_ready b_made c_made absz expz logz sqz reluz "
                       "poly big logs dt_made dx_made dt_r1 dx_r1 dt_r2 dx_r2 b_ready c_ready "
                       "dt_spread dx_spread decay u_made h_made hc_made summed y_added")
        stacked = [stack.enter_context(nc.semaphore(f"stacked{q}")) for q in range(NQ)]
        steps = []
        for k in range(K):
            steps += [(k, 0), (k, None), (k, NCH - 1)]

        def run(eng, body, warm, tail):
            warm()
            for k, i in steps:
                if i is None:
                    with eng.Fori(1, NCH - 1) as r:
                        if k < 2:
                            body(k, r, k * NCH + r, (k, r - 1), (k, r + 1))
                        else:
                            down = r * -1 + (NCH - 1)
                            body(k, down, k * NCH + r, (k, down + 1), (k, down - 1))
                else:
                    s = k * NCH + i
                    prev, nxt = place(s - 1) if s else None, place(s + 1) if s + 1 < NSTEP else None
                    body(*place(s), s, prev, nxt)
            tail()

        with nc.Block() as block:
            @block.sync
            def _(sp):
                sp.dma_start(wt, w_scan).then_inc(S.weights, 16)
                sp.dma_start(ranks, w_rank.rearrange("p (w k c) -> p w k c", w=2, k=K)).then_inc(S.weights, 16)
                sp.dma_start(neg_a, w_alog).then_inc(S.weights, 16)

                def stack_parts(s):
                    sp.wait_ge(S.dt_r2, s + 1)
                    sp.wait_ge(S.dx_r2, s + 1)
                    for q in range(NQ):
                        h, j = q // 3, q % 3
                        sp.wait_ge(S.dt_spread, s * NG + 4 * (q + 1) - NG)
                        sp.wait_ge(S.dx_spread, s * NG + 4 * (q + 1) - NG)
                        for r in range(3):
                            sp.dma_start(stacks[32 * r:32 * r + 32, :, q, :],
                                         parts[32 * j:32 * j + 32, :, r, h, :]).then_inc(stacked[q], 16)

                def first_stacks():
                    sp.wait_ge(S.dt_r2, 1)
                    sp.wait_ge(S.dx_r2, 1)
                    for q in range(NQ):
                        h, j = q // 3, q % 3
                        for r in range(3):
                            sp.dma_start(stacks[32 * r:32 * r + 32, :, q, :],
                                         parts[32 * j:32 * j + 32, :, r, h, :]).then_inc(stacked[q], 16)

                run(sp, lambda k, i, s, prev, nxt: nxt and stack_parts(s + 1), first_stacks, lambda: None)

            @block.tensor
            def _(pe):
                pe.wait_ge(S.weights, 48)
                for k in range(K):
                    for h in range(2):
                        n = 2 * k + h
                        if n >= 4:
                            pe.wait_ge(S.wz_ready, n - 3)
                        pe.matmul(ps[0:HC, n % 4, 0:C], ranks[:, 0, k, h * HC:(h + 1) * HC], ranks[:, 1, k, :],
                                  start=True, stop=True).then_inc(S.wz_made, 1)
                pe.wait_ge(S.wz_ready, 2 * K)

                def prepare_z(k, i, s):
                    pe.wait_ge(S.b_ready, s)
                    pe.wait_ge(S.c_ready, s)
                    for o in range(2):
                        for h in range(2):
                            m = pe.matmul(shape(ps[0:HC, PBANK + o, :]), wz[:, k, h, o * HC:(o + 1) * HC],
                                          px(xs[:, h, :], k, i), start=h == 0, stop=h == 1)
                    m.then_inc(S.z_ready, 1)

                def prepare_bc(k, i, s):
                    pe.wait_ge(S.absz, s + 1)
                    pe.wait_ge(S.reluz, s + 1)
                    for n, (wm, made) in enumerate(((wb, S.b_made), (wc, S.c_made))):
                        for h in range(2):
                            m = pe.matmul(shape(ps[:, PBANK + n, :]), wm[:, k, h, :], px(xs[:, h, :], k, i),
                                          start=h == 0, stop=h == 1)
                        m.then_inc(made, 1)

                def spread_dt(s, g):
                    wait_used(S.h_made, s, g, 2)
                    pe.matmul(ps[:, DBANK + g % 2, :], t.sel[:, g % 4, :], top_half(stacks[:, 0, g // 4, :]),
                              start=True, stop=True).then_inc(S.dt_spread, 1)

                def spread_dx(s, g):
                    if g % 4 == 0:
                        pe.wait_ge(stacked[g // 4], 48 * (s + 1))
                    wait_used(S.u_made, s, g, 2)
                    pe.matmul(ps[:, XBANK + g % 2, :], t.sel[:, g % 4, :], top_half(stacks[:, 1, g // 4, :]),
                              start=True, stop=True).then_inc(S.dx_spread, 1)

                def wait_used(sem, s, g, ahead):
                    if isinstance(s, int) and s * NG + g < ahead:
                        return
                    pe.wait_ge(sem, s * NG + (g - ahead + 1))

                def sum_states(s, g):
                    half, n = g // NGH, g % NGH
                    if n == 0:
                        pe.wait_ge(S.y_added, 2 * s + half - 1) if not (isinstance(s, int) and 2 * s + half < 2) else None
                    pe.wait_ge(S.hc_made, s * NG + g + 1)
                    off = (NGH - 1 - n) * CG
                    pe.matmul(ps[0:HC, YBANK + half, :], t.gather[:, off:off + HC], hc[:, g % 3, :],
                              start=n == 0, stop=n == NGH - 1).then_inc(S.summed, 1)

                def body(k, i, s, prev, nxt):
                    spread_dx(s, 0)
                    for g in range(NG):
                        spread_dt(s, g)
                        if g + 1 < NG:
                            spread_dx(s, g + 1)
                        if g >= LAG:
                            sum_states(s, g - LAG)
                        elif prev:
                            sum_states(s - 1, NG + g - LAG)
                        if nxt and g == 5:
                            prepare_z(*nxt, s + 1)
                        if nxt and g == 11:
                            prepare_bc(*nxt, s + 1)

                def warm():
                    prepare_z(*place(0), 0)
                    prepare_bc(*place(0), 0)

                def tail():
                    for g in range(NG - LAG, NG):
                        sum_states(NSTEP - 1, g)

                run(pe, body, warm, tail)

            @block.scalar
            def _(act):
                act.wait_ge(S.weights, 48)
                act.activation(neg_a, neg_a, ACT.Exp).then_inc(S.a_exp, 1)
                for n in range(2 * K):
                    act.wait_ge(S.wz_made, n + 1)
                    act.activation(wz[:, n // 2, n % 2, :], ps[0:HC, n % 4, 0:C], ACT.Copy).then_inc(S.wz_ready, 1)
                act.wait_ge(S.a_ready, 1)

                def softplus(k, s):
                    act.wait_ge(S.z_ready, s + 1)
                    if not isinstance(s, int) or s:
                        for q in range(NQ):
                            act.wait_ge(stacked[q], 48 * s)
                    for h in range(2):
                        m = act.activation(e_buf[:, h, :], ps[0:HC, PBANK + h, :], ACT.Abs, bias=dtb[:, h, k:k + 1])
                    m.then_inc(S.absz, 1)
                    for h in range(2):
                        m = act.activation(relu_buf[:, h, :], ps[0:HC, PBANK + h, :], ACT.Relu, bias=dtb[:, h, k:k + 1])
                    m.then_inc(S.reluz, 1)
                    act.wait_ge(S.absz, s + 1)
                    act.activation(e_buf, e_buf, ACT.Exp, scale=-1.0).then_inc(S.expz, 1)
                    act.wait_ge(S.expz, s + 1)
                    act.activation(log_buf, e_buf, ACT.Ln, bias=1.0).then_inc(S.logz, 1)
                    act.activation(poly_buf, e_buf, ACT.Square, scale=float(np.sqrt(0.5))).then_inc(S.sqz, 1)

                def copy_b(s):
                    act.wait_ge(S.b_made, s + 1)
                    if not isinstance(s, int) or s:
                        act.wait_ge(S.u_made, s * NG)
                    act.activation(b_rep, ps[:, PBANK, :], ACT.Copy).then_inc(S.b_ready, 1)

                def copy_c(s):
                    act.wait_ge(S.c_made, s + 1)
                    if not isinstance(s, int) or s:
                        act.wait_ge(S.hc_made, s * NG)
                    act.activation(c_rep, ps[:, PBANK + 1, :], ACT.Copy).then_inc(S.c_ready, 1)

                def body(k, i, s, prev, nxt):
                    for g in range(NG):
                        if g == 1:
                            copy_c(s)
                        act.wait_ge(S.dt_spread, s * NG + g + 1)
                        bank = ps[:, DBANK + g % 2, :]
                        act.activation(bank, bank, ACT.Exp, scale=neg_a[:, k * NG + g:k * NG + g + 1])\
                           .then_inc(S.decay, 1)
                        if nxt and g == 7:
                            softplus(nxt[0], s + 1)
                    if nxt:
                        copy_b(s + 1)

                def warm():
                    softplus(0, 0)
                    copy_b(0)

                run(act, body, warm, lambda: None)

            @block.vector
            def _(v):
                v.wait_ge(S.a_exp, 1)
                v.tensor_scalar(neg_a, neg_a, -1.0, None, ALU.mult).then_inc(S.a_ready, 1)

                def make_u(s, g):
                    v.wait_ge(S.dx_spread, s * NG + g + 1)
                    if g == 0:
                        v.wait_ge(S.b_ready, s + 1)
                    if not isinstance(s, int) or s or g >= 3:
                        v.wait_ge(S.h_made, s * NG + g - 2)
                    v.tensor_tensor(u[:, g % 3, :], ps[:, XBANK + g % 2, :], b_rep, ALU.mult).then_inc(S.u_made, 1)

                def make_h(k, i, s, g):
                    v.wait_ge(S.decay, s * NG + g + 1)
                    v.wait_ge(S.u_made, s * NG + g + 1)
                    if not isinstance(s, int) or s:
                        v.wait_ge(S.hc_made, (s - 1) * NG + g + 1)
                        v.wait_ge(S.h_made, (s - 1) * NG + g + 1)
                    first = isinstance(s, int) and s % NCH == 0
                    last = T - 1 if k < 2 else 0
                    v.tensor_tensor_scan(flip(hs[:, g, :], k), flip(ps[:, DBANK + g % 2, :], k), flip(u[:, g % 3, :], k),
                                         0.0 if first else hs[:, g, last:last + 1], ALU.mult, ALU.add)\
                     .then_inc(S.h_made, 1)

                def logs(s):
                    v.wait_ge(S.logz, s + 1)
                    v.scalar_tensor_tensor(log_buf, e_buf, SMALL, log_buf, ALU.is_ge, ALU.mult).then_inc(S.big, 1)
                    v.wait_ge(S.big, s + 1)
                    v.wait_ge(S.poly, s + 1)
                    v.tensor_tensor(dt, log_buf, poly_buf, ALU.max).then_inc(S.logs, 1)

                def split(s, v0, v1, v2, made, r1, r2):
                    v.wait_ge(made, s + 1)
                    v.tensor_tensor(v1, v0, top_half(v0), ALU.subtract).then_inc(r1, 1)
                    v.wait_ge(r1, s + 1)
                    v.tensor_tensor(v2, v1, top_half(v1), ALU.subtract).then_inc(r2, 1)

                def add_y(pk, pi, s, half):
                    v.wait_ge(S.summed, s * NG + NGH * (half + 1))
                    dst = px(ys[:, half, :], pk, pi)
                    v.tensor_tensor(dst, dst, shape(ps[0:HC, YBANK + half, :]), ALU.add).then_inc(S.y_added, 1)

                def body(k, i, s, prev, nxt):
                    make_u(s, 0)
                    for g in range(NG):
                        if g + 1 < NG:
                            make_u(s, g + 1)
                        make_h(k, i, s, g)
                        if prev and g == LAG + 1:
                            add_y(*prev, s - 1, 1)
                        if g == NGH + LAG + 1:
                            add_y(k, i, s, 0)
                        if nxt and g == 10:
                            logs(s + 1)
                        if nxt and g == 14:
                            split(s + 1, dt, dt1, dt2, S.dt_made, S.dt_r1, S.dt_r2)
                        if nxt and g == 17:
                            split(s + 1, dx, dx1, dx2, S.dx_made, S.dx_r1, S.dx_r2)

                def warm():
                    logs(0)
                    split(0, dt, dt1, dt2, S.dt_made, S.dt_r1, S.dt_r2)
                    split(0, dx, dx1, dx2, S.dx_made, S.dx_r1, S.dx_r2)

                run(v, body, warm, lambda: add_y(*place(NSTEP - 1), NSTEP - 1, 1))

            @block.gpsimd
            def _(pool):
                def combine(k, i, s):
                    pool.wait_ge(S.sqz, s + 1)
                    pool.tensor_tensor(poly_buf, e_buf, poly_buf, ALU.subtract).then_inc(S.poly, 1)
                    pool.wait_ge(S.logs, s + 1)
                    pool.wait_ge(S.reluz, s + 1)
                    pool.tensor_tensor(dt, dt, relu_buf, ALU.add).then_inc(S.dt_made, 1)
                    pool.wait_ge(S.dt_made, s + 1)
                    for h in range(2):
                        m = pool.tensor_tensor(shape(dx[:, h, :]), shape(dt[:, h, :]), px(xs[:, h, :], k, i), ALU.mult)
                    m.then_inc(S.dx_made, 1)

                def body(k, i, s, prev, nxt):
                    for g in range(NG):
                        if g == 0:
                            pool.wait_ge(S.c_ready, s + 1)
                        pool.wait_ge(S.h_made, s * NG + g + 1)
                        if not (isinstance(s, int) and s == 0 and g < 3):
                            pool.wait_ge(S.summed, s * NG + (g - 2))
                        pool.tensor_tensor(hc[:, g % 3, :], hs[:, g, :], c_rep, ALU.mult).then_inc(S.hc_made, 1)
                        if nxt and g == 9:
                            combine(*nxt, s + 1)

                run(pool, body, lambda: combine(*place(0), 0), lambda: None)
        for q in range(NQ):
            nc.gpsimd.sem_clear(stacked[q])
        end_phase(nc, S)


def layer0_after(nc, t, b):
    cv = Carver(t.arena)
    wt = cv.take(HC, L1_N)
    w = {n: wt[:, a:e] for n, (a, e) in L1_W.items()}
    ca1 = w["ca1"].rearrange("p (h m) -> p h m", h=2)
    ca2 = cv.take(12, C)
    cab = cv.take(HC, 3)
    xc, sq, yn, gate = (halves(cv.take(HC, 2 * T), T) for _ in range(4))
    rstd = cv.take(HC, T)
    mean, hid, att = cv.take(HC, 2), cv.take(12, 1), cv.take(HC, 2)
    xs, ys, ps = halves(t.xs[0:HC, :], L), halves(t.ys[0:HC, :], L), t.ps
    with ExitStack() as stack:
        S = semaphores(nc, stack, LN_SEMS + " weights gate_loaded image gated mean_done hid_made hid_done att_made att_done added")
        with nc.Block() as block:
            @block.sync
            def _(sp):
                sp.dma_start(wt, t.inp["l1_w"]).then_inc(S.weights, 16)
                sp.dma_start(ca2, t.inp["ca2"]).then_inc(S.weights, 16)
                sp.dma_start(cab, t.inp["cab"]).then_inc(S.weights, 16)
                sp.dma_start(xs, t.inp["x_in"][b].rearrange("(h p) l -> p h l", h=2)).then_inc(S.image, 16)
                with sp.Fori(0, NCH) as i:
                    sp.wait_ge(S.gated, i)
                    sp.dma_start(gate, t.gate_scratch[:, :, bass.ds(i * T, T)]).then_inc(S.gate_loaded, 16)

            @block.tensor
            def _(pe):
                pe.wait_ge(S.weights, 48)
                with pe.Fori(0, NCH) as i:
                    pe.wait_ge(S.ln_rstd, i)
                    ln_pe(pe, S, i, ps, w["mean"], chunk(ys, i), sq)
                pe.wait_ge(S.mean_done, 1)
                for h in range(2):
                    m = pe.matmul(ps[0:12, 2, 0:1], ca1[:, h, :], mean[:, h:h + 1], start=h == 0, stop=h == 1)
                m.then_inc(S.hid_made, 1)
                pe.wait_ge(S.hid_done, 1)
                for h in range(2):
                    m = pe.matmul(ps[0:HC, 3 + h, 0:1], ca2[:, h * HC:(h + 1) * HC], hid, start=True, stop=True)
                m.then_inc(S.att_made, 1)

            @block.scalar
            def _(act):
                act.wait_ge(S.weights, 48)
                with act.Fori(0, NCH) as i:
                    act.wait_ge(S.gated, i)
                    ln_act(act, S, i, ps, xc, sq, rstd, t.eps, w["l0b"], yn)
                act.wait_ge(S.hid_made, 1)
                act.activation(hid, ps[0:12, 2, 0:1], ACT.Relu, bias=cab[0:12, 2:3], scale=1.0 / L).then_inc(S.hid_done, 1)
                act.wait_ge(S.att_made, 1)
                for h in range(2):
                    act.activation(att[:, h:h + 1], ps[0:HC, 3 + h, 0:1], ACT.Sigmoid, bias=cab[:, h:h + 1])\
                       .then_inc(S.att_done, 1)

            @block.vector
            def _(v):
                v.wait_ge(S.weights, 48)
                with v.Fori(0, NCH) as i:
                    v.wait_ge(S.ln_out, i)
                    ln_dve(v, S, i, ps, chunk(ys, i), xc, rstd, w["l0g"])
                    v.wait_ge(S.ln_out, i + 1)
                    v.wait_ge(S.gate_loaded, 16 * (i + 1))
                    v.tensor_tensor(chunk(ys, i), yn, gate, ALU.mult).then_inc(S.gated, 1)
                v.wait_ge(S.gated, NCH)
                v.tensor_reduce(mean, ys, AX.X, ALU.add).then_inc(S.mean_done, 1)
                v.wait_ge(S.image, 16)
                for h in range(2):
                    v.wait_ge(S.att_done, h + 1)
                    v.scalar_tensor_tensor(xs[:, h, :], ys[:, h, :], att[:, h:h + 1], xs[:, h, :], ALU.mult, ALU.add)\
                     .then_inc(S.added, 1)
        end_phase(nc, S)


def layer1(nc, t):
    cv = Carver(t.arena)
    wt = cv.take(HC, L1_N)
    w = {n: wt[:, a:e] for n, (a, e) in L1_W.items()}
    half2 = lambda n: w[n].rearrange("p (h o) -> p h o", h=2)
    win, ssmin, wx2, so, wo = (half2(n) for n in ("win", "ssmin", "wx2", "so", "wo"))
    xb, xcw, xd, dtb, dd = (half2(n) for n in ("xb", "xc", "xd", "dtb", "D"))
    dtw = cv.take(K * DTR1, K * C).rearrange("p (k c) -> p k c", k=K)
    pick = cv.take(K * DS1, K * HC).rearrange("p (k c) -> p k c", k=K)
    wu = cv.take(HC, 4 * C).rearrange("p (h o) -> p h o", h=2)
    xc, sq, xn, xss, z, sx2, ez, rz, gain, term = (halves(cv.take(HC, 2 * T), T) for _ in range(10))
    rstd = cv.take(HC, T)
    dsum, dsum2 = cv.take(HC, 2), cv.take(HC, 2)
    ddp = cv.take(HC, 2 * K)
    rows_b, bc, rows_dt = cv.take(K * DS1, T), cv.take(K * DS1, T), cv.take(K * DTR1, T)
    xs, ys, ps = halves(t.xs[0:HC, :], L), halves(t.ys[0:HC, :], L), t.ps
    pair = lambda n: ps[0:HC, n:n + 2, :]
    with ExitStack() as stack:
        S = semaphores(nc, stack, LN_SEMS + " weights wu_made wu_ready u_made x2_made xss_done z_done sx2_done rows_made "
                       "dt_rows_made b_copied dt_copied bc_done dt_z bc_spread abs_done exp_done ln_done relu_done dt_done "
                       "term_done gain_done y_done yz_done out_made s_done o_made x_done dsum_done dsum2_done init_done "
                       "m_mean m_centered m_square m_var m_std m_rstd m_normed m_out")
        M = namedtuple("Norm", LN_SEMS.split())(S.m_mean, S.m_centered, S.m_square, S.m_var, S.m_std, S.m_rstd,
                                                S.m_normed, S.m_out)
        with nc.Block() as block:
            @block.sync
            def _(sp):
                sp.dma_start(wt, t.inp["l1_w"]).then_inc(S.weights, 16)
                sp.dma_start(dtw, t.inp["l1_dtw"].rearrange("p (k c) -> p k c", k=K)).then_inc(S.weights, 16)
                sp.dma_start(pick, t.inp["pick"].rearrange("p (k c) -> p k c", k=K)).then_inc(S.weights, 16)
                sp.dma_start(ddp, t.inp["l2_d"]).then_inc(S.weights, 16)

            @block.tensor
            def _(pe):
                pe.wait_ge(S.weights, 64)
                for h in range(2):
                    for m in range(2):
                        mm = pe.matmul(ps[0:HC, h, 0:2 * C], win[:, m, h * HC:(h + 1) * HC], ssmin[:, m, :],
                                       start=m == 0, stop=m == 1)
                    mm.then_inc(S.wu_made, 1)
                pe.wait_ge(S.wu_ready, 2)
                with pe.Fori(0, NCH) as i:
                    pe.wait_ge(S.bc_done, i)
                    pe.wait_ge(S.term_done, 2 * K * i)
                    pe.wait_ge(M.ln_rstd, i)
                    ln_pe(pe, S, i, ps, w["mean"], chunk(xs, i), sq)
                    pe.wait_ge(S.ln_out, i + 1)
                    pe.wait_ge(S.dt_copied, i)
                    pe.wait_ge(S.s_done, i)
                    for n in range(4):
                        if n == 2:
                            pe.wait_ge(S.x_done, i)
                        for h in range(2):
                            m = pe.matmul(ps[0:HC, 2 + n, :], wu[:, h, n * HC:(n + 1) * HC], xn[:, h, :],
                                          start=h == 0, stop=h == 1)
                    m.then_inc(S.u_made, 1)
                    conv192(pe, ps, (6, 7), wx2, xn).then_inc(S.x2_made, 1)
                    pe.wait_ge(S.xss_done, i + 1)
                    pe.wait_ge(S.ln_rstd, i + 1)
                    for bank, wm, rows in ((0, xb, K * DS1), (1, xcw, K * DS1), (2, xd, K * DTR1)):
                        for h in range(2):
                            m = pe.matmul(ps[0:rows, bank, :], wm[:, h, :], xss[:, h, :], start=h == 0, stop=h == 1)
                        if bank:
                            m.then_inc(S.rows_made if bank == 1 else S.dt_rows_made, 1)
                    pe.wait_ge(S.bc_done, i + 1)
                    pe.wait_ge(S.dt_copied, i + 1)
                    for k in range(K):
                        bank = 4 + 2 * (k % 2)
                        if k < 2:
                            pe.wait_ge(S.z_done if k == 0 else S.sx2_done, i + 1)
                        else:
                            pe.wait_ge(S.relu_done, K * i + k - 1)
                            pe.wait_ge(S.term_done, 2 * (K * i + k - 1))
                        for h in range(2):
                            m = pe.matmul(ps[0:HC, bank + h, :], dtw[:, k, h * HC:(h + 1) * HC], rows_dt,
                                          start=True, stop=True)
                        m.then_inc(S.dt_z, 1)
                        pe.matmul(ps[0:HC, k % 2, :], pick[:, k, :], bc, start=True, stop=True).then_inc(S.bc_spread, 1)
                    pe.wait_ge(S.y_done, i + 1)
                    ln_pe(pe, M, i, ps, w["mean"], gain, sq)
                    pe.wait_ge(S.yz_done, i + 1)
                    conv192(pe, ps, (2, 3), so, xc).then_inc(S.out_made, 1)
                    pe.wait_ge(S.s_done, i + 1)
                    conv192(pe, ps, (4, 5), wo, z).then_inc(S.o_made, 1)

            @block.scalar
            def _(act):
                act.wait_ge(S.weights, 64)
                for h in range(2):
                    act.wait_ge(S.wu_made, h + 1)
                    act.activation(wu[:, h, :], ps[0:HC, h, 0:2 * C], ACT.Copy).then_inc(S.wu_ready, 1)
                with act.Fori(0, NCH) as i:
                    act.wait_ge(S.x2_made, i)
                    ln_act(act, S, i, ps, xc, sq, rstd, t.eps, w["b"], xn)
                    act.wait_ge(S.u_made, i + 1)
                    act.activation(xss, pair(2), ACT.Silu).then_inc(S.xss_done, 1)
                    act.wait_ge(S.o_made, i)
                    act.activation(z, pair(4), ACT.Silu).then_inc(S.z_done, 1)
                    act.wait_ge(S.x2_made, i + 1)
                    act.activation(sx2, pair(6), ACT.Silu).then_inc(S.sx2_done, 1)
                    act.wait_ge(S.rows_made, i + 1)
                    act.activation(rows_b, ps[0:K * DS1, 0, :], ACT.Copy).then_inc(S.b_copied, 1)
                    act.wait_ge(S.dt_rows_made, i + 1)
                    act.activation(rows_dt, ps[0:K * DTR1, 2, :], ACT.Copy).then_inc(S.dt_copied, 1)
                    for k in range(K):
                        n = K * i + k
                        bank = 4 + 2 * (k % 2)
                        act.wait_ge(S.dt_z, n + 1)
                        act.wait_ge(S.dt_done, n)
                        for h in range(2):
                            m = act.activation(ez[:, h, :], ps[0:HC, bank + h, :], ACT.Abs, bias=dtb[:, h, k:k + 1])
                        m.then_inc(S.abs_done, 1)
                        for h in range(2):
                            m = act.activation(rz[:, h, :], ps[0:HC, bank + h, :], ACT.Relu, bias=dtb[:, h, k:k + 1])
                        m.then_inc(S.relu_done, 1)
                        act.wait_ge(S.abs_done, n + 1)
                        act.activation(ez, ez, ACT.Exp, scale=-1.0).then_inc(S.exp_done, 1)
                        act.wait_ge(S.exp_done, n + 1)
                        act.activation(ez, ez, ACT.Ln, bias=1.0).then_inc(S.ln_done, 1)
                    ln_act(act, M, i, ps, xc, sq, rstd, t.eps, w["ob"], xc)

            @block.vector
            def _(v):
                v.wait_ge(S.weights, 64)
                v.tensor_reduce(dsum, dd, AX.X, ALU.add).then_inc(S.dsum_done, 1)
                v.tensor_reduce(dsum2, ddp.rearrange("p (h k) -> p h k", h=2), AX.X, ALU.add).then_inc(S.dsum2_done, 1)
                v.wait_ge(S.dsum_done, 1)
                v.wait_ge(S.dsum2_done, 1)
                with v.Fori(0, NCH) as i:
                    v.wait_ge(S.out_made, i)
                    ln_dve(v, S, i, ps, chunk(xs, i), xc, rstd, w["g"])
                    v.wait_ge(S.b_copied, i + 1)
                    v.wait_ge(S.bc_spread, K * i)
                    v.tensor_tensor(bc, rows_b, ps[0:K * DS1, 1, :], ALU.mult).then_inc(S.bc_done, 1)
                    for k in range(K):
                        n = K * i + k
                        v.wait_ge(S.relu_done, n + 1)
                        v.wait_ge(S.ln_done, n + 1)
                        if k:
                            v.wait_ge(S.gain_done, (K - 1) * i + k - 1)
                            v.wait_ge(S.term_done, 2 * n)
                        out = term if k else gain
                        v.tensor_tensor(out, ez, rz, ALU.add).then_inc(S.dt_done, 1)
                        v.wait_ge(S.dt_done, n + 1)
                        v.wait_ge(S.bc_spread, n + 1)
                        for h in range(2):
                            v.tensor_tensor(out[:, h, :], out[:, h, :], ps[0:HC, k % 2, :], ALU.mult)\
                             .then_inc(S.term_done, 1)
                        if k:
                            v.wait_ge(S.term_done, 2 * (n + 1))
                            v.tensor_tensor(gain, gain, term, ALU.add).then_inc(S.gain_done, 1)
                    v.wait_ge(S.gain_done, (K - 1) * (i + 1))
                    for h in range(2):
                        m = v.scalar_tensor_tensor(gain[:, h, :], gain[:, h, :], dsum[:, h:h + 1], xss[:, h, :],
                                                   ALU.add, ALU.mult)
                    m.then_inc(S.y_done, 1)
                    ln_dve(v, M, i, ps, gain, xc, rstd, w["og"])
                    v.wait_ge(M.ln_out, i + 1)
                    v.tensor_tensor(xc, xc, z, ALU.mult).then_inc(S.yz_done, 1)
                    v.wait_ge(S.out_made, i + 1)
                    v.wait_ge(S.yz_done, i + 1)
                    v.tensor_tensor(z, pair(2), sx2, ALU.mult).then_inc(S.s_done, 1)
                    v.wait_ge(S.o_made, i + 1)
                    v.tensor_tensor(chunk(xs, i), chunk(xs, i), pair(4), ALU.add).then_inc(S.x_done, 1)
                v.wait_ge(S.x_done, NCH)
                for h in range(2):
                    v.tensor_scalar(ys[:, h, :], xs[:, h, :], dsum2[:, h:h + 1], None, ALU.mult).then_inc(S.init_done, 1)
        end_phase(nc, S)


def layer3_first(nc, t):
    cv = Carver(t.arena)
    xc64 = cv.take(CB, L)
    wt, wt2 = cv.take(HC, L3_N), cv.take(128, L3B_N)
    w = {n: wt[:, a:e] for n, (a, e) in L3_W.items()}
    w1 = w["w1"].rearrange("p (h o) -> p h o", h=2)
    b1 = wt2[0:CB, slice(*L3B_W["b1"])]
    xc, sq = (halves(cv.take(HC, 2 * T), T) for _ in range(2))
    rstd = cv.take(HC, T)
    ys, ps = halves(t.ys[0:HC, :], L), t.ps
    with ExitStack() as stack:
        S = semaphores(nc, stack, LN_SEMS + " weights conv_made conv_done")
        with nc.Block() as block:
            @block.sync
            def _(sp):
                sp.dma_start(wt, t.inp["l3_w"]).then_inc(S.weights, 16)
                sp.dma_start(wt2, t.inp["l3b_w"]).then_inc(S.weights, 16)

            @block.tensor
            def _(pe):
                pe.wait_ge(S.weights, 32)
                with pe.Fori(0, NCH) as i:
                    pe.wait_ge(S.ln_rstd, i)
                    ln_pe(pe, S, i, ps, w["mean"], chunk(ys, i), sq)
                    pe.wait_ge(S.ln_out, i + 1)
                    pe.wait_ge(S.conv_done, i)
                    for h in range(2):
                        m = pe.matmul(ps[:, 2, :], w1[:, h, :], ys[:, h, bass.ds(i * T, T)], start=h == 0, stop=h == 1)
                    m.then_inc(S.conv_made, 1)

            @block.scalar
            def _(act):
                act.wait_ge(S.weights, 32)
                with act.Fori(0, NCH) as i:
                    ln_act(act, S, i, ps, xc, sq, rstd, t.eps, w["b"], chunk(ys, i))
                    act.wait_ge(S.conv_made, i + 1)
                    act.activation(xc64[:, bass.ds(i * T, T)], ps[0:CB, 2, :], ACT.Identity, bias=b1)\
                       .then_inc(S.conv_done, 1)

            @block.vector
            def _(v):
                v.wait_ge(S.weights, 32)
                with v.Fori(0, NCH) as i:
                    v.wait_ge(S.ln_out, i)
                    ln_dve(v, S, i, ps, chunk(ys, i), xc, rstd, w["g"])
        end_phase(nc, S)


def layer3_windows(nc, t, n_win):
    nw, step, k = WINS[n_win]
    kk, nn = k * k, nw * nw
    P2 = nn // 2
    KP = k + 2
    LU, LP = P2 * kk, P2 * KP * KP
    cv = Carver(t.arena)
    xc = cv.take(CB, L)
    fold12 = cv.take(CB, L)
    at = cv.at
    unf = cv.take(CB, kk * nn).rearrange("p (a b m n) -> p a b m n", a=k, b=k, m=nw)
    cv.at = at
    pad = cv.take(128, LP)
    acc = cv.take(128, LP)
    cv.at = at + 17424
    uc = cv.take(128, LU)
    wt2 = cv.take(128, L3B_N)
    se2 = cv.take(8, 128)
    icnt = xc if nw == 12 else None
    ysum, hid, att = cv.take(128, P2), cv.take(8, P2), cv.take(128, P2)
    w = {n: wt2[:, a:e] for n, (a, e) in L3B_W.items()}
    out = (t.xs[0:CB, 0:L], t.xs[0:CB, L:2 * L], fold12)[n_win]
    pad4 = pad.rearrange("p (n y x) -> p n y x", n=P2, y=KP)
    acc4 = acc.rearrange("p (n y x) -> p n y x", n=P2, y=KP)
    uc4 = uc.rearrange("p (n y x) -> p n y x", n=P2, y=k)
    uc3 = uc.rearrange("p (n r) -> p n r", n=P2)
    ps = t.ps
    total = CB * kk * nn
    flat = t.fold_scratch[0:total]
    as_unf = flat.rearrange("(c j) -> c j", c=CB)
    as_patch = flat.rearrange("(a n c r) -> a c n r", a=2, c=CB, r=kk)
    flat2 = t.fold_scratch2[0:total]
    as_unf2 = flat2.rearrange("(c j) -> c j", c=CB)
    as_patch2 = flat2.rearrange("(a n c r) -> a c n r", a=2, c=CB, r=kk)
    unf2 = unf.rearrange("p a b m n -> p (a b m n)")
    spans = [(a, min(a + T, LU)) for a in range(0, LU, T)]

    with ExitStack() as stack:
        S = semaphores(nc, stack, "weights counts unfolded stored patches cleared padded conv_made conv_done summed hid_made hid_done "
                       "att_made att_done scaled taps joined stored2 unf_loaded folded")
        with nc.Block() as block:
            @block.sync
            def _(sp):
                sp.dma_start(wt2, t.inp["l3b_w"]).then_inc(S.weights, 16)
                sp.dma_start(se2, t.inp["se2"]).then_inc(S.weights, 16)
                sp.wait_ge(S.unfolded, k)
                if icnt is not None:
                    sp.dma_start(icnt, t.inp["inv_count"]).then_inc(S.counts, 16)
                sp.dma_start(as_unf, unf2).then_inc(S.stored, 16)
                sp.wait_ge(S.stored, 16)
                for a in range(2):
                    sp.dma_start(uc3[a * CB:(a + 1) * CB], as_patch[a]).then_inc(S.patches, 16)
                sp.wait_ge(S.joined, 1)
                for a in range(2):
                    sp.dma_start(as_patch2[a], uc3[a * CB:(a + 1) * CB]).then_inc(S.stored2, 16)
                sp.wait_ge(S.stored2, 32)
                sp.dma_start(unf2, as_unf2).then_inc(S.unf_loaded, 16)
                sp.wait_ge(S.unf_loaded, 16)

            @block.gpsimd
            def _(pool):
                for a in range(k):
                    src = as_rows(xc)[:, a:a + step * (nw - 1) + 1:step, :]
                    for c in range(k):
                        m = pool.tensor_copy(unf[:, a, c], src[:, :, c:c + step * (nw - 1) + 1:step])
                    m.then_inc(S.unfolded, 1)
                pool.wait_ge(S.stored, 16)
                pool.memset(pad, 0.0).then_inc(S.cleared, 1)
                pool.wait_ge(S.cleared, 1)
                pool.wait_ge(S.patches, 32)
                pool.tensor_copy(pad4[:, :, 1:k + 1, 1:k + 1], uc4).then_inc(S.padded, 1)

            @block.tensor
            def _(pe):
                pe.wait_ge(S.weights, 32)
                pe.wait_ge(S.patches, 32)
                for n, (a, e) in enumerate(spans):
                    if n >= 4:
                        pe.wait_ge(S.conv_done, n - 3)
                    pe.matmul(ps[:, n % 4, 0:e - a], w["w2"], uc[:, a:e], start=True, stop=True).then_inc(S.conv_made, 1)
                pe.wait_ge(S.summed, 1)
                pe.matmul(ps[0:8, 4, 0:P2], w["se1"], ysum, start=True, stop=True).then_inc(S.hid_made, 1)
                pe.wait_ge(S.hid_done, 1)
                pe.matmul(ps[:, 5, 0:P2], se2, hid, start=True, stop=True).then_inc(S.att_made, 1)

            @block.scalar
            def _(act):
                act.wait_ge(S.padded, 1)
                for n, (a, e) in enumerate(spans):
                    act.wait_ge(S.conv_made, n + 1)
                    act.activation(uc[:, a:e], ps[:, n % 4, 0:e - a], ACT.Identity, bias=w["b2"]).then_inc(S.conv_done, 1)
                act.wait_ge(S.hid_made, 1)
                act.activation(hid, ps[0:8, 4, 0:P2], ACT.Relu, scale=1.0 / kk).then_inc(S.hid_done, 1)
                act.wait_ge(S.att_made, 1)
                act.activation(att, ps[:, 5, 0:P2], ACT.Sigmoid).then_inc(S.att_done, 1)

            @block.vector
            def _(v):
                v.wait_ge(S.weights, 32)
                v.wait_ge(S.padded, 1)
                lo, n = KP + 1, LP - 2 * KP - 2
                for j in range(9):
                    off = lo + (j // 3 - 1) * KP + j % 3 - 1
                    src, dst, tap = pad[:, off:off + n], acc[:, lo:lo + n], w["dw"][:, j:j + 1]
                    if j == 0:
                        v.tensor_scalar(dst, src, tap, w["dwb"], ALU.mult, ALU.add).then_inc(S.taps, 1)
                    else:
                        v.wait_ge(S.taps, j)
                        v.scalar_tensor_tensor(dst, src, tap, dst, ALU.mult, ALU.add).then_inc(S.taps, 1)
                v.wait_ge(S.conv_done, len(spans))
                v.tensor_reduce(ysum, uc3, AX.X, ALU.add).then_inc(S.summed, 1)
                v.wait_ge(S.att_done, 1)
                v.tensor_tensor(uc3, uc3, att.unsqueeze(2).broadcast_to([128, P2, kk]), ALU.mult).then_inc(S.scaled, 1)
                v.wait_ge(S.scaled, 1)
                v.wait_ge(S.taps, 9)
                v.tensor_tensor(uc4, uc4, acc4[:, :, 1:k + 1, 1:k + 1], ALU.add).then_inc(S.joined, 1)
                v.wait_ge(S.unf_loaded, 16)
                img = as_rows(out)
                done = 0
                if step == k:
                    for a in range(k):
                        for c in range(k):
                            v.tensor_copy(img[:, a::k, c::k], unf[:, a, c]).then_inc(S.folded, 1)
                else:
                    v.memset(out, 0.0).then_inc(S.folded, 1)
                    done = 1
                    for a in range(k):
                        for c0, c1 in ((0, step), (step, k)):
                            dst = img[:, a:a + step * (nw - 1) + 1:step, c0 // step * step:]
                            x0 = c0 // step * step
                            rows = img[:, a:a + step * (nw - 1) + 1:step, x0:x0 + step * nw] if x0 + step * nw <= W else None
                            if rows is not None:
                                dst = rows.rearrange("p m (n c) -> p m n c", c=step)[:, :, :, 0:c1 - c0]
                                src = unf[:, a, c0:c1].rearrange("p c m n -> p m n c")
                                v.wait_ge(S.folded, done)
                                v.tensor_tensor(dst, dst, src, ALU.add).then_inc(S.folded, 1)
                                done += 1
                            else:
                                dst = img[:, a:a + step * (nw - 1) + 1:step, x0:x0 + step * (nw - 1)]
                                dst = dst.rearrange("p m (n c) -> p m n c", c=step)[:, :, :, 0:c1 - c0]
                                src = unf[:, a, c0:c1, :, 0:nw - 1].rearrange("p c m n -> p m n c")
                                v.wait_ge(S.folded, done)
                                v.tensor_tensor(dst, dst, src, ALU.add).then_inc(S.folded, 1)
                                x1 = x0 + step * (nw - 1)
                                dst = img[:, a:a + step * (nw - 1) + 1:step, x1:x1 + c1 - c0]
                                src = unf[:, a, c0:c1, :, nw - 1].rearrange("p c m -> p m c")
                                v.wait_ge(S.folded, done + 1)
                                v.tensor_tensor(dst, dst, src, ALU.add).then_inc(S.folded, 1)
                                done += 2
                    v.wait_ge(S.counts, 16)
                    v.wait_ge(S.folded, done)
                    v.tensor_tensor(out, out, icnt, ALU.mult).then_inc(S.folded, 1)
        end_phase(nc, S)


def layer3_last(nc, t, b):
    cv = Carver(t.arena)
    cv.take(CB, L)
    fold12 = cv.take(CB, L)
    wt, wt2 = cv.take(HC, L3_N), cv.take(128, L3B_N)
    w3x = wt[:, slice(*L3_W["w3x"])].rearrange("p (h o) -> p h o", h=2)
    b3 = wt[:, slice(*L3_W["b3"])]
    w3c = wt2[0:CB, slice(*L3B_W["w3c"])].rearrange("p (n o) -> p n o", n=3)
    res = cv.take(HC, 4 * T).rearrange("p (h n t) -> p h n t", h=2, n=2)
    ys, ps = halves(t.ys[0:HC, :], L), t.ps
    folds = (t.xs[0:CB, 0:L], t.xs[0:CB, L:2 * L], fold12)
    out = t.out[b].rearrange("(h p) l -> p h l", h=2)
    with ExitStack() as stack:
        S = semaphores(nc, stack, "weights made0 made1 biased0 biased1 stored0 stored1")
        made, biased, stored = (S.made0, S.made1), (S.biased0, S.biased1), (S.stored0, S.stored1)
        with nc.Block() as block:
            @block.sync
            def _(sp):
                sp.dma_start(wt, t.inp["l3_w"]).then_inc(S.weights, 16)
                sp.dma_start(wt2, t.inp["l3b_w"]).then_inc(S.weights, 16)
                with sp.Fori(0, NCH // 2) as i:
                    for n in range(2):
                        sp.wait_ge(biased[n], i + 1)
                        sp.dma_start(out[:, :, bass.ds((2 * i + n) * T, T)], res[:, :, n, :]).then_inc(stored[n], 16)
                for n in range(2):
                    sp.wait_ge(stored[n], 16 * (NCH // 2))

            @block.tensor
            def _(pe):
                pe.wait_ge(S.weights, 32)
                with pe.Fori(0, NCH // 2) as i:
                    for n in range(2):
                        at = bass.ds((2 * i + n) * T, T)
                        pe.wait_ge(biased[n], i)
                        for o in range(2):
                            bank = ps[0:HC, 2 * n + o, :]
                            cut = slice(o * HC, (o + 1) * HC)
                            for h in range(2):
                                pe.matmul(bank, w3x[:, h, cut], ys[:, h, at], start=h == 0, stop=False)
                            for f in range(3):
                                m = pe.matmul(bank, w3c[:, f, cut], folds[f][:, at], start=False, stop=f == 2)
                        m.then_inc(made[n], 1)

            @block.scalar
            def _(act):
                with act.Fori(0, NCH // 2) as i:
                    for n in range(2):
                        act.wait_ge(made[n], i + 1)
                        act.wait_ge(stored[n], 16 * i)
                        for o in range(2):
                            m = act.activation(res[:, o, n, :], ps[0:HC, 2 * n + o, :], ACT.Identity, bias=b3[:, o:o + 1])
                        m.then_inc(biased[n], 1)
        end_phase(nc, S)


class Tensors:
    pass


def build(nc, d, out):
    t = Tensors()
    t.inp, t.out = d, out
    with ExitStack() as stack:
        sb = lambda n, s, dt: stack.enter_context(nc.sbuf_tensor(n, s, dt))
        t.xs = sb("xs", [128, 2 * L], F32)
        t.ys = sb("ys", [128, 2 * L], F32)
        sel = sb("sel", [HC, 4, 128], BF16)
        gather = sb("gather", [128, (2 * NGH - 1) * CG], F32)
        t.arena = sb("arena", [128, 36000], F32)
        t.ps = stack.enter_context(nc.psum_tensor("ps", [128, 8, T], F32))
        t.gate_scratch = nc.dram_tensor("gate_scratch", (HC, 2, L), F32).ap()
        t.fold_scratch = nc.dram_tensor("fold_scratch", (CB * 81 * 144,), F32).ap()
        t.fold_scratch2 = nc.dram_tensor("fold_scratch2", (CB * 81 * 144,), F32).ap()
        t.sel, t.gather = sel, gather
        t.eps = sb("eps", [128, 1], F32)
        S = semaphores(nc, stack, "constants eps_set")
        with nc.Block() as block:
            @block.gpsimd
            def _(pool):
                pool.memset(t.eps[:, :], EPS).then_inc(S.eps_set, 1)

            @block.sync
            def _(sp):
                sp.dma_start(sel[:, :, :], t.inp["sel_c"]).then_inc(S.constants, 16)
                sp.dma_start(gather[:, :], t.inp["gather_c"]).then_inc(S.constants, 16)
                sp.wait_ge(S.constants, 32)
        with nc.Fori(0, NIMG) as b:
            layer0_before(nc, t, b)
            scan_layer(nc, t, 12, t.inp["s0_w"], t.inp["s0_r"], t.inp["s0_a"], (True, False, True, False))
            layer0_after(nc, t, b)
            layer1(nc, t)
            scan_layer(nc, t, 6, t.inp["s2_w"], t.inp["s2_r"], t.inp["s2_a"], (False, True, False, True))
            layer3_first(nc, t)
            for n in range(3):
                layer3_windows(nc, t, n)
            layer3_last(nc, t, b)


def by_half(w):
    w = np.asarray(w)
    return np.ascontiguousarray(w.reshape(2, HC, -1).transpose(1, 0, 2)).reshape(HC, -1)


def host_layouts(a):
    a = {k: np.asarray(v) for k, v in a.items()}
    f = np.float32
    mean = np.full((HC, HC), 1.0 / C, f)
    d = {"x_in": a["x"].reshape(NIMG, C, L)}

    def put(name, spec, parts):
        assert [n for n, _ in spec.items()] == list(parts), name
        d[name] = np.concatenate([p.reshape(p.shape[0], -1) for p in parts.values()], axis=1)
        assert all(p.size // p.shape[0] == spec[n][1] - spec[n][0] for n, p in parts.items())

    put("pre_w", PRE_W, {
        "p1": by_half(a["L0_conv_p1_w"].T), "p2": by_half(a["L0_conv_p2in_w"].T),
        "g": by_half(a["L0_conv_ln_g"]), "b": by_half(a["L0_conv_ln_b"]),
        "p1b": by_half(a["L0_conv_p1_b"]), "p2b": by_half(a["L0_conv_p2in_b"]),
        "dw": by_half(a["L0_conv_dw_w"].reshape(C, 9)), "dwb": by_half(a["L0_conv_dw_b"]),
        "D": by_half(a["L0_conv_Dp"].T), "mean": mean})
    for s, xp, dp, db, al, rank in (("s0", "L0_conv_x_proj_w", "L0_conv_dt_proj_w", "L0_conv_dt_proj_b", "L0_conv_A_log", 12),
                                    ("s2", "L2_conv_x_proj_weight", "L2_conv_dt_projs_weight", "L2_conv_dt_projs_bias",
                                     "L2_conv_A_logs", 6)):
        w = a[xp]
        rep = {}
        for name, at in (("wb", rank), ("wc", rank + NS)):
            rows = np.tile(w[:, at:at + NS], (1, CG, 1))
            rep[name] = rows.reshape(K, 128, 2, HC).transpose(3, 0, 2, 1)
        put(s + "_w", SCAN_W, {**rep, "dtb": by_half(a[db].T)})
        d[s + "_r"] = np.stack([w[:, :rank].transpose(1, 0, 2), a[dp].transpose(2, 0, 1)], axis=1).reshape(rank, -1)
        al = a[al].reshape(K, NG, CG * NS)
        d[s + "_a"] = np.ascontiguousarray(al.transpose(2, 0, 1)).reshape(128, -1)
    xp = a["L1_conv_x_proj_w"]
    win, ca1 = a["L1_conv_w_in"], a["L0_conv_ca_w1"]
    rows = lambda w: by_half(w.reshape(-1, C).T)
    put("l1_w", L1_W, {
        "win": by_half(win[:C]), "ssmin": by_half(a["L1_conv_ssm_in_w"].T), "wx2": by_half(win[C:].T),
        "xb": rows(xp[:, DTR1:DTR1 + DS1]), "xc": rows(xp[:, DTR1 + DS1:]), "xd": rows(xp[:, :DTR1]),
        "dtb": by_half(a["L1_conv_dt_b"].T), "D": by_half(a["L1_conv_Ds"].reshape(K, C).T),
        "g": by_half(a["L1_conv_norm_w"]), "b": by_half(a["L1_conv_norm_b"]),
        "og": by_half(a["L1_conv_out_norm_w"]), "ob": by_half(a["L1_conv_out_norm_b"]),
        "so": by_half(a["L1_conv_ssm_out_w"].T), "wo": by_half(a["L1_conv_w_out"].T), "mean": mean,
        "l0g": by_half(a["L0_conv_on_g"]), "l0b": by_half(a["L0_conv_on_b"]), "ca1": by_half(ca1.T)})
    dtw = np.zeros((K, DTR1, K, C), f)
    pick = np.zeros((K, DS1, K, HC), f)
    for k in range(K):
        dtw[k, :, k] = a["L1_conv_dt_w"][k].T
        pick[k, :, k] = 1.0
    d["l1_dtw"], d["pick"] = dtw.reshape(K * DTR1, -1), pick.reshape(K * DS1, -1)
    d["l2_d"] = by_half(a["L2_conv_Ds"].reshape(K, C).T)
    d["ca2"] = np.ascontiguousarray(a["L0_conv_ca_w2"].T)
    cab = np.zeros((HC, 3), f)
    cab[:, 0:2] = by_half(a["L0_conv_ca_b2"])
    cab[0:12, 2] = a["L0_conv_ca_b1"]
    d["cab"] = cab
    w3 = a["L3_conv_w3"]
    put("l3_w", L3_W, {"w1": by_half(np.concatenate([a["L3_conv_w1"].T] * 2, axis=1)), "w3x": by_half(w3.T), "b3": by_half(a["L3_conv_b3"]),
                       "g": by_half(a["L2_conv_ln_g"].reshape(C)), "b": by_half(a["L2_conv_ln_b"].reshape(C)), "mean": mean})
    w2 = np.zeros((2, CB, 2, CB), f)
    se1 = np.zeros((2, CB, 2, 4), f)
    se2 = np.zeros((2, 4, 2, CB), f)
    for h in range(2):
        w2[h, :, h] = a["L3_conv_w2"].T
        se1[h, :, h] = a["L3_conv_wse1"].T
        se2[h, :, h] = a["L3_conv_wse2"].T
    two = lambda v: np.concatenate([v.reshape(CB, -1)] * 2, axis=0)
    put("l3b_w", L3B_W, {"w2": w2.reshape(128, 128), "se1": se1.reshape(128, 8), "b2": two(a["L3_conv_b2"]),
                         "dw": two(a["L3_conv_wpos"]), "dwb": two(a["L3_conv_bpos"]),
                         "w3c": two(np.ascontiguousarray(w3.T.reshape(3, CB, C).transpose(1, 0, 2))),
                         "b1": two(a["L3_conv_b1"])})
    d["se2"] = se2.reshape(8, 128)
    bf = mybir.dt.np(BF16)
    sel = np.zeros((3, 4, CG, 4, CG, NS), f)
    for g in range(4):
        for c in range(CG):
            sel[:, g, c, g, c] = 1.0
    d["sel_c"] = sel.reshape(HC, 4, 128).astype(bf)
    gather = np.zeros((CG, NS, (2 * NGH - 1) * CG), f)
    for c in range(CG):
        gather[c, :, (NGH - 1) * CG + c] = 1.0
    d["gather_c"] = gather.reshape(128, -1)
    nw, step, k = WINS[2]
    n = np.zeros(H, f)
    for m in range(nw):
        n[m * step:m * step + k] += 1.0
    d["inv_count"] = np.broadcast_to((1.0 / np.outer(n, n)).reshape(1, L), (CB, L)).astype(f)
    return {n: np.ascontiguousarray(v) for n, v in d.items()}


def kernel(**inputs):
    import concourse.bacc as bacc
    from concourse.bass_utils import run_bass_kernel_spmd

    nc = bacc.Bacc("TRN2", target_bir_lowering=False, num_devices=1)
    arrays = host_layouts(inputs)
    aps = {n: nc.dram_tensor(n, v.shape, mybir.dt.from_np(v.dtype), kind="ExternalInput").ap()
           for n, v in arrays.items()}
    out = nc.dram_tensor("out", (NIMG, C, L), F32, kind="ExternalOutput").ap()
    build(nc, aps, out)
    r = run_bass_kernel_spmd(nc, [arrays], core_ids=[0])
    return r.results[0]["out"].reshape(NIMG, C, H, W)
```

```python
from collections import namedtuple
from contextlib import ExitStack

import numpy as np
import concourse.bass as bass
from concourse import mybir

ALU = mybir.AluOpType
ACT = mybir.ActivationFunctionType
AX = mybir.AxisListType
F32 = mybir.dt.float32
BF16 = mybir.dt.bfloat16

NIMG, C, H, W = 8, 192, 64, 64
L = H * W
HC = C // 2
T = 512
NCH = L // T
PAIRS = NCH // 2
ROWS = T // W
K = 4
NS = 16
CG = 128 // NS
NHC = 8
NG = C // CG
NGH = NG // 2
NQ = C // 32
PADW = W + 2
EPS = 1e-5
SMALL = 0.00390625
CB = 64
WINS = ((4, 16, 16), (8, 8, 8), (12, 5, 9))
DTR1, DS1 = 12, 8


def columns(spec):
    out, at = {}, 0
    for name, n in spec:
        out[name] = (at, at + n)
        at += n
    return out, at


PRE_W, PRE_N = columns([("p1", 2 * C), ("p2", 2 * C), ("g", 2), ("b", 2), ("p1b", 2), ("p2b", 2),
                        ("dw", 18), ("dwb", 2), ("D", 2 * K), ("mean", HC)])
SCAN_W, SCAN_N = columns([("wb", 2 * K * 128), ("wc", 2 * K * 128), ("dtb", 2 * K)])
RANK_N = 2 * K * C
L1_W, L1_N = columns([("win", 2 * C), ("ssmin", 4 * C), ("wx2", 2 * C), ("xb", 2 * 32), ("xc", 2 * 32),
                      ("xd", 2 * K * DTR1), ("dtb", 2 * K), ("D", 2 * K), ("g", 2), ("b", 2),
                      ("og", 2), ("ob", 2), ("so", 2 * C), ("wo", 2 * C), ("mean", HC),
                      ("l0g", 2), ("l0b", 2), ("ca1", 2 * 12)])
L3_W, L3_N = columns([("w1", 2 * 2 * CB), ("w3x", 2 * C), ("b3", 2), ("g", 2), ("b", 2), ("mean", HC)])
L3B_W, L3B_N = columns([("w2", 128), ("se1", 8), ("b2", 1), ("dw", 9), ("dwb", 1), ("w3c", 3 * C), ("b1", 1)])


def semaphores(nc, stack, names):
    names = names.split()
    return namedtuple("Semaphores", names)(*[stack.enter_context(nc.semaphore(n)) for n in names])


def semaphore_pair(nc, stack, names, prefix=""):
    names = names.split()
    kind = namedtuple("Semaphores", names)
    return [kind(*[stack.enter_context(nc.semaphore(f"{prefix}{n}{m}")) for n in names]) for m in range(2)]


def end_phase(nc, sems):
    for s in sems:
        nc.gpsimd.sem_clear(s)
    nc.all_engine_barrier()


class Carver:

    def __init__(self, arena):
        self.arena, self.at = arena, 0

    def take(self, partitions, n):
        a = self.arena[0:partitions, self.at:self.at + n]
        self.at += n
        assert self.at <= self.arena.shape[1], self.at
        return a


def halves(ap, n):
    return ap.rearrange("p (h t) -> p h t", h=2, t=n)


def take_pair(cv, n):
    bufs = [cv.take(HC, n * T) for _ in range(2)]
    return [halves(a, T) for a in bufs] if n == 2 else bufs


def pair_of(ap3, r):
    return ap3[:, :, bass.ds(r * (2 * T), 2 * T)]


def as_rows(ap2):
    return ap2.rearrange("p (y x) -> p y x", x=W)


def chunk(ap3, i):
    return ap3[:, :, bass.ds(i * T, T)]


def top_half(ap):
    if len(ap.shape) == 2:
        return ap.bitcast(BF16).rearrange("p (t two) -> p t two", two=2)[:, :, 1]
    return ap.bitcast(BF16).rearrange("p h (t two) -> p h t two", two=2)[:, :, :, 1]


def conv192(pe, ps, banks, w, x, first=True, last=True):
    for j, bank in enumerate(banks):
        for h in range(2):
            m = pe.matmul(ps[0:HC, bank, :], w[:, h, j * HC:(j + 1) * HC], x[:, h, :],
                          start=first and h == 0, stop=last and h == 1)
    return m


LN_SEMS = "ln_mean ln_centered ln_square ln_var ln_std ln_rstd ln_normed ln_out"


def ln_mean(pe, S, bank, ones, x):
    for h in range(2):
        m = pe.matmul(bank, ones, x[:, h, :], start=h == 0, stop=h == 1)
    m.then_inc(S.ln_mean, 1)


def ln_variance(pe, S, r, bank, ones, sq):
    pe.wait_ge(S.ln_square, r + 1)
    for h in range(2):
        m = pe.matmul(bank, ones, sq[:, h, :], start=h == 0, stop=h == 1)
    m.then_inc(S.ln_var, 1)


def ln_centre(v, S, r, bank, x, xc):
    v.wait_ge(S.ln_mean, r + 1)
    for h in range(2):
        m = v.tensor_tensor(xc[:, h, :], x[:, h, :], bank, ALU.subtract)
    m.then_inc(S.ln_centered, 1)


def ln_scale(v, S, r, xc, rstd, gain):
    v.wait_ge(S.ln_std, r + 1)
    v.reciprocal(rstd, rstd).then_inc(S.ln_rstd, 1)
    v.wait_ge(S.ln_rstd, r + 1)
    for h in range(2):
        m = v.scalar_tensor_tensor(xc[:, h, :], xc[:, h, :], gain[:, h:h + 1], rstd, ALU.mult, ALU.mult)
    m.then_inc(S.ln_normed, 1)


def ln_square(act, S, r, xc, sq):
    act.wait_ge(S.ln_centered, r + 1)
    act.activation(sq, xc, ACT.Square).then_inc(S.ln_square, 1)


def ln_root(act, S, r, banks, rstd, eps):
    for n in range(2):
        act.wait_ge(S[n].ln_var, r + 1)
        act.activation(rstd[n], banks[n], ACT.Sqrt, bias=eps[0:HC, 0:1]).then_inc(S[n].ln_std, 1)


def ln_bias(act, S, r, xc, bias, out):
    act.wait_ge(S.ln_normed, r + 1)
    for h in range(2):
        m = act.activation(out[:, h, :], xc[:, h, :], ACT.Identity, bias=bias[:, h:h + 1])
    m.then_inc(S.ln_out, 1)


def layer0_before(nc, t, b):
    cv = Carver(t.arena)
    wt = cv.take(HC, PRE_N)
    w = {n: wt[:, a:e] for n, (a, e) in PRE_W.items()}
    p1, p2 = (w[n].rearrange("p (h o) -> p h o", h=2) for n in ("p1", "p2"))
    taps = w["dw"].rearrange("p (h k) -> p h k", h=2)
    pad = cv.take(HC, 2 * PADW * PADW).rearrange("p (h y x) -> p h y x", h=2, y=PADW)
    xc, sq, xn, gate = (take_pair(cv, 2) for _ in range(4))
    rstd = take_pair(cv, 1)
    dsum = cv.take(HC, 2)
    x, xs, ps = halves(t.ys[0:HC, :], L), halves(t.xs[0:HC, :], L), t.ps
    mean_bank, var_bank = [ps[0:HC, 4 * n, :] for n in range(2)], [ps[0:HC, 4 * n + 1, :] for n in range(2)]
    with ExitStack() as stack:
        G = semaphores(nc, stack, "weights image0 image1 cleared taps_summed silu_done dsum_done init_done")
        S = semaphore_pair(nc, stack, LN_SEMS + " gate_conv branch_conv gate_done gate_stored branch_padded")

        def run(eng, body):
            body(0, None)
            with eng.Fori(1, PAIRS) as r:
                body(r, r - 1)
            body(None, PAIRS - 1)

        with nc.Block() as block:
            @block.sync
            def _(sp):
                sp.dma_start(wt, t.inp["pre_w"]).then_inc(G.weights, 16)
                image = t.inp["x_in"][b].rearrange("(h p) l -> p h l", h=2)
                sp.dma_start(x[:, :, 0:2 * T], image[:, :, 0:2 * T]).then_inc(G.image0, 16)
                sp.dma_start(x[:, :, 2 * T:L], image[:, :, 2 * T:L]).then_inc(G.image1, 16)
                with sp.Fori(0, PAIRS) as r:
                    for n in range(2):
                        sp.wait_ge(S[n].gate_done, r + 1)
                        sp.dma_start(t.gate_scratch[:, :, bass.ds((2 * r + n) * T, T)], gate[n])\
                          .then_inc(S[n].gate_stored, 16)
                for n in range(2):
                    sp.wait_ge(S[n].gate_stored, 16 * PAIRS)

            @block.gpsimd
            def _(pool):
                nc.gpsimd.memset(pad, 0.0).then_inc(G.cleared, 1)

            @block.tensor
            def _(pe):
                pe.wait_ge(G.weights, 16)
                pe.wait_ge(G.image0, 16)

                def pair(r):
                    if not isinstance(r, int):
                        pe.wait_ge(G.image1, 16)
                    for n in range(2):
                        pe.wait_ge(S[n].branch_padded, r)
                        ln_mean(pe, S[n], mean_bank[n], w["mean"], chunk(x, 2 * r + n))
                    for n in range(2):
                        ln_variance(pe, S[n], r, var_bank[n], w["mean"], sq[n])
                    for n in range(2):
                        pe.wait_ge(S[n].ln_out, r + 1)
                        pe.wait_ge(S[n].gate_done, r)
                        conv192(pe, ps, (4 * n + 2, 4 * n + 3), p1, xn[n]).then_inc(S[n].gate_conv, 1)
                        conv192(pe, ps, (4 * n, 4 * n + 1), p2, xn[n]).then_inc(S[n].branch_conv, 1)

                pair(0)
                with pe.Fori(1, PAIRS) as r:
                    pair(r)

            @block.scalar
            def _(act):
                act.wait_ge(G.cleared, 1)
                act.wait_ge(G.dsum_done, 1)

                def body(r, conv):
                    if r is not None:
                        act.preload_act_table_set("natural_log_exp_and_others")
                        for n in range(2):
                            ln_square(act, S[n], r, xc[n], sq[n])
                        ln_root(act, S, r, var_bank, rstd, t.eps)
                        for n in range(2):
                            act.wait_ge(S[n].branch_conv, r)
                            ln_bias(act, S[n], r, xc[n], w["b"], xn[n])
                        for n in range(2):
                            act.wait_ge(S[n].gate_conv, r + 1)
                            act.wait_ge(S[n].gate_stored, 16 * r)
                            for h in range(2):
                                m = act.activation(gate[n][:, h, :], ps[0:HC, 4 * n + 2 + h, :], ACT.Silu,
                                                   bias=w["p1b"][:, h:h + 1])
                            m.then_inc(S[n].gate_done, 1)
                            act.wait_ge(S[n].branch_conv, r + 1)
                            for h in range(2):
                                m = act.activation(pad[:, h, bass.ds((2 * r + n) * ROWS + 1, ROWS), 1:W + 1],
                                                   as_rows(ps[0:HC, 4 * n + h, :]), ACT.Identity,
                                                   bias=w["p2b"][:, h:h + 1])
                            m.then_inc(S[n].branch_padded, 1)
                    if conv is not None:
                        rows = pair_of(xs, conv)
                        act.wait_ge(G.taps_summed, 18 * conv + 18)
                        for h in range(2):
                            act.activation(rows[:, h, :], rows[:, h, :], ACT.Silu, bias=w["dwb"][:, h:h + 1])\
                               .then_inc(G.silu_done, 1)
                        for h in range(2):
                            act.wait_ge(G.silu_done, 2 * conv + h + 1)
                            act.activation(pair_of(x, conv)[:, h, :], rows[:, h, :], ACT.Identity,
                                           scale=dsum[:, h:h + 1]).then_inc(G.init_done, 1)

                run(act, body)

            @block.vector
            def _(v):
                v.wait_ge(G.weights, 16)
                v.wait_ge(G.image0, 16)
                v.tensor_reduce(dsum, w["D"].rearrange("p (h k) -> p h k", h=2), AX.X, ALU.add).then_inc(G.dsum_done, 1)

                def convolve(c, ks):
                    for k in ks:
                        for h in range(2):
                            acc = as_rows(pair_of(xs, c)[:, h, :])
                            tap = pad[:, h, bass.ds(c * (2 * ROWS) + k // 3, 2 * ROWS), k % 3:k % 3 + W]
                            if k:
                                v.wait_ge(G.taps_summed, 18 * c + (2 * (k - 1) + h + 1))
                                v.scalar_tensor_tensor(acc, tap, taps[:, h, k:k + 1], acc, ALU.mult, ALU.add)\
                                 .then_inc(G.taps_summed, 1)
                            else:
                                v.tensor_scalar(acc, tap, taps[:, h, 0:1], None, ALU.mult).then_inc(G.taps_summed, 1)

                def body(r, conv):
                    if r is not None:
                        if not isinstance(r, int):
                            v.wait_ge(G.image1, 16)
                        for n in range(2):
                            v.wait_ge(S[n].ln_out, r)
                            ln_centre(v, S[n], r, mean_bank[n], chunk(x, 2 * r + n), xc[n])
                    early = range(0, 5)
                    if conv is not None:
                        v.wait_ge(S[1].branch_padded, conv + 1)
                        convolve(conv, early)
                    if r is not None:
                        for n in range(2):
                            ln_scale(v, S[n], r, xc[n], rstd[n], w["g"])
                    if conv is not None:
                        if r is not None:
                            v.wait_ge(S[0].branch_padded, r + 1)
                        convolve(conv, range(5, 9))

                run(v, body)
        end_phase(nc, S[0] + S[1] + G)


def scan_layer(nc, t, rank, w_scan, w_rank, w_alog, cols):
    NSTEP = K * NCH
    cv = Carver(t.arena)
    wt = cv.take(HC, SCAN_N)
    wb, wc = (wt[:, slice(*SCAN_W[n])].rearrange("p (k h m) -> p k h m", k=K, h=2) for n in ("wb", "wc"))
    dtb = wt[:, slice(*SCAN_W["dtb"])].rearrange("p (h k) -> p h k", h=2)
    wz = cv.take(HC, 2 * K * C).rearrange("p (k h o) -> p k h o", k=K, h=2)
    neg_a = cv.take(128, K * NG)
    hs = cv.take(128, NG * T).rearrange("p (g t) -> p g t", g=NG)
    parts = cv.take(HC, 2 * 3 * 2 * T).rearrange("p (q r h t) -> p q r h t", q=2, r=3, h=2)
    stacks = cv.take(HC, 2 * NQ * T).rearrange("p (q j h t) -> p q j h t", q=2, h=2, t=T)
    u = cv.take(128, 3 * T).rearrange("p (n t) -> p n t", n=3)
    hc = cv.take(128, NHC * T).rearrange("p (n t) -> p n t", n=NHC)
    b_rep, c_rep = cv.take(128, T), cv.take(128, T)
    ranks = hs[0:rank, 0:6, :].rearrange("p g t -> p (g t)")[:, 0:RANK_N]
    ranks = ranks.rearrange("p (w k c) -> p w k c", w=2, k=K)
    xs, ys, ps = halves(t.xs[0:HC, :], L), halves(t.ys[0:HC, :], L), t.ps
    dt, dt1, dt2 = (parts[:, 0, r] for r in range(3))
    dx, dx1, dx2 = (parts[:, 1, r] for r in range(3))
    e_buf, log_buf, relu_buf, poly_buf = dx1, dt, dt2, dx2
    DBANK, XBANK, YBANK, PBANK = 0, 2, 4, 6
    LAG = 8

    Z_AT, BC_AT = (0, 1, 3, 4), (9, 10, 11, 12)
    ABS_AT, EXP_AT = (3, 6), 7
    BIG_AT, EITHER_AT, RESTS_AT = 10, 12, (15, 16, 18, 19)
    POLY_AT, ADD_AT = 9, 12

    def place(s):
        k, i = s // NCH, s % NCH
        return k, i if k < 2 else NCH - 1 - i

    def stack_of(n, g):
        return stacks[:, n, g // 4 % 3, g // NGH, :]

    def flip(ap, k):
        return ap if k < 2 else ap[:, ::-1]

    def px(ap2, k, i):
        lines = ap2.rearrange("p (y x) -> p x y", x=W) if cols[k] else as_rows(ap2)
        return lines[:, bass.ds(i * ROWS, ROWS), :]

    def shape(ap2):
        return as_rows(ap2)

    with ExitStack() as stack:
        S = semaphores(nc, stack, "weights a_exp a_ready wz_made wz_ready z_ready b_made c_made absz expz logz sqz reluz "
                       "poly big logs dt_made dx_made dt_r1 dx_r1 dt_r2 dx_r2 b_ready c_ready "
                       "dt_spread dx_spread decay u_made h_made hc_made summed y_added")
        stacked = [stack.enter_context(nc.semaphore(f"stacked{q}")) for q in range(NQ // 2)]
        steps = []
        for k in range(K):
            steps += [(k, 0), (k, None), (k, NCH - 1)]

        def run(eng, body, warm, tail):
            warm()
            for k, i in steps:
                if i is None:
                    with eng.Fori(1, NCH - 1) as r:
                        if k < 2:
                            body(k, r, k * NCH + r, (k, r - 1), (k, r + 1))
                        else:
                            down = r * -1 + (NCH - 1)
                            body(k, down, k * NCH + r, (k, down + 1), (k, down - 1))
                else:
                    s = k * NCH + i
                    prev, nxt = place(s - 1) if s else None, place(s + 1) if s + 1 < NSTEP else None
                    body(*place(s), s, prev, nxt)
            tail()

        with nc.Block() as block:
            @block.sync
            def _(sp):
                sp.dma_start(wt, w_scan).then_inc(S.weights, 16)
                sp.dma_start(ranks, w_rank.rearrange("p (w k c) -> p w k c", w=2, k=K)).then_inc(S.weights, 16)
                sp.dma_start(neg_a, w_alog).then_inc(S.weights, 16)

                def stack_parts(s):
                    sp.wait_ge(S.dt_r2, s + 1)
                    sp.wait_ge(S.dx_r2, s + 1)
                    for j in range(NQ // 2):
                        if not isinstance(s, int) or s:
                            sp.wait_ge(S.dt_spread, (s - 1) * NG + 4 * (NQ // 2 + j + 1))
                            sp.wait_ge(S.dx_spread, (s - 1) * NG + 4 * (NQ // 2 + j + 1))
                        for r in range(3):
                            sp.dma_start(stacks[32 * r:32 * r + 32, :, j, :, :],
                                         parts[32 * j:32 * j + 32, :, r, :, :]).then_inc(stacked[j], 16)

                run(sp, lambda k, i, s, prev, nxt: nxt and stack_parts(s + 1), lambda: stack_parts(0), lambda: None)

            @block.tensor
            def _(pe):
                pe.wait_ge(S.weights, 48)
                for k in range(K):
                    for h in range(2):
                        n = 2 * k + h
                        if n >= 4:
                            pe.wait_ge(S.wz_ready, n - 3)
                        pe.matmul(ps[0:HC, n % 4, 0:C], ranks[:, 0, k, h * HC:(h + 1) * HC], ranks[:, 1, k, :],
                                  start=True, stop=True).then_inc(S.wz_made, 1)
                pe.wait_ge(S.wz_ready, 2 * K)

                def prepare_z(k, i, s, o, h):
                    if h == 0:
                        pe.wait_ge((S.b_ready, S.c_ready)[o], s)
                    m = pe.matmul(shape(ps[0:HC, PBANK + o, :]), wz[:, k, h, o * HC:(o + 1) * HC],
                                  px(xs[:, h, :], k, i), start=h == 0, stop=h == 1)
                    if h:
                        m.then_inc(S.z_ready, 1)

                def prepare_bc(k, i, s, n, h):
                    if h == 0:
                        pe.wait_ge(S.absz, 2 * s + n + 1)
                        pe.wait_ge(S.reluz, 2 * s + n + 1)
                    m = pe.matmul(shape(ps[:, PBANK + n, :]), (wb, wc)[n][:, k, h, :], px(xs[:, h, :], k, i),
                                  start=h == 0, stop=h == 1)
                    if h:
                        m.then_inc((S.b_made, S.c_made)[n], 1)

                def spread_dt(s, g):
                    wait_used(S.h_made, s, g, 2)
                    pe.matmul(ps[:, DBANK + g % 2, :], t.sel[:, g % 4, :], top_half(stack_of(0, g)),
                              start=True, stop=True).then_inc(S.dt_spread, 1)

                def spread_dx(s, g):
                    if g % 4 == 0 and g < NGH:
                        pe.wait_ge(stacked[g // 4], 48 * (s + 1))
                    wait_used(S.u_made, s, g, 2)
                    pe.matmul(ps[:, XBANK + g % 2, :], t.sel[:, g % 4, :], top_half(stack_of(1, g)),
                              start=True, stop=True).then_inc(S.dx_spread, 1)

                def wait_used(sem, s, g, ahead):
                    if isinstance(s, int) and s * NG + g < ahead:
                        return
                    pe.wait_ge(sem, s * NG + (g - ahead + 1))

                def sum_states(s, g):
                    half, n = g // NGH, g % NGH
                    if n == 0:
                        pe.wait_ge(S.y_added, 2 * s + half - 1) if not (isinstance(s, int) and 2 * s + half < 2) else None
                    pe.wait_ge(S.hc_made, s * NG + g + 1)
                    off = (NGH - 1 - n) * CG
                    pe.matmul(ps[0:HC, YBANK + half, :], t.gather[:, off:off + HC], hc[:, g % NHC, :],
                              start=n == 0, stop=n == NGH - 1).then_inc(S.summed, 1)

                def body(k, i, s, prev, nxt):
                    spread_dx(s, 0)
                    for g in range(NG):
                        spread_dt(s, g)
                        if g + 1 < NG:
                            spread_dx(s, g + 1)
                        if g >= LAG:
                            sum_states(s, g - LAG)
                        elif prev:
                            sum_states(s - 1, NG + g - LAG)
                        if nxt and g in Z_AT:
                            prepare_z(*nxt, s + 1, *divmod(Z_AT.index(g), 2))
                        if nxt and g in BC_AT:
                            prepare_bc(*nxt, s + 1, *divmod(BC_AT.index(g), 2))

                def warm():
                    for n in range(4):
                        prepare_z(*place(0), 0, *divmod(n, 2))
                    for n in range(4):
                        prepare_bc(*place(0), 0, *divmod(n, 2))

                def tail():
                    for g in range(NG - LAG, NG):
                        sum_states(NSTEP - 1, g)

                run(pe, body, warm, tail)

            @block.scalar
            def _(act):
                act.preload_act_table_set("natural_log_exp_and_others")
                act.wait_ge(S.weights, 48)
                act.activation(neg_a, neg_a, ACT.Exp).then_inc(S.a_exp, 1)
                for n in range(2 * K):
                    act.wait_ge(S.wz_made, n + 1)
                    act.activation(wz[:, n // 2, n % 2, :], ps[0:HC, n % 4, 0:C], ACT.Copy).then_inc(S.wz_ready, 1)
                act.wait_ge(S.a_ready, 1)

                def abs_relu(k, s, h):
                    act.wait_ge(S.z_ready, 2 * s + h + 1)
                    if h == 0 and (not isinstance(s, int) or s):
                        for q in range(NQ // 2):
                            act.wait_ge(stacked[q], 48 * s)
                    act.activation(e_buf[:, h, :], ps[0:HC, PBANK + h, :], ACT.Abs, bias=dtb[:, h, k:k + 1])\
                       .then_inc(S.absz, 1)
                    act.activation(relu_buf[:, h, :], ps[0:HC, PBANK + h, :], ACT.Relu, bias=dtb[:, h, k:k + 1])\
                       .then_inc(S.reluz, 1)

                def exp_z(s):
                    act.wait_ge(S.absz, 2 * s + 2)
                    act.activation(e_buf, e_buf, ACT.Exp, scale=-1.0).then_inc(S.expz, 1)

                def log_z(s):
                    act.wait_ge(S.expz, s + 1)
                    act.activation(log_buf, e_buf, ACT.Ln, bias=1.0).then_inc(S.logz, 1)

                def square_e(s):
                    act.activation(poly_buf, e_buf, ACT.Square, scale=float(np.sqrt(0.5))).then_inc(S.sqz, 1)

                def copy_b(s):
                    act.wait_ge(S.b_made, s + 1)
                    if not isinstance(s, int) or s:
                        act.wait_ge(S.u_made, s * NG)
                    act.activation(b_rep, ps[:, PBANK, :], ACT.Copy).then_inc(S.b_ready, 1)

                def copy_c(s):
                    act.wait_ge(S.c_made, s + 1)
                    if not isinstance(s, int) or s:
                        act.wait_ge(S.hc_made, s * NG)
                    act.activation(c_rep, ps[:, PBANK + 1, :], ACT.Copy).then_inc(S.c_ready, 1)

                def body(k, i, s, prev, nxt):
                    for g in range(NG):
                        if g == 1:
                            copy_c(s)
                        act.wait_ge(S.dt_spread, s * NG + g + 1)
                        bank = ps[:, DBANK + g % 2, :]
                        act.activation(bank, bank, ACT.Exp, scale=neg_a[:, k * NG + g:k * NG + g + 1])\
                           .then_inc(S.decay, 1)
                        if nxt and g in ABS_AT:
                            abs_relu(nxt[0], s + 1, ABS_AT.index(g))
                        if nxt and g == EXP_AT:
                            exp_z(s + 1)
                        if nxt and g == EXP_AT + 1:
                            log_z(s + 1)
                        if nxt and g == EXP_AT + 2:
                            square_e(s + 1)
                    if nxt:
                        copy_b(s + 1)

                def warm():
                    for h in range(2):
                        abs_relu(0, 0, h)
                    exp_z(0)
                    log_z(0)
                    square_e(0)
                    copy_b(0)

                run(act, body, warm, lambda: None)

            @block.vector
            def _(v):
                v.wait_ge(S.a_exp, 1)
                v.tensor_scalar(neg_a, neg_a, -1.0, None, ALU.mult).then_inc(S.a_ready, 1)

                def make_u(s, g):
                    v.wait_ge(S.dx_spread, s * NG + g + 1)
                    if g == 0:
                        v.wait_ge(S.b_ready, s + 1)
                    if not isinstance(s, int) or s or g >= 3:
                        v.wait_ge(S.h_made, s * NG + g - 2)
                    v.tensor_tensor(u[:, g % 3, :], ps[:, XBANK + g % 2, :], b_rep, ALU.mult).then_inc(S.u_made, 1)

                def make_h(k, i, s, g):
                    v.wait_ge(S.decay, s * NG + g + 1)
                    v.wait_ge(S.u_made, s * NG + g + 1)
                    if not isinstance(s, int) or s:
                        v.wait_ge(S.hc_made, (s - 1) * NG + g + 1)
                        v.wait_ge(S.h_made, (s - 1) * NG + g + 1)
                    first = isinstance(s, int) and s % NCH == 0
                    last = T - 1 if k < 2 else 0
                    v.tensor_tensor_scan(flip(hs[:, g, :], k), flip(ps[:, DBANK + g % 2, :], k), flip(u[:, g % 3, :], k),
                                         0.0 if first else hs[:, g, last:last + 1], ALU.mult, ALU.add)\
                     .then_inc(S.h_made, 1)

                def big(s):
                    v.wait_ge(S.logz, s + 1)
                    v.scalar_tensor_tensor(log_buf, e_buf, SMALL, log_buf, ALU.is_ge, ALU.mult).then_inc(S.big, 1)

                def either(s):
                    v.wait_ge(S.big, s + 1)
                    v.wait_ge(S.poly, s + 1)
                    v.tensor_tensor(dt, log_buf, poly_buf, ALU.max).then_inc(S.logs, 1)

                def rest(s, value, left, ready, done):
                    v.wait_ge(ready, s + 1)
                    v.tensor_tensor(left, value, top_half(value), ALU.subtract).then_inc(done, 1)

                rests = ((dt, dt1, S.dt_made, S.dt_r1), (dt1, dt2, S.dt_r1, S.dt_r2),
                         (dx, dx1, S.dx_made, S.dx_r1), (dx1, dx2, S.dx_r1, S.dx_r2))

                def add_y(pk, pi, s, half):
                    v.wait_ge(S.summed, s * NG + NGH * (half + 1))
                    dst = px(ys[:, half, :], pk, pi)
                    v.tensor_tensor(dst, dst, shape(ps[0:HC, YBANK + half, :]), ALU.add).then_inc(S.y_added, 1)

                def body(k, i, s, prev, nxt):
                    make_u(s, 0)
                    for g in range(NG):
                        if g + 1 < NG:
                            make_u(s, g + 1)
                        make_h(k, i, s, g)
                        if prev and g == LAG + 1:
                            add_y(*prev, s - 1, 1)
                        if g == NGH + LAG + 1:
                            add_y(k, i, s, 0)
                        if nxt and g == BIG_AT:
                            big(s + 1)
                        if nxt and g == EITHER_AT:
                            either(s + 1)
                        if nxt and g in RESTS_AT:
                            rest(s + 1, *rests[RESTS_AT.index(g)])

                def warm():
                    big(0)
                    either(0)
                    for r in rests:
                        rest(0, *r)

                run(v, body, warm, lambda: add_y(*place(NSTEP - 1), NSTEP - 1, 1))

            @block.gpsimd
            def _(pool):
                def poly(s):
                    pool.wait_ge(S.sqz, s + 1)
                    pool.tensor_tensor(poly_buf, e_buf, poly_buf, ALU.subtract).then_inc(S.poly, 1)

                def add_relu(s):
                    pool.wait_ge(S.logs, s + 1)
                    pool.wait_ge(S.reluz, 2 * s + 2)
                    pool.tensor_tensor(dt, dt, relu_buf, ALU.add).then_inc(S.dt_made, 1)

                def times_x(k, i, s):
                    pool.wait_ge(S.dt_made, s + 1)
                    for h in range(2):
                        m = pool.tensor_tensor(shape(dx[:, h, :]), shape(dt[:, h, :]), px(xs[:, h, :], k, i), ALU.mult)
                    m.then_inc(S.dx_made, 1)

                def warm():
                    poly(0)
                    add_relu(0)
                    times_x(*place(0), 0)

                def body(k, i, s, prev, nxt):
                    for g in range(NG):
                        if g == 0:
                            pool.wait_ge(S.c_ready, s + 1)
                        pool.wait_ge(S.h_made, s * NG + g + 1)
                        if not (isinstance(s, int) and s == 0 and g < NHC):
                            pool.wait_ge(S.summed, s * NG + (g - NHC + 1))
                        pool.tensor_tensor(hc[:, g % NHC, :], hs[:, g, :], c_rep, ALU.mult).then_inc(S.hc_made, 1)
                        if nxt and g == POLY_AT:
                            poly(s + 1)
                        if nxt and g == ADD_AT:
                            add_relu(s + 1)
                        if nxt and g == ADD_AT + 1:
                            times_x(*nxt, s + 1)

                run(pool, body, warm, lambda: None)
        for q in range(NQ // 2):
            nc.gpsimd.sem_clear(stacked[q])
        end_phase(nc, S)


def layer0_after(nc, t, b):
    cv = Carver(t.arena)
    wt = cv.take(HC, L1_N)
    w = {n: wt[:, a:e] for n, (a, e) in L1_W.items()}
    ca1 = w["ca1"].rearrange("p (h m) -> p h m", h=2)
    ca2 = cv.take(12, C)
    cab = cv.take(HC, 3)
    xc, sq, yn, gate = (take_pair(cv, 2) for _ in range(4))
    rstd = take_pair(cv, 1)
    part, mean, hid, att = cv.take(HC, 2 * NCH), cv.take(HC, 2), cv.take(12, 1), cv.take(HC, 2)
    part = part.rearrange("p (h i) -> p h i", h=2)
    xs, ys, ps = halves(t.xs[0:HC, :], L), halves(t.ys[0:HC, :], L), t.ps
    mean_bank, var_bank = [ps[0:HC, 4 * n, :] for n in range(2)], [ps[0:HC, 4 * n + 1, :] for n in range(2)]
    with ExitStack() as stack:
        G = semaphores(nc, stack, "weights image mean_done hid_made hid_done att_made att_done added")
        S = semaphore_pair(nc, stack, LN_SEMS + " gate_loaded gated part_done")
        with nc.Block() as block:
            @block.sync
            def _(sp):
                sp.dma_start(wt, t.inp["l1_w"]).then_inc(G.weights, 16)
                sp.dma_start(ca2, t.inp["ca2"]).then_inc(G.weights, 16)
                sp.dma_start(cab, t.inp["cab"]).then_inc(G.weights, 16)

                def load_gates(r):
                    for n in range(2):
                        sp.wait_ge(S[n].gated, r)
                        sp.dma_start(gate[n], t.gate_scratch[:, :, bass.ds((2 * r + n) * T, T)])\
                          .then_inc(S[n].gate_loaded, 16)

                load_gates(0)
                sp.dma_start(xs, t.inp["x_in"][b].rearrange("(h p) l -> p h l", h=2)).then_inc(G.image, 16)
                with sp.Fori(1, PAIRS) as r:
                    load_gates(r)

            @block.tensor
            def _(pe):
                pe.wait_ge(G.weights, 48)
                with pe.Fori(0, PAIRS) as r:
                    for n in range(2):
                        pe.wait_ge(S[n].ln_centered, r)
                        ln_mean(pe, S[n], mean_bank[n], w["mean"], chunk(ys, 2 * r + n))
                    for n in range(2):
                        pe.wait_ge(S[n].ln_std, r)
                        ln_variance(pe, S[n], r, var_bank[n], w["mean"], sq[n])
                pe.wait_ge(G.mean_done, 1)
                for h in range(2):
                    m = pe.matmul(ps[0:12, 2, 0:1], ca1[:, h, :], mean[:, h:h + 1], start=h == 0, stop=h == 1)
                m.then_inc(G.hid_made, 1)
                pe.wait_ge(G.hid_done, 1)
                for h in range(2):
                    m = pe.matmul(ps[0:HC, 2 + 4 * h, 1:2], ca2[:, h * HC:(h + 1) * HC], hid, start=True, stop=True)
                m.then_inc(G.att_made, 1)

            @block.scalar
            def _(act):
                act.preload_act_table_set("natural_log_exp_and_others")
                act.wait_ge(G.weights, 48)
                with act.Fori(0, PAIRS) as r:
                    for n in range(2):
                        ln_square(act, S[n], r, xc[n], sq[n])
                    ln_root(act, S, r, var_bank, rstd, t.eps)
                    for n in range(2):
                        act.wait_ge(S[n].gated, r)
                        ln_bias(act, S[n], r, xc[n], w["l0b"], yn[n])
                act.wait_ge(G.hid_made, 1)
                act.activation(hid, ps[0:12, 2, 0:1], ACT.Relu, bias=cab[0:12, 2:3], scale=1.0 / L).then_inc(G.hid_done, 1)
                act.wait_ge(G.att_made, 1)
                for h in range(2):
                    act.activation(att[:, h:h + 1], ps[0:HC, 2 + 4 * h, 1:2], ACT.Sigmoid, bias=cab[:, h:h + 1])\
                       .then_inc(G.att_done, 1)

            @block.vector
            def _(v):
                v.wait_ge(G.weights, 48)
                with v.Fori(0, PAIRS) as r:
                    for n in range(2):
                        v.wait_ge(S[n].ln_out, r)
                        ln_centre(v, S[n], r, mean_bank[n], chunk(ys, 2 * r + n), xc[n])
                    for n in range(2):
                        ln_scale(v, S[n], r, xc[n], rstd[n], w["l0g"])
                    for n in range(2):
                        v.wait_ge(S[n].ln_out, r + 1)
                        v.wait_ge(S[n].gate_loaded, 16 * (r + 1))
                        v.tensor_tensor(chunk(ys, 2 * r + n), yn[n], gate[n], ALU.mult).then_inc(S[n].gated, 1)
                    for n in range(2):
                        v.wait_ge(S[n].gated, r + 1)
                        v.tensor_reduce(part[:, :, bass.ds(2 * r + n, 1)], chunk(ys, 2 * r + n), AX.X, ALU.add)\
                         .then_inc(S[n].part_done, 1)
                for n in range(2):
                    v.wait_ge(S[n].part_done, PAIRS)
                v.tensor_reduce(mean, part, AX.X, ALU.add).then_inc(G.mean_done, 1)
                v.wait_ge(G.image, 16)
                for h in range(2):
                    v.wait_ge(G.att_done, h + 1)
                    v.scalar_tensor_tensor(xs[:, h, :], ys[:, h, :], att[:, h:h + 1], xs[:, h, :], ALU.mult, ALU.add)\
                     .then_inc(G.added, 1)
        end_phase(nc, S[0] + S[1] + G)


def layer1(nc, t):
    cv = Carver(t.arena)
    wt = cv.take(HC, L1_N)
    w = {n: wt[:, a:e] for n, (a, e) in L1_W.items()}
    half2 = lambda n: w[n].rearrange("p (h o) -> p h o", h=2)
    win, ssmin, wx2, so, wo = (half2(n) for n in ("win", "ssmin", "wx2", "so", "wo"))
    xb, xcw, xd, dtb, dd = (half2(n) for n in ("xb", "xc", "xd", "dtb", "D"))
    dtw = cv.take(K * DTR1, K * C).rearrange("p (k c) -> p k c", k=K)
    pick = cv.take(K * DS1, K * HC).rearrange("p (k c) -> p k c", k=K)
    wu = cv.take(HC, 4 * C).rearrange("p (h o) -> p h o", h=2)
    xc, sq, xn, xss, z, sx2, ez, rz, gain, term = (take_pair(cv, 2) for _ in range(10))
    rstd = take_pair(cv, 1)
    dsum, dsum2 = cv.take(HC, 2), cv.take(HC, 2)
    ddp = cv.take(HC, 2 * K)
    rows_b, bc = ([cv.take(K * DS1, T) for _ in range(2)] for _ in range(2))
    rows_dt = [cv.take(K * DTR1, T) for _ in range(2)]
    xs, ys, ps = halves(t.xs[0:HC, :], L), halves(t.ys[0:HC, :], L), t.ps
    mean_bank, var_bank = [ps[0:HC, 4 * n, :] for n in range(2)], [ps[0:HC, 4 * n + 1, :] for n in range(2)]
    low = [ps[0:HC, 4 * n:4 * n + 2, :] for n in range(2)]
    high = [ps[0:HC, 4 * n + 2:4 * n + 4, :] for n in range(2)]
    with ExitStack() as stack:
        G = semaphores(nc, stack, "weights wu_made wu_ready dsum_done dsum2_done init_done")
        S = semaphore_pair(nc, stack, LN_SEMS + " uss_made uz_made x2_made xss_done z_done sx2_done rows_made "
                           "dt_rows_made b_copied dt_copied bc_done dt_z bc_spread abs_done exp_done log_done relu_done "
                           "dt_done term_done gain_done y_done yz_done out_made s_done o_made x_done")
        M = semaphore_pair(nc, stack, LN_SEMS, "second_")
        with nc.Block() as block:
            @block.sync
            def _(sp):
                sp.dma_start(wt, t.inp["l1_w"]).then_inc(G.weights, 16)
                sp.dma_start(dtw, t.inp["l1_dtw"].rearrange("p (k c) -> p k c", k=K)).then_inc(G.weights, 16)
                sp.dma_start(pick, t.inp["pick"].rearrange("p (k c) -> p k c", k=K)).then_inc(G.weights, 16)
                sp.dma_start(ddp, t.inp["l2_d"]).then_inc(G.weights, 16)

            @block.tensor
            def _(pe):
                pe.wait_ge(G.weights, 64)
                for h in range(2):
                    for m in range(2):
                        mm = pe.matmul(ps[0:HC, h, 0:2 * C], win[:, m, h * HC:(h + 1) * HC], ssmin[:, m, :],
                                       start=m == 0, stop=m == 1)
                    mm.then_inc(G.wu_made, 1)
                pe.wait_ge(G.wu_ready, 2)
                with pe.Fori(0, PAIRS) as r:
                    for n in range(2):
                        pe.wait_ge(S[n].x_done, r)
                        ln_mean(pe, S[n], mean_bank[n], w["mean"], chunk(xs, 2 * r + n))
                    for n in range(2):
                        ln_variance(pe, S[n], r, var_bank[n], w["mean"], sq[n])
                    for n in range(2):
                        pe.wait_ge(S[n].ln_out, r + 1)
                        pe.wait_ge(S[n].s_done, r)
                        conv192(pe, ps, (4 * n + 2, 4 * n + 3), wu, xn[n]).then_inc(S[n].uss_made, 1)
                        conv192(pe, ps, (4 * n, 4 * n + 1), wu[:, :, C:2 * C], xn[n]).then_inc(S[n].uz_made, 1)
                    for n in range(2):
                        pe.wait_ge(S[n].xss_done, r + 1)
                        conv192(pe, ps, (4 * n + 2, 4 * n + 3), wx2, xn[n]).then_inc(S[n].x2_made, 1)
                    for n in range(2):
                        pe.wait_ge(S[n].z_done, r + 1)
                        for bank, wm in ((0, xb), (1, xcw)):
                            for h in range(2):
                                m = pe.matmul(ps[0:K * DS1, 4 * n + bank, :], wm[:, h, :], xss[n][:, h, :],
                                              start=h == 0, stop=h == 1)
                        m.then_inc(S[n].rows_made, 1)
                        pe.wait_ge(S[n].sx2_done, r + 1)
                        for h in range(2):
                            m = pe.matmul(ps[0:K * DTR1, 4 * n + 2, :], xd[:, h, :], xss[n][:, h, :],
                                          start=h == 0, stop=h == 1)
                        m.then_inc(S[n].dt_rows_made, 1)
                    for k in range(K):
                        for n in range(2):
                            if k == 0:
                                pe.wait_ge(S[n].dt_copied, r + 1)
                            else:
                                pe.wait_ge(S[n].relu_done, K * r + k)
                            for h in range(2):
                                m = pe.matmul(ps[0:HC, 4 * n + 2 + h, :], dtw[:, k, h * HC:(h + 1) * HC], rows_dt[n],
                                              start=True, stop=True)
                            m.then_inc(S[n].dt_z, 1)
                        for n in range(2):
                            if k == 0:
                                pe.wait_ge(S[n].bc_done, r + 1)
                            elif k >= 2:
                                pe.wait_ge(S[n].term_done, 2 * K * r + 2 * (k - 1))
                            pe.matmul(ps[0:HC, 4 * n + k % 2, :], pick[:, k, :], bc[n], start=True, stop=True)\
                              .then_inc(S[n].bc_spread, 1)
                    for n in range(2):
                        pe.wait_ge(S[n].y_done, r + 1)
                        ln_mean(pe, M[n], mean_bank[n], w["mean"], gain[n])
                    for n in range(2):
                        ln_variance(pe, M[n], r, var_bank[n], w["mean"], sq[n])
                    for n in range(2):
                        pe.wait_ge(S[n].yz_done, r + 1)
                        conv192(pe, ps, (4 * n + 2, 4 * n + 3), so, xc[n]).then_inc(S[n].out_made, 1)
                    for n in range(2):
                        pe.wait_ge(S[n].s_done, r + 1)
                        conv192(pe, ps, (4 * n, 4 * n + 1), wo, z[n]).then_inc(S[n].o_made, 1)

            @block.scalar
            def _(act):
                act.wait_ge(G.weights, 64)
                for h in range(2):
                    act.wait_ge(G.wu_made, h + 1)
                    act.activation(wu[:, h, :], ps[0:HC, h, 0:2 * C], ACT.Copy).then_inc(G.wu_ready, 1)
                act.preload_act_table_set("natural_log_exp_and_others")
                with act.Fori(0, PAIRS) as r:
                    for n in range(2):
                        ln_square(act, S[n], r, xc[n], sq[n])
                    ln_root(act, S, r, var_bank, rstd, t.eps)
                    for n in range(2):
                        act.wait_ge(S[n].x2_made, r)
                        ln_bias(act, S[n], r, xc[n], w["b"], xn[n])
                    for n in range(2):
                        act.wait_ge(S[n].uss_made, r + 1)
                        act.activation(xss[n], high[n], ACT.Silu).then_inc(S[n].xss_done, 1)
                        act.wait_ge(S[n].uz_made, r + 1)
                        act.wait_ge(S[n].o_made, r)
                        act.activation(z[n], low[n], ACT.Silu).then_inc(S[n].z_done, 1)
                    for n in range(2):
                        act.wait_ge(S[n].x2_made, r + 1)
                        act.activation(sx2[n], high[n], ACT.Silu).then_inc(S[n].sx2_done, 1)
                    act.preload_act_table_set("natural_log_exp_and_others")
                    for n in range(2):
                        act.wait_ge(S[n].rows_made, r + 1)
                        act.activation(rows_b[n], ps[0:K * DS1, 4 * n, :], ACT.Copy).then_inc(S[n].b_copied, 1)
                        act.wait_ge(S[n].dt_rows_made, r + 1)
                        act.activation(rows_dt[n], ps[0:K * DTR1, 4 * n + 2, :], ACT.Copy).then_inc(S[n].dt_copied, 1)
                    for k in range(K):
                        for n in range(2):
                            act.wait_ge(S[n].dt_z, K * r + k + 1)
                            act.wait_ge(S[n].dt_done, K * r + k)
                            for out, func, done in ((ez, ACT.Abs, S[n].abs_done), (rz, ACT.Relu, S[n].relu_done)):
                                for h in range(2):
                                    m = act.activation(out[n][:, h, :], ps[0:HC, 4 * n + 2 + h, :], func,
                                                       bias=dtb[:, h, k:k + 1])
                                m.then_inc(done, 1)
                        for n in range(2):
                            act.wait_ge(S[n].abs_done, K * r + k + 1)
                            act.activation(ez[n], ez[n], ACT.Exp, scale=-1.0).then_inc(S[n].exp_done, 1)
                        for n in range(2):
                            act.wait_ge(S[n].exp_done, K * r + k + 1)
                            act.activation(ez[n], ez[n], ACT.Ln, bias=1.0).then_inc(S[n].log_done, 1)
                    for n in range(2):
                        ln_square(act, M[n], r, xc[n], sq[n])
                    ln_root(act, M, r, var_bank, rstd, t.eps)
                    for n in range(2):
                        ln_bias(act, M[n], r, xc[n], w["ob"], xc[n])

            @block.vector
            def _(v):
                v.wait_ge(G.weights, 64)
                v.tensor_reduce(dsum, dd, AX.X, ALU.add).then_inc(G.dsum_done, 1)
                v.tensor_reduce(dsum2, ddp.rearrange("p (h k) -> p h k", h=2), AX.X, ALU.add).then_inc(G.dsum2_done, 1)
                v.wait_ge(G.dsum_done, 1)
                v.wait_ge(G.dsum2_done, 1)
                with v.Fori(0, PAIRS) as r:
                    for n in range(2):
                        v.wait_ge(S[n].out_made, r)
                        ln_centre(v, S[n], r, mean_bank[n], chunk(xs, 2 * r + n), xc[n])
                    for n in range(2):
                        ln_scale(v, S[n], r, xc[n], rstd[n], w["g"])
                    for n in range(2):
                        v.wait_ge(S[n].b_copied, r + 1)
                        v.wait_ge(S[n].bc_spread, K * r)
                        v.tensor_tensor(bc[n], rows_b[n], ps[0:K * DS1, 4 * n + 1, :], ALU.mult).then_inc(S[n].bc_done, 1)
                    for k in range(K):
                        out = term if k else gain
                        for n in range(2):
                            v.wait_ge(S[n].relu_done, K * r + k + 1)
                            v.wait_ge(S[n].log_done, K * r + k + 1)
                            if k >= 2:
                                v.wait_ge(S[n].gain_done, (K - 1) * r + k - 1)
                            v.tensor_tensor(out[n], ez[n], rz[n], ALU.add).then_inc(S[n].dt_done, 1)
                        for n in range(2):
                            v.wait_ge(S[n].dt_done, K * r + k + 1)
                            v.wait_ge(S[n].bc_spread, K * r + k + 1)
                            for h in range(2):
                                v.tensor_tensor(out[n][:, h, :], out[n][:, h, :], ps[0:HC, 4 * n + k % 2, :], ALU.mult)\
                                 .then_inc(S[n].term_done, 1)
                        if k:
                            for n in range(2):
                                v.wait_ge(S[n].term_done, 2 * K * r + 2 * (k + 1))
                                if k >= 2:
                                    v.wait_ge(S[n].gain_done, (K - 1) * r + k - 1)
                                v.tensor_tensor(gain[n], gain[n], term[n], ALU.add).then_inc(S[n].gain_done, 1)
                    for n in range(2):
                        v.wait_ge(S[n].gain_done, (K - 1) * (r + 1))
                        for h in range(2):
                            m = v.scalar_tensor_tensor(gain[n][:, h, :], gain[n][:, h, :], dsum[:, h:h + 1],
                                                       xss[n][:, h, :], ALU.add, ALU.mult)
                        m.then_inc(S[n].y_done, 1)
                    for n in range(2):
                        ln_centre(v, M[n], r, mean_bank[n], gain[n], xc[n])
                    for n in range(2):
                        ln_scale(v, M[n], r, xc[n], rstd[n], w["og"])
                    for n in range(2):
                        v.wait_ge(M[n].ln_out, r + 1)
                        v.tensor_tensor(xc[n], xc[n], z[n], ALU.mult).then_inc(S[n].yz_done, 1)
                    for n in range(2):
                        v.wait_ge(S[n].out_made, r + 1)
                        v.wait_ge(S[n].yz_done, r + 1)
                        v.tensor_tensor(z[n], high[n], sx2[n], ALU.mult).then_inc(S[n].s_done, 1)
                    for n in range(2):
                        v.wait_ge(S[n].o_made, r + 1)
                        v.tensor_tensor(chunk(xs, 2 * r + n), chunk(xs, 2 * r + n), low[n], ALU.add).then_inc(S[n].x_done, 1)
                for n in range(2):
                    v.wait_ge(S[n].x_done, PAIRS)
                for h in range(2):
                    v.tensor_scalar(ys[:, h, :], xs[:, h, :], dsum2[:, h:h + 1], None, ALU.mult).then_inc(G.init_done, 1)
        end_phase(nc, S[0] + S[1] + M[0] + M[1] + G)


def layer3_first(nc, t):
    cv = Carver(t.arena)
    xc64 = cv.take(CB, L)
    wt, wt2 = cv.take(HC, L3_N), cv.take(128, L3B_N)
    w = {n: wt[:, a:e] for n, (a, e) in L3_W.items()}
    w1 = w["w1"].rearrange("p (h o) -> p h o", h=2)
    b1 = wt2[0:CB, slice(*L3B_W["b1"])]
    xc, sq, rstd = take_pair(cv, 2), take_pair(cv, 2), take_pair(cv, 1)
    ys, ps = halves(t.ys[0:HC, :], L), t.ps
    mean_bank, var_bank = [ps[0:HC, 4 * n, :] for n in range(2)], [ps[0:HC, 4 * n + 1, :] for n in range(2)]
    with ExitStack() as stack:
        G = semaphores(nc, stack, "weights")
        S = semaphore_pair(nc, stack, LN_SEMS + " conv_made conv_done")
        with nc.Block() as block:
            @block.sync
            def _(sp):
                sp.dma_start(wt, t.inp["l3_w"]).then_inc(G.weights, 16)
                sp.dma_start(wt2, t.inp["l3b_w"]).then_inc(G.weights, 16)

            @block.tensor
            def _(pe):
                pe.wait_ge(G.weights, 32)
                with pe.Fori(0, PAIRS) as r:
                    for n in range(2):
                        pe.wait_ge(S[n].ln_centered, r)
                        ln_mean(pe, S[n], mean_bank[n], w["mean"], chunk(ys, 2 * r + n))
                    for n in range(2):
                        pe.wait_ge(S[n].ln_std, r)
                        ln_variance(pe, S[n], r, var_bank[n], w["mean"], sq[n])
                    for n in range(2):
                        pe.wait_ge(S[n].ln_out, r + 1)
                        pe.wait_ge(S[n].conv_done, r)
                        for h in range(2):
                            m = pe.matmul(ps[:, 4 * n + 2, :], w1[:, h, :], ys[:, h, bass.ds((2 * r + n) * T, T)],
                                          start=h == 0, stop=h == 1)
                        m.then_inc(S[n].conv_made, 1)

            @block.scalar
            def _(act):
                act.preload_act_table_set("natural_log_exp_and_others")
                act.wait_ge(G.weights, 32)
                with act.Fori(0, PAIRS) as r:
                    for n in range(2):
                        ln_square(act, S[n], r, xc[n], sq[n])
                    ln_root(act, S, r, var_bank, rstd, t.eps)
                    for n in range(2):
                        ln_bias(act, S[n], r, xc[n], w["b"], chunk(ys, 2 * r + n))
                    for n in range(2):
                        act.wait_ge(S[n].conv_made, r + 1)
                        act.activation(xc64[:, bass.ds((2 * r + n) * T, T)], ps[0:CB, 4 * n + 2, :], ACT.Identity, bias=b1)\
                           .then_inc(S[n].conv_done, 1)

            @block.vector
            def _(v):
                v.wait_ge(G.weights, 32)
                with v.Fori(0, PAIRS) as r:
                    for n in range(2):
                        v.wait_ge(S[n].ln_out, r)
                        ln_centre(v, S[n], r, mean_bank[n], chunk(ys, 2 * r + n), xc[n])
                    for n in range(2):
                        ln_scale(v, S[n], r, xc[n], rstd[n], w["g"])
        end_phase(nc, S[0] + S[1] + G)


def layer3_windows(nc, t, n_win):
    nw, step, k = WINS[n_win]
    kk, nn = k * k, nw * nw
    P2 = nn // 2
    KP = k + 2
    LU, LP = P2 * kk, P2 * KP * KP
    cv = Carver(t.arena)
    xc = cv.take(CB, L)
    fold12 = cv.take(CB, L)
    at = cv.at
    unf = cv.take(CB, kk * nn).rearrange("p (a b m n) -> p a b m n", a=k, b=k, m=nw)
    cv.at = at
    pad = cv.take(128, LP)
    acc = cv.take(128, LP)
    cv.at = at + 17424
    uc = cv.take(128, LU)
    wt2 = cv.take(128, L3B_N)
    se2 = cv.take(8, 128)
    icnt = xc if nw == 12 else None
    ysum, hid, att = cv.take(128, P2), cv.take(8, P2), cv.take(128, P2)
    w = {n: wt2[:, a:e] for n, (a, e) in L3B_W.items()}
    out = (t.xs[0:CB, 0:L], t.xs[0:CB, L:2 * L], fold12)[n_win]
    pad4 = pad.rearrange("p (n y x) -> p n y x", n=P2, y=KP)
    acc4 = acc.rearrange("p (n y x) -> p n y x", n=P2, y=KP)
    uc4 = uc.rearrange("p (n y x) -> p n y x", n=P2, y=k)
    uc3 = uc.rearrange("p (n r) -> p n r", n=P2)
    ps = t.ps
    total = CB * kk * nn
    flat = t.fold_scratch[0:total]
    as_unf = flat.rearrange("(c j) -> c j", c=CB)
    as_patch = flat.rearrange("(a n c r) -> a c n r", a=2, c=CB, r=kk)
    flat2 = t.fold_scratch2[0:total]
    as_unf2 = flat2.rearrange("(c j) -> c j", c=CB)
    as_patch2 = flat2.rearrange("(a n c r) -> a c n r", a=2, c=CB, r=kk)
    unf2 = unf.rearrange("p a b m n -> p (a b m n)")
    spans = [(a, min(a + T, LU)) for a in range(0, LU, T)]

    with ExitStack() as stack:
        S = semaphores(nc, stack, "weights counts unfolded stored patches cleared padded conv_made conv_done summed hid_made hid_done "
                       "att_made att_done scaled taps joined stored2 unf_loaded folded")
        with nc.Block() as block:
            @block.sync
            def _(sp):
                sp.dma_start(wt2, t.inp["l3b_w"]).then_inc(S.weights, 16)
                sp.dma_start(se2, t.inp["se2"]).then_inc(S.weights, 16)
                sp.wait_ge(S.unfolded, k)
                if icnt is not None:
                    sp.dma_start(icnt, t.inp["inv_count"]).then_inc(S.counts, 16)
                sp.dma_start(as_unf, unf2).then_inc(S.stored, 16)
                sp.wait_ge(S.stored, 16)
                for a in range(2):
                    sp.dma_start(uc3[a * CB:(a + 1) * CB], as_patch[a]).then_inc(S.patches, 16)
                sp.wait_ge(S.joined, 1)
                for a in range(2):
                    sp.dma_start(as_patch2[a], uc3[a * CB:(a + 1) * CB]).then_inc(S.stored2, 16)
                sp.wait_ge(S.stored2, 32)
                sp.dma_start(unf2, as_unf2).then_inc(S.unf_loaded, 16)
                sp.wait_ge(S.unf_loaded, 16)

            @block.gpsimd
            def _(pool):
                for a in range(k):
                    src = as_rows(xc)[:, a:a + step * (nw - 1) + 1:step, :]
                    for c in range(k):
                        m = pool.tensor_copy(unf[:, a, c], src[:, :, c:c + step * (nw - 1) + 1:step])
                    m.then_inc(S.unfolded, 1)
                pool.wait_ge(S.stored, 16)
                pool.memset(pad, 0.0).then_inc(S.cleared, 1)
                pool.wait_ge(S.cleared, 1)
                pool.wait_ge(S.patches, 32)
                pool.tensor_copy(pad4[:, :, 1:k + 1, 1:k + 1], uc4).then_inc(S.padded, 1)

            @block.tensor
            def _(pe):
                pe.wait_ge(S.weights, 32)
                pe.wait_ge(S.patches, 32)
                for n, (a, e) in enumerate(spans):
                    if n >= 4:
                        pe.wait_ge(S.conv_done, n - 3)
                    pe.matmul(ps[:, n % 4, 0:e - a], w["w2"], uc[:, a:e], start=True, stop=True).then_inc(S.conv_made, 1)
                pe.wait_ge(S.summed, 1)
                pe.matmul(ps[0:8, 4, 0:P2], w["se1"], ysum, start=True, stop=True).then_inc(S.hid_made, 1)
                pe.wait_ge(S.hid_done, 1)
                pe.matmul(ps[:, 5, 0:P2], se2, hid, start=True, stop=True).then_inc(S.att_made, 1)

            @block.scalar
            def _(act):
                act.wait_ge(S.padded, 1)
                for n, (a, e) in enumerate(spans):
                    act.wait_ge(S.conv_made, n + 1)
                    act.activation(uc[:, a:e], ps[:, n % 4, 0:e - a], ACT.Identity, bias=w["b2"]).then_inc(S.conv_done, 1)
                act.wait_ge(S.hid_made, 1)
                act.activation(hid, ps[0:8, 4, 0:P2], ACT.Relu, scale=1.0 / kk).then_inc(S.hid_done, 1)
                act.wait_ge(S.att_made, 1)
                act.activation(att, ps[:, 5, 0:P2], ACT.Sigmoid).then_inc(S.att_done, 1)

            @block.vector
            def _(v):
                v.wait_ge(S.weights, 32)
                v.wait_ge(S.padded, 1)
                lo, n = KP + 1, LP - 2 * KP - 2
                for j in range(9):
                    off = lo + (j // 3 - 1) * KP + j % 3 - 1
                    src, dst, tap = pad[:, off:off + n], acc[:, lo:lo + n], w["dw"][:, j:j + 1]
                    if j == 0:
                        v.tensor_scalar(dst, src, tap, w["dwb"], ALU.mult, ALU.add).then_inc(S.taps, 1)
                    else:
                        v.wait_ge(S.taps, j)
                        v.scalar_tensor_tensor(dst, src, tap, dst, ALU.mult, ALU.add).then_inc(S.taps, 1)
                v.wait_ge(S.conv_done, len(spans))
                v.tensor_reduce(ysum, uc3, AX.X, ALU.add).then_inc(S.summed, 1)
                v.wait_ge(S.att_done, 1)
                v.tensor_tensor(uc3, uc3, att.unsqueeze(2).broadcast_to([128, P2, kk]), ALU.mult).then_inc(S.scaled, 1)
                v.wait_ge(S.scaled, 1)
                v.wait_ge(S.taps, 9)
                v.tensor_tensor(uc4, uc4, acc4[:, :, 1:k + 1, 1:k + 1], ALU.add).then_inc(S.joined, 1)
                v.wait_ge(S.unf_loaded, 16)
                img = as_rows(out)
                done = 0
                if step == k:
                    for a in range(k):
                        for c in range(k):
                            v.tensor_copy(img[:, a::k, c::k], unf[:, a, c]).then_inc(S.folded, 1)
                else:
                    v.memset(out, 0.0).then_inc(S.folded, 1)
                    done = 1
                    for a in range(k):
                        for c0, c1 in ((0, step), (step, k)):
                            dst = img[:, a:a + step * (nw - 1) + 1:step, c0 // step * step:]
                            x0 = c0 // step * step
                            rows = img[:, a:a + step * (nw - 1) + 1:step, x0:x0 + step * nw] if x0 + step * nw <= W else None
                            if rows is not None:
                                dst = rows.rearrange("p m (n c) -> p m n c", c=step)[:, :, :, 0:c1 - c0]
                                src = unf[:, a, c0:c1].rearrange("p c m n -> p m n c")
                                v.wait_ge(S.folded, done)
                                v.tensor_tensor(dst, dst, src, ALU.add).then_inc(S.folded, 1)
                                done += 1
                            else:
                                dst = img[:, a:a + step * (nw - 1) + 1:step, x0:x0 + step * (nw - 1)]
                                dst = dst.rearrange("p m (n c) -> p m n c", c=step)[:, :, :, 0:c1 - c0]
                                src = unf[:, a, c0:c1, :, 0:nw - 1].rearrange("p c m n -> p m n c")
                                v.wait_ge(S.folded, done)
                                v.tensor_tensor(dst, dst, src, ALU.add).then_inc(S.folded, 1)
                                x1 = x0 + step * (nw - 1)
                                dst = img[:, a:a + step * (nw - 1) + 1:step, x1:x1 + c1 - c0]
                                src = unf[:, a, c0:c1, :, nw - 1].rearrange("p c m -> p m c")
                                v.wait_ge(S.folded, done + 1)
                                v.tensor_tensor(dst, dst, src, ALU.add).then_inc(S.folded, 1)
                                done += 2
                    v.wait_ge(S.counts, 16)
                    v.wait_ge(S.folded, done)
                    v.tensor_tensor(out, out, icnt, ALU.mult).then_inc(S.folded, 1)
        end_phase(nc, S)


def layer3_last(nc, t, b):
    cv = Carver(t.arena)
    cv.take(CB, L)
    fold12 = cv.take(CB, L)
    wt, wt2 = cv.take(HC, L3_N), cv.take(128, L3B_N)
    w3x = wt[:, slice(*L3_W["w3x"])].rearrange("p (h o) -> p h o", h=2)
    b3 = wt[:, slice(*L3_W["b3"])]
    w3c = wt2[0:CB, slice(*L3B_W["w3c"])].rearrange("p (n o) -> p n o", n=3)
    res = cv.take(HC, 4 * T).rearrange("p (h n t) -> p h n t", h=2, n=2)
    ys, ps = halves(t.ys[0:HC, :], L), t.ps
    folds = (t.xs[0:CB, 0:L], t.xs[0:CB, L:2 * L], fold12)
    out = t.out[b].rearrange("(h p) l -> p h l", h=2)
    with ExitStack() as stack:
        S = semaphores(nc, stack, "weights made0 made1 biased0 biased1 stored0 stored1")
        made, biased, stored = (S.made0, S.made1), (S.biased0, S.biased1), (S.stored0, S.stored1)
        with nc.Block() as block:
            @block.sync
            def _(sp):
                sp.dma_start(wt, t.inp["l3_w"]).then_inc(S.weights, 16)
                sp.dma_start(wt2, t.inp["l3b_w"]).then_inc(S.weights, 16)
                with sp.Fori(0, NCH // 2) as i:
                    for n in range(2):
                        sp.wait_ge(biased[n], i + 1)
                        sp.dma_start(out[:, :, bass.ds((2 * i + n) * T, T)], res[:, :, n, :]).then_inc(stored[n], 16)
                for n in range(2):
                    sp.wait_ge(stored[n], 16 * (NCH // 2))

            @block.tensor
            def _(pe):
                pe.wait_ge(S.weights, 32)
                with pe.Fori(0, NCH // 2) as i:
                    for n in range(2):
                        at = bass.ds((2 * i + n) * T, T)
                        pe.wait_ge(biased[n], i)
                        for o in range(2):
                            bank = ps[0:HC, 2 * n + o, :]
                            cut = slice(o * HC, (o + 1) * HC)
                            for h in range(2):
                                pe.matmul(bank, w3x[:, h, cut], ys[:, h, at], start=h == 0, stop=False)
                            for f in range(3):
                                m = pe.matmul(bank, w3c[:, f, cut], folds[f][:, at], start=False, stop=f == 2)
                        m.then_inc(made[n], 1)

            @block.scalar
            def _(act):
                with act.Fori(0, NCH // 2) as i:
                    for n in range(2):
                        act.wait_ge(made[n], i + 1)
                        act.wait_ge(stored[n], 16 * i)
                        for o in range(2):
                            m = act.activation(res[:, o, n, :], ps[0:HC, 2 * n + o, :], ACT.Identity, bias=b3[:, o:o + 1])
                        m.then_inc(biased[n], 1)
        end_phase(nc, S)


class Tensors:
    pass


def build(nc, d, out):
    t = Tensors()
    t.inp, t.out = d, out
    with ExitStack() as stack:
        sb = lambda n, s, dt: stack.enter_context(nc.sbuf_tensor(n, s, dt))
        t.xs = sb("xs", [128, 2 * L], F32)
        t.ys = sb("ys", [128, 2 * L], F32)
        sel = sb("sel", [HC, 4, 128], BF16)
        gather = sb("gather", [128, (2 * NGH - 1) * CG], F32)
        t.arena = sb("arena", [128, 36350], F32)
        t.ps = stack.enter_context(nc.psum_tensor("ps", [128, 8, T], F32))
        t.gate_scratch = nc.dram_tensor("gate_scratch", (HC, 2, L), F32).ap()
        t.fold_scratch = nc.dram_tensor("fold_scratch", (CB * 81 * 144,), F32).ap()
        t.fold_scratch2 = nc.dram_tensor("fold_scratch2", (CB * 81 * 144,), F32).ap()
        t.sel, t.gather = sel, gather
        t.eps = sb("eps", [128, 1], F32)
        S = semaphores(nc, stack, "constants eps_set")
        with nc.Block() as block:
            @block.gpsimd
            def _(pool):
                pool.memset(t.eps[:, :], EPS).then_inc(S.eps_set, 1)

            @block.sync
            def _(sp):
                sp.dma_start(sel[:, :, :], t.inp["sel_c"]).then_inc(S.constants, 16)
                sp.dma_start(gather[:, :], t.inp["gather_c"]).then_inc(S.constants, 16)
                sp.wait_ge(S.constants, 32)
        with nc.Fori(0, NIMG) as b:
            layer0_before(nc, t, b)
            scan_layer(nc, t, 12, t.inp["s0_w"], t.inp["s0_r"], t.inp["s0_a"], (True, False, True, False))
            layer0_after(nc, t, b)
            layer1(nc, t)
            scan_layer(nc, t, 6, t.inp["s2_w"], t.inp["s2_r"], t.inp["s2_a"], (False, True, False, True))
            layer3_first(nc, t)
            for n in range(3):
                layer3_windows(nc, t, n)
            layer3_last(nc, t, b)


def by_half(w):
    w = np.asarray(w)
    return np.ascontiguousarray(w.reshape(2, HC, -1).transpose(1, 0, 2)).reshape(HC, -1)


def host_layouts(a):
    a = {k: np.asarray(v) for k, v in a.items()}
    f = np.float32
    mean = np.full((HC, HC), 1.0 / C, f)
    d = {"x_in": a["x"].reshape(NIMG, C, L)}

    def put(name, spec, parts):
        assert [n for n, _ in spec.items()] == list(parts), name
        d[name] = np.concatenate([p.reshape(p.shape[0], -1) for p in parts.values()], axis=1)
        assert all(p.size // p.shape[0] == spec[n][1] - spec[n][0] for n, p in parts.items())

    put("pre_w", PRE_W, {
        "p1": by_half(a["L0_conv_p1_w"].T), "p2": by_half(a["L0_conv_p2in_w"].T),
        "g": by_half(a["L0_conv_ln_g"]), "b": by_half(a["L0_conv_ln_b"]),
        "p1b": by_half(a["L0_conv_p1_b"]), "p2b": by_half(a["L0_conv_p2in_b"]),
        "dw": by_half(a["L0_conv_dw_w"].reshape(C, 9)), "dwb": by_half(a["L0_conv_dw_b"]),
        "D": by_half(a["L0_conv_Dp"].T), "mean": mean})
    for s, xp, dp, db, al, rank in (("s0", "L0_conv_x_proj_w", "L0_conv_dt_proj_w", "L0_conv_dt_proj_b", "L0_conv_A_log", 12),
                                    ("s2", "L2_conv_x_proj_weight", "L2_conv_dt_projs_weight", "L2_conv_dt_projs_bias",
                                     "L2_conv_A_logs", 6)):
        w = a[xp]
        rep = {}
        for name, at in (("wb", rank), ("wc", rank + NS)):
            rows = np.tile(w[:, at:at + NS], (1, CG, 1))
            rep[name] = rows.reshape(K, 128, 2, HC).transpose(3, 0, 2, 1)
        put(s + "_w", SCAN_W, {**rep, "dtb": by_half(a[db].T)})
        d[s + "_r"] = np.stack([w[:, :rank].transpose(1, 0, 2), a[dp].transpose(2, 0, 1)], axis=1).reshape(rank, -1)
        al = a[al].reshape(K, NG, CG * NS)
        d[s + "_a"] = np.ascontiguousarray(al.transpose(2, 0, 1)).reshape(128, -1)
    xp = a["L1_conv_x_proj_w"]
    win, ca1 = a["L1_conv_w_in"], a["L0_conv_ca_w1"]
    rows = lambda w: by_half(w.reshape(-1, C).T)
    put("l1_w", L1_W, {
        "win": by_half(win[:C]), "ssmin": by_half(a["L1_conv_ssm_in_w"].T), "wx2": by_half(win[C:].T),
        "xb": rows(xp[:, DTR1:DTR1 + DS1]), "xc": rows(xp[:, DTR1 + DS1:]), "xd": rows(xp[:, :DTR1]),
        "dtb": by_half(a["L1_conv_dt_b"].T), "D": by_half(a["L1_conv_Ds"].reshape(K, C).T),
        "g": by_half(a["L1_conv_norm_w"]), "b": by_half(a["L1_conv_norm_b"]),
        "og": by_half(a["L1_conv_out_norm_w"]), "ob": by_half(a["L1_conv_out_norm_b"]),
        "so": by_half(a["L1_conv_ssm_out_w"].T), "wo": by_half(a["L1_conv_w_out"].T), "mean": mean,
        "l0g": by_half(a["L0_conv_on_g"]), "l0b": by_half(a["L0_conv_on_b"]), "ca1": by_half(ca1.T)})
    dtw = np.zeros((K, DTR1, K, C), f)
    pick = np.zeros((K, DS1, K, HC), f)
    for k in range(K):
        dtw[k, :, k] = a["L1_conv_dt_w"][k].T
        pick[k, :, k] = 1.0
    d["l1_dtw"], d["pick"] = dtw.reshape(K * DTR1, -1), pick.reshape(K * DS1, -1)
    d["l2_d"] = by_half(a["L2_conv_Ds"].reshape(K, C).T)
    d["ca2"] = np.ascontiguousarray(a["L0_conv_ca_w2"].T)
    cab = np.zeros((HC, 3), f)
    cab[:, 0:2] = by_half(a["L0_conv_ca_b2"])
    cab[0:12, 2] = a["L0_conv_ca_b1"]
    d["cab"] = cab
    w3 = a["L3_conv_w3"]
    put("l3_w", L3_W, {"w1": by_half(np.concatenate([a["L3_conv_w1"].T] * 2, axis=1)), "w3x": by_half(w3.T), "b3": by_half(a["L3_conv_b3"]),
                       "g": by_half(a["L2_conv_ln_g"].reshape(C)), "b": by_half(a["L2_conv_ln_b"].reshape(C)), "mean": mean})
    w2 = np.zeros((2, CB, 2, CB), f)
    se1 = np.zeros((2, CB, 2, 4), f)
    se2 = np.zeros((2, 4, 2, CB), f)
    for h in range(2):
        w2[h, :, h] = a["L3_conv_w2"].T
        se1[h, :, h] = a["L3_conv_wse1"].T
        se2[h, :, h] = a["L3_conv_wse2"].T
    two = lambda v: np.concatenate([v.reshape(CB, -1)] * 2, axis=0)
    put("l3b_w", L3B_W, {"w2": w2.reshape(128, 128), "se1": se1.reshape(128, 8), "b2": two(a["L3_conv_b2"]),
                         "dw": two(a["L3_conv_wpos"]), "dwb": two(a["L3_conv_bpos"]),
                         "w3c": two(np.ascontiguousarray(w3.T.reshape(3, CB, C).transpose(1, 0, 2))),
                         "b1": two(a["L3_conv_b1"])})
    d["se2"] = se2.reshape(8, 128)
    bf = mybir.dt.np(BF16)
    sel = np.zeros((3, 4, CG, 4, CG, NS), f)
    for g in range(4):
        for c in range(CG):
            sel[:, g, c, g, c] = 1.0
    d["sel_c"] = sel.reshape(HC, 4, 128).astype(bf)
    gather = np.zeros((CG, NS, (2 * NGH - 1) * CG), f)
    for c in range(CG):
        gather[c, :, (NGH - 1) * CG + c] = 1.0
    d["gather_c"] = gather.reshape(128, -1)
    nw, step, k = WINS[2]
    n = np.zeros(H, f)
    for m in range(nw):
        n[m * step:m * step + k] += 1.0
    d["inv_count"] = np.broadcast_to((1.0 / np.outer(n, n)).reshape(1, L), (CB, L)).astype(f)
    return {n: np.ascontiguousarray(v) for n, v in d.items()}


def kernel(**inputs):
    import concourse.bacc as bacc
    from concourse.bass_utils import run_bass_kernel_spmd

    nc = bacc.Bacc("TRN2", target_bir_lowering=False, num_devices=1)
    arrays = host_layouts(inputs)
    aps = {n: nc.dram_tensor(n, v.shape, mybir.dt.from_np(v.dtype), kind="ExternalInput").ap()
           for n, v in arrays.items()}
    out = nc.dram_tensor("out", (NIMG, C, L), F32, kind="ExternalOutput").ap()
    build(nc, aps, out)
    r = run_bass_kernel_spmd(nc, [arrays], core_ids=[0])
    return r.results[0]["out"].reshape(NIMG, C, H, W)
```

```python
from collections import namedtuple
from contextlib import ExitStack

import numpy as np
import concourse.bass as bass
from concourse import mybir

ALU = mybir.AluOpType
ACT = mybir.ActivationFunctionType
AX = mybir.AxisListType
F32 = mybir.dt.float32
BF16 = mybir.dt.bfloat16

NIMG, C, H, W = 8, 192, 64, 64
L = H * W
HC = C // 2
T = 512
NCH = L // T
PAIRS = NCH // 2
QUAD = 4
ROWS = T // W
K = 4
NS = 16
CG = 128 // NS
NHC = 8
NG = C // CG
NGH = NG // 2
NQ = C // 32
PADW = W + 2
EPS = 1e-5
SMALL = 0.00390625
CB = 64
WINS = ((4, 16, 16), (8, 8, 8), (12, 5, 9))
DTR1, DS1 = 12, 8


def columns(spec):
    out, at = {}, 0
    for name, n in spec:
        out[name] = (at, at + n)
        at += n
    return out, at


PRE_W, PRE_N = columns([("p1", 2 * C), ("p2", 2 * C), ("g", 2), ("b", 2), ("p1b", 2), ("p2b", 2),
                        ("dw", 18), ("dwb", 2), ("D", 2 * K), ("mean", HC)])
SCAN_W, SCAN_N = columns([("wb", 2 * K * 128), ("wc", 2 * K * 128), ("dtb", 2 * K)])
RANK_N = 2 * K * C
L1_W, L1_N = columns([("win", 2 * C), ("ssmin", 4 * C), ("wx2", 2 * C), ("xb", 2 * 32), ("xc", 2 * 32),
                      ("xd", 2 * K * DTR1), ("D", 2 * K), ("g", 2), ("b", 2),
                      ("og", 2), ("ob", 2), ("so", 2 * C), ("wo", 2 * C), ("mean", HC),
                      ("l0g", 2), ("l0b", 2), ("ca1", 2 * 12)])
L3_W, L3_N = columns([("w1", 2 * 2 * CB), ("b3", 2), ("g", 2), ("b", 2), ("mean", HC)])
L3B_W, L3B_N = columns([("w2", 128), ("se1", 8), ("b2", 1), ("dw", 9), ("dwb", 1), ("w3", 3 * C), ("b1", 1)])


def semaphores(nc, stack, names):
    names = names.split()
    return namedtuple("Semaphores", names)(*[stack.enter_context(nc.semaphore(n)) for n in names])


def semaphore_pair(nc, stack, names, prefix="", ways=2):
    names = names.split()
    kind = namedtuple("Semaphores", names)
    return [kind(*[stack.enter_context(nc.semaphore(f"{prefix}{n}{m}")) for n in names]) for m in range(ways)]


def end_phase(nc, sems):
    for s in sems:
        nc.gpsimd.sem_clear(s)
    nc.all_engine_barrier()


class Carver:

    def __init__(self, arena):
        self.arena, self.at = arena, 0

    def take(self, partitions, n):
        a = self.arena[0:partitions, self.at:self.at + n]
        self.at += n
        assert self.at <= self.arena.shape[1], self.at
        return a


def halves(ap, n):
    return ap.rearrange("p (h t) -> p h t", h=2, t=n)


def take_pair(cv, n, ways=2):
    bufs = [cv.take(HC, n * T) for _ in range(ways)]
    return [halves(a, T) for a in bufs] if n == 2 else bufs


def pair_of(ap3, r):
    return ap3[:, :, bass.ds(r * (2 * T), 2 * T)]


def as_rows(ap2):
    return ap2.rearrange("p (y x) -> p y x", x=W)


def chunk(ap3, i):
    return ap3[:, :, bass.ds(i * T, T)]


def top_half(ap):
    if len(ap.shape) == 2:
        return ap.bitcast(BF16).rearrange("p (t two) -> p t two", two=2)[:, :, 1]
    return ap.bitcast(BF16).rearrange("p h (t two) -> p h t two", two=2)[:, :, :, 1]


def conv192(pe, ps, banks, w, x, first=True, last=True):
    for j, bank in enumerate(banks):
        for h in range(2):
            m = pe.matmul(ps[0:HC, bank, :], w[:, h, j * HC:(j + 1) * HC], x[:, h, :],
                          start=first and h == 0, stop=last and h == 1)
    return m


LN_SEMS = "ln_mean ln_centered ln_square ln_var ln_std ln_rstd ln_normed ln_out"


def ln_mean(pe, S, bank, ones, x):
    for h in range(2):
        m = pe.matmul(bank, ones, x[:, h, :], start=h == 0, stop=h == 1)
    m.then_inc(S.ln_mean, 1)


def ln_variance(pe, S, r, bank, ones, sq):
    pe.wait_ge(S.ln_square, r + 1)
    for h in range(2):
        m = pe.matmul(bank, ones, sq[:, h, :], start=h == 0, stop=h == 1)
    m.then_inc(S.ln_var, 1)


def ln_centre(v, S, r, bank, x, xc):
    v.wait_ge(S.ln_mean, r + 1)
    for h in range(2):
        m = v.tensor_tensor(xc[:, h, :], x[:, h, :], bank, ALU.subtract)
    m.then_inc(S.ln_centered, 1)


def ln_scale(v, S, r, xc, rstd, gain):
    v.wait_ge(S.ln_std, r + 1)
    v.reciprocal(rstd, rstd).then_inc(S.ln_rstd, 1)
    v.wait_ge(S.ln_rstd, r + 1)
    for h in range(2):
        m = v.scalar_tensor_tensor(xc[:, h, :], xc[:, h, :], gain[:, h:h + 1], rstd, ALU.mult, ALU.mult)
    m.then_inc(S.ln_normed, 1)


def ln_square(act, S, r, xc, sq):
    act.wait_ge(S.ln_centered, r + 1)
    act.activation(sq, xc, ACT.Square).then_inc(S.ln_square, 1)


def ln_root(act, S, r, banks, rstd, eps):
    for n in range(len(S)):
        act.wait_ge(S[n].ln_var, r + 1)
        act.activation(rstd[n], banks[n], ACT.Sqrt, bias=eps[0:HC, 0:1]).then_inc(S[n].ln_std, 1)


def ln_bias(act, S, r, xc, bias, out):
    act.wait_ge(S.ln_normed, r + 1)
    for h in range(2):
        m = act.activation(out[:, h, :], xc[:, h, :], ACT.Identity, bias=bias[:, h:h + 1])
    m.then_inc(S.ln_out, 1)


def layer0_before(nc, t, b):
    cv = Carver(t.arena)
    wt = cv.take(HC, PRE_N)
    w = {n: wt[:, a:e] for n, (a, e) in PRE_W.items()}
    p1, p2 = (w[n].rearrange("p (h o) -> p h o", h=2) for n in ("p1", "p2"))
    taps = w["dw"].rearrange("p (h k) -> p h k", h=2)
    pad = cv.take(HC, 2 * PADW * PADW).rearrange("p (h y x) -> p h y x", h=2, y=PADW)
    xc, sq, xn, gate = (take_pair(cv, 2) for _ in range(4))
    rstd = take_pair(cv, 1)
    dsum = cv.take(HC, 2)
    x, xs, ps = halves(t.ys[0:HC, :], L), halves(t.xs[0:HC, :], L), t.ps
    mean_bank, var_bank = [ps[0:HC, 4 * n, :] for n in range(2)], [ps[0:HC, 4 * n + 1, :] for n in range(2)]
    with ExitStack() as stack:
        G = semaphores(nc, stack, "weights image0 image1 cleared taps_summed silu_done dsum_done init_done")
        S = semaphore_pair(nc, stack, LN_SEMS + " gate_conv branch_conv gate_done gate_stored branch_padded")

        def run(eng, body):
            body(0, None)
            with eng.Fori(1, PAIRS) as r:
                body(r, r - 1)
            body(None, PAIRS - 1)

        with nc.Block() as block:
            @block.sync
            def _(sp):
                sp.dma_start(wt, t.inp["pre_w"]).then_inc(G.weights, 16)
                image = t.inp["x_in"][b].rearrange("(h p) l -> p h l", h=2)
                sp.dma_start(x[:, :, 0:2 * T], image[:, :, 0:2 * T]).then_inc(G.image0, 16)
                sp.dma_start(x[:, :, 2 * T:L], image[:, :, 2 * T:L]).then_inc(G.image1, 16)
                with sp.Fori(0, PAIRS) as r:
                    for n in range(2):
                        sp.wait_ge(S[n].gate_done, r + 1)
                        sp.dma_start(t.gate_scratch[:, :, bass.ds((2 * r + n) * T, T)], gate[n])\
                          .then_inc(S[n].gate_stored, 16)
                for n in range(2):
                    sp.wait_ge(S[n].gate_stored, 16 * PAIRS)

            @block.gpsimd
            def _(pool):
                nc.gpsimd.memset(pad, 0.0).then_inc(G.cleared, 1)

            @block.tensor
            def _(pe):
                pe.wait_ge(G.weights, 16)
                pe.wait_ge(G.image0, 16)

                def pair(r):
                    if not isinstance(r, int):
                        pe.wait_ge(G.image1, 16)
                    for n in range(2):
                        pe.wait_ge(S[n].branch_padded, r)
                        ln_mean(pe, S[n], mean_bank[n], w["mean"], chunk(x, 2 * r + n))
                    for n in range(2):
                        ln_variance(pe, S[n], r, var_bank[n], w["mean"], sq[n])
                    for n in range(2):
                        pe.wait_ge(S[n].ln_out, r + 1)
                        pe.wait_ge(S[n].gate_done, r)
                        conv192(pe, ps, (4 * n + 2, 4 * n + 3), p1, xn[n]).then_inc(S[n].gate_conv, 1)
                        conv192(pe, ps, (4 * n, 4 * n + 1), p2, xn[n]).then_inc(S[n].branch_conv, 1)

                pair(0)
                with pe.Fori(1, PAIRS) as r:
                    pair(r)

            @block.scalar
            def _(act):
                act.wait_ge(G.cleared, 1)
                act.wait_ge(G.dsum_done, 1)

                def body(r, conv):
                    if r is not None:
                        for n in range(2):
                            ln_square(act, S[n], r, xc[n], sq[n])
                        ln_root(act, S, r, var_bank, rstd, t.eps)
                        for n in range(2):
                            act.wait_ge(S[n].branch_conv, r)
                            ln_bias(act, S[n], r, xc[n], w["b"], xn[n])
                        for n in range(2):
                            act.wait_ge(S[n].gate_conv, r + 1)
                            act.wait_ge(S[n].gate_stored, 16 * r)
                            for h in range(2):
                                m = act.activation(gate[n][:, h, :], ps[0:HC, 4 * n + 2 + h, :], ACT.Silu,
                                                   bias=w["p1b"][:, h:h + 1])
                            m.then_inc(S[n].gate_done, 1)
                            act.wait_ge(S[n].branch_conv, r + 1)
                            for h in range(2):
                                m = act.activation(pad[:, h, bass.ds((2 * r + n) * ROWS + 1, ROWS), 1:W + 1],
                                                   as_rows(ps[0:HC, 4 * n + h, :]), ACT.Identity,
                                                   bias=w["p2b"][:, h:h + 1])
                            m.then_inc(S[n].branch_padded, 1)
                    if conv is not None:
                        rows = pair_of(xs, conv)
                        act.wait_ge(G.taps_summed, 18 * conv + 18)
                        for h in range(2):
                            act.activation(rows[:, h, :], rows[:, h, :], ACT.Silu, bias=w["dwb"][:, h:h + 1])\
                               .then_inc(G.silu_done, 1)
                        for h in range(2):
                            act.wait_ge(G.silu_done, 2 * conv + h + 1)
                            act.activation(pair_of(x, conv)[:, h, :], rows[:, h, :], ACT.Identity,
                                           scale=dsum[:, h:h + 1]).then_inc(G.init_done, 1)

                run(act, body)

            @block.vector
            def _(v):
                v.wait_ge(G.weights, 16)
                v.wait_ge(G.image0, 16)
                v.tensor_reduce(dsum, w["D"].rearrange("p (h k) -> p h k", h=2), AX.X, ALU.add).then_inc(G.dsum_done, 1)

                EARLY = 3

                def convolve(c, ks):
                    for k in ks:
                        for h in range(2):
                            acc = as_rows(pair_of(xs, c)[:, h, :])
                            tap = pad[:, h, bass.ds(c * (2 * ROWS) + k // 3, 2 * ROWS), k % 3:k % 3 + W]
                            if k:
                                v.wait_ge(G.taps_summed, 18 * c + (2 * (k - 1) + h + 1))
                                v.scalar_tensor_tensor(acc, tap, taps[:, h, k:k + 1], acc, ALU.mult, ALU.add)\
                                 .then_inc(G.taps_summed, 1)
                            else:
                                v.tensor_scalar(acc, tap, taps[:, h, 0:1], None, ALU.mult).then_inc(G.taps_summed, 1)

                def body(r, conv):
                    if r is not None:
                        if not isinstance(r, int):
                            v.wait_ge(G.image1, 16)
                        for n in range(2):
                            v.wait_ge(S[n].ln_out, r)
                            ln_centre(v, S[n], r, mean_bank[n], chunk(x, 2 * r + n), xc[n])
                    if conv is not None:
                        v.wait_ge(S[1].branch_padded, conv + 1)
                        convolve(conv, range(0, EARLY))
                    if r is not None:
                        for n in range(2):
                            ln_scale(v, S[n], r, xc[n], rstd[n], w["g"])
                    if conv is not None:
                        convolve(conv, range(EARLY, 6))
                        if r is not None:
                            v.wait_ge(S[0].branch_padded, r + 1)
                        convolve(conv, range(6, 9))

                run(v, body)
        end_phase(nc, S[0] + S[1] + G)


def scan_layer(nc, t, rank, w_scan, w_rank, w_alog, cols):
    NSTEP = K * NCH
    cv = Carver(t.arena)
    wt = cv.take(HC, SCAN_N)
    wb, wc = (wt[:, slice(*SCAN_W[n])].rearrange("p (k h m) -> p k h m", k=K, h=2) for n in ("wb", "wc"))
    dtb = wt[:, slice(*SCAN_W["dtb"])].rearrange("p (h k) -> p h k", h=2)
    wz = cv.take(HC, 2 * K * C).rearrange("p (k h o) -> p k h o", k=K, h=2)
    neg_a = cv.take(128, K * NG)
    hs = cv.take(128, NG * T).rearrange("p (g t) -> p g t", g=NG)
    parts = cv.take(HC, 2 * 3 * 2 * T).rearrange("p (q r h t) -> p q r h t", q=2, r=3, h=2)
    stacks = cv.take(HC, 2 * NQ * T).rearrange("p (q j h t) -> p q j h t", q=2, h=2, t=T)
    u = cv.take(128, 3 * T).rearrange("p (n t) -> p n t", n=3)
    hc = cv.take(128, NHC * T).rearrange("p (n t) -> p n t", n=NHC)
    b_rep, c_rep = cv.take(128, T), cv.take(128, T)
    ranks = hs[0:rank, 0:6, :].rearrange("p g t -> p (g t)")[:, 0:RANK_N]
    ranks = ranks.rearrange("p (w k c) -> p w k c", w=2, k=K)
    xs, ys, ps = halves(t.xs[0:HC, :], L), halves(t.ys[0:HC, :], L), t.ps
    dt, dt1, dt2 = (parts[:, 0, r] for r in range(3))
    dx, dx1, dx2 = (parts[:, 1, r] for r in range(3))
    e_buf, log_buf, relu_buf, poly_buf = dx1, dt, dt2, dx2
    DBANK, XBANK, YBANK, PBANK = 0, 2, 4, 6
    LAG = 5

    Z_AT, BC_AT = (0, 2, 3, 4), (10, 16, 17, 18)
    ABS_AT, EXP_AT = (4, 5), 7
    BIG_AT, EITHER_AT, RESTS_AT = 9, 11, (15, 16, 17, 18)
    SUM_AT = (4, 7)
    POLY_AT, ADD_AT = 8, 10

    def place(s):
        k, i = s // NCH, s % NCH
        return k, i if k < 2 else NCH - 1 - i

    def stack_of(n, g):
        return stacks[:, n, g // 4 % 3, g // NGH, :]

    def flip(ap, k):
        return ap if k < 2 else ap[:, ::-1]

    def px(ap2, k, i):
        lines = ap2.rearrange("p (y x) -> p x y", x=W) if cols[k] else as_rows(ap2)
        return lines[:, bass.ds(i * ROWS, ROWS), :]

    def shape(ap2):
        return as_rows(ap2)

    with ExitStack() as stack:
        S = semaphores(nc, stack, "weights a_exp a_ready wz_made wz_ready z_ready b_made c_made absz expz logz sqz reluz "
                       "poly big logs dt_made dx_made dt_r1 dx_r1 dt_r2 dx_r2 b_ready c_ready "
                       "dt_spread dx_spread decay u_made h_made hc_made summed y_added")
        stacked = [stack.enter_context(nc.semaphore(f"stacked{q}")) for q in range(NQ // 2)]
        steps = []
        for k in range(K):
            steps += [(k, 0), (k, None), (k, NCH - 1)]

        def run(eng, body, warm, tail):
            warm()
            for k, i in steps:
                if i is None:
                    with eng.Fori(1, NCH - 1) as r:
                        if k < 2:
                            body(k, r, k * NCH + r, (k, r - 1), (k, r + 1))
                        else:
                            down = r * -1 + (NCH - 1)
                            body(k, down, k * NCH + r, (k, down + 1), (k, down - 1))
                else:
                    s = k * NCH + i
                    prev, nxt = place(s - 1) if s else None, place(s + 1) if s + 1 < NSTEP else None
                    body(*place(s), s, prev, nxt)
            tail()

        with nc.Block() as block:
            @block.sync
            def _(sp):
                sp.dma_start(wt, w_scan).then_inc(S.weights, 16)
                sp.dma_start(ranks, w_rank.rearrange("p (w k c) -> p w k c", w=2, k=K)).then_inc(S.weights, 16)
                sp.dma_start(neg_a, w_alog).then_inc(S.weights, 16)

                def stack_parts(s):
                    sp.wait_ge(S.dt_r2, s + 1)
                    sp.wait_ge(S.dx_r2, s + 1)
                    for j in range(NQ // 2):
                        if not isinstance(s, int) or s:
                            sp.wait_ge(S.dt_spread, (s - 1) * NG + 4 * (NQ // 2 + j + 1))
                            sp.wait_ge(S.dx_spread, (s - 1) * NG + 4 * (NQ // 2 + j + 1))
                        for r in range(3):
                            sp.dma_start(stacks[32 * r:32 * r + 32, :, j, :, :],
                                         parts[32 * j:32 * j + 32, :, r, :, :]).then_inc(stacked[j], 16)

                run(sp, lambda k, i, s, prev, nxt: nxt and stack_parts(s + 1), lambda: stack_parts(0), lambda: None)

            @block.tensor
            def _(pe):
                pe.wait_ge(S.weights, 48)
                for k in range(K):
                    for h in range(2):
                        n = 2 * k + h
                        if n >= 4:
                            pe.wait_ge(S.wz_ready, n - 3)
                        pe.matmul(ps[0:HC, n % 4, 0:C], ranks[:, 0, k, h * HC:(h + 1) * HC], ranks[:, 1, k, :],
                                  start=True, stop=True).then_inc(S.wz_made, 1)
                pe.wait_ge(S.wz_ready, 2 * K)

                def prepare_z(k, i, s, o, h):
                    if h == 0:
                        pe.wait_ge((S.b_ready, S.c_ready)[o], s)
                    m = pe.matmul(shape(ps[0:HC, PBANK + o, :]), wz[:, k, h, o * HC:(o + 1) * HC],
                                  px(xs[:, h, :], k, i), start=h == 0, stop=h == 1)
                    if h:
                        m.then_inc(S.z_ready, 1)

                def prepare_bc(k, i, s, n, h):
                    if h == 0:
                        pe.wait_ge(S.absz, 2 * s + n + 1)
                        pe.wait_ge(S.reluz, 2 * s + n + 1)
                    m = pe.matmul(shape(ps[:, PBANK + n, :]), (wb, wc)[n][:, k, h, :], px(xs[:, h, :], k, i),
                                  start=h == 0, stop=h == 1)
                    if h:
                        m.then_inc((S.b_made, S.c_made)[n], 1)

                def spread_dt(s, g):
                    wait_used(S.h_made, s, g, 2)
                    pe.matmul(ps[:, DBANK + g % 2, :], t.sel[:, g % 4, :], top_half(stack_of(0, g)),
                              start=True, stop=True).then_inc(S.dt_spread, 1)

                def spread_dx(s, g):
                    if g % 4 == 0 and g < NGH:
                        pe.wait_ge(stacked[g // 4], 48 * (s + 1))
                    wait_used(S.u_made, s, g, 2)
                    pe.matmul(ps[:, XBANK + g % 2, :], t.sel[:, g % 4, :], top_half(stack_of(1, g)),
                              start=True, stop=True).then_inc(S.dx_spread, 1)

                def wait_used(sem, s, g, ahead):
                    if isinstance(s, int) and s * NG + g < ahead:
                        return
                    pe.wait_ge(sem, s * NG + (g - ahead + 1))

                def sum_states(s, g):
                    half, n = g // NGH, g % NGH
                    if n == 0:
                        pe.wait_ge(S.y_added, 2 * s + half - 1) if not (isinstance(s, int) and 2 * s + half < 2) else None
                    pe.wait_ge(S.hc_made, s * NG + g + 1)
                    off = (NGH - 1 - n) * CG
                    pe.matmul(ps[0:HC, YBANK + half, :], t.gather[:, off:off + HC], hc[:, g % NHC, :],
                              start=n == 0, stop=n == NGH - 1).then_inc(S.summed, 1)

                def body(k, i, s, prev, nxt):
                    spread_dx(s, 0)
                    for g in range(NG):
                        spread_dt(s, g)
                        if g + 1 < NG:
                            spread_dx(s, g + 1)
                        if g >= LAG:
                            sum_states(s, g - LAG)
                        elif prev:
                            sum_states(s - 1, NG + g - LAG)
                        if nxt and g in Z_AT:
                            prepare_z(*nxt, s + 1, *divmod(Z_AT.index(g), 2))
                        if nxt and g in BC_AT:
                            prepare_bc(*nxt, s + 1, *divmod(BC_AT.index(g), 2))

                def warm():
                    for n in range(4):
                        prepare_z(*place(0), 0, *divmod(n, 2))
                    for n in range(4):
                        prepare_bc(*place(0), 0, *divmod(n, 2))

                def tail():
                    for g in range(NG - LAG, NG):
                        sum_states(NSTEP - 1, g)

                run(pe, body, warm, tail)

            @block.scalar
            def _(act):
                act.preload_act_table_set("natural_log_exp_and_others")
                act.wait_ge(S.weights, 48)
                act.activation(neg_a, neg_a, ACT.Exp).then_inc(S.a_exp, 1)
                for n in range(2 * K):
                    act.wait_ge(S.wz_made, n + 1)
                    act.activation(wz[:, n // 2, n % 2, :], ps[0:HC, n % 4, 0:C], ACT.Copy).then_inc(S.wz_ready, 1)
                act.wait_ge(S.a_ready, 1)

                def abs_relu(k, s, h):
                    act.wait_ge(S.z_ready, 2 * s + h + 1)
                    if h == 0 and (not isinstance(s, int) or s):
                        for q in range(NQ // 2):
                            act.wait_ge(stacked[q], 48 * s)
                    act.activation(e_buf[:, h, :], ps[0:HC, PBANK + h, :], ACT.Abs, bias=dtb[:, h, k:k + 1])\
                       .then_inc(S.absz, 1)
                    act.activation(relu_buf[:, h, :], ps[0:HC, PBANK + h, :], ACT.Relu, bias=dtb[:, h, k:k + 1])\
                       .then_inc(S.reluz, 1)

                def exp_z(s):
                    act.wait_ge(S.absz, 2 * s + 2)
                    act.activation(e_buf, e_buf, ACT.Exp, scale=-1.0).then_inc(S.expz, 1)

                def log_z(s):
                    act.wait_ge(S.expz, s + 1)
                    act.activation(log_buf, e_buf, ACT.Ln, bias=1.0).then_inc(S.logz, 1)

                def square_e(s):
                    act.activation(poly_buf, e_buf, ACT.Square, scale=float(np.sqrt(0.5))).then_inc(S.sqz, 1)

                def copy_b(s):
                    act.wait_ge(S.b_made, s + 1)
                    if not isinstance(s, int) or s:
                        act.wait_ge(S.u_made, s * NG)
                    act.activation(b_rep, ps[:, PBANK, :], ACT.Copy).then_inc(S.b_ready, 1)

                def copy_c(s):
                    act.wait_ge(S.c_made, s + 1)
                    if not isinstance(s, int) or s:
                        act.wait_ge(S.hc_made, s * NG)
                    act.activation(c_rep, ps[:, PBANK + 1, :], ACT.Copy).then_inc(S.c_ready, 1)

                def body(k, i, s, prev, nxt):
                    for g in range(NG):
                        if g == 1:
                            copy_c(s)
                        act.wait_ge(S.dt_spread, s * NG + g + 1)
                        bank = ps[:, DBANK + g % 2, :]
                        act.activation(bank, bank, ACT.Exp, scale=neg_a[:, k * NG + g:k * NG + g + 1])\
                           .then_inc(S.decay, 1)
                        if nxt and g in ABS_AT:
                            abs_relu(nxt[0], s + 1, ABS_AT.index(g))
                        if nxt and g == EXP_AT:
                            exp_z(s + 1)
                        if nxt and g == EXP_AT + 1:
                            log_z(s + 1)
                        if nxt and g == EXP_AT + 2:
                            square_e(s + 1)
                    if nxt:
                        copy_b(s + 1)

                def warm():
                    for h in range(2):
                        abs_relu(0, 0, h)
                    exp_z(0)
                    log_z(0)
                    square_e(0)
                    copy_b(0)

                run(act, body, warm, lambda: None)

            @block.vector
            def _(v):
                v.wait_ge(S.a_exp, 1)
                v.tensor_scalar(neg_a, neg_a, -1.0, None, ALU.mult).then_inc(S.a_ready, 1)

                def make_u(s, g):
                    v.wait_ge(S.dx_spread, s * NG + g + 1)
                    if g == 0:
                        v.wait_ge(S.b_ready, s + 1)
                    if not isinstance(s, int) or s or g >= 3:
                        v.wait_ge(S.h_made, s * NG + g - 2)
                    v.tensor_tensor(u[:, g % 3, :], ps[:, XBANK + g % 2, :], b_rep, ALU.mult).then_inc(S.u_made, 1)

                def make_h(k, i, s, g):
                    v.wait_ge(S.decay, s * NG + g + 1)
                    v.wait_ge(S.u_made, s * NG + g + 1)
                    if not isinstance(s, int) or s:
                        v.wait_ge(S.hc_made, (s - 1) * NG + g + 1)
                        v.wait_ge(S.h_made, (s - 1) * NG + g + 1)
                    first = isinstance(s, int) and s % NCH == 0
                    last = T - 1 if k < 2 else 0
                    v.tensor_tensor_scan(flip(hs[:, g, :], k), flip(ps[:, DBANK + g % 2, :], k), flip(u[:, g % 3, :], k),
                                         0.0 if first else hs[:, g, last:last + 1], ALU.mult, ALU.add)\
                     .then_inc(S.h_made, 1)

                def big(s):
                    v.wait_ge(S.logz, s + 1)
                    v.scalar_tensor_tensor(log_buf, e_buf, SMALL, log_buf, ALU.is_ge, ALU.mult).then_inc(S.big, 1)

                def either(s):
                    v.wait_ge(S.big, s + 1)
                    v.wait_ge(S.poly, s + 1)
                    v.tensor_tensor(dt, log_buf, poly_buf, ALU.max).then_inc(S.logs, 1)

                def rest(s, value, left, ready, done):
                    v.wait_ge(ready, s + 1)
                    v.tensor_tensor(left, value, top_half(value), ALU.subtract).then_inc(done, 1)

                rests = ((dt, dt1, S.dt_made, S.dt_r1), (dt1, dt2, S.dt_r1, S.dt_r2),
                         (dx, dx1, S.dx_made, S.dx_r1), (dx1, dx2, S.dx_r1, S.dx_r2))

                def add_y(pk, pi, s, half):
                    v.wait_ge(S.summed, s * NG + NGH * (half + 1))
                    dst = px(ys[:, half, :], pk, pi)
                    v.tensor_tensor(dst, dst, shape(ps[0:HC, YBANK + half, :]), ALU.add).then_inc(S.y_added, 1)

                def body(k, i, s, prev, nxt):
                    make_u(s, 0)
                    for g in range(NG):
                        if g + 1 < NG:
                            make_u(s, g + 1)
                        make_h(k, i, s, g)
                        if prev and g in SUM_AT:
                            add_y(*prev, s - 1, SUM_AT.index(g))
                        if nxt and g == BIG_AT:
                            big(s + 1)
                        if nxt and g == EITHER_AT:
                            either(s + 1)
                        if nxt and g in RESTS_AT:
                            rest(s + 1, *rests[RESTS_AT.index(g)])

                def warm():
                    big(0)
                    either(0)
                    for r in rests:
                        rest(0, *r)

                def tail():
                    for half in range(2):
                        add_y(*place(NSTEP - 1), NSTEP - 1, half)

                run(v, body, warm, tail)

            @block.gpsimd
            def _(pool):
                def poly(s):
                    pool.wait_ge(S.sqz, s + 1)
                    pool.tensor_tensor(poly_buf, e_buf, poly_buf, ALU.subtract).then_inc(S.poly, 1)

                def add_relu(s):
                    pool.wait_ge(S.logs, s + 1)
                    pool.wait_ge(S.reluz, 2 * s + 2)
                    pool.tensor_tensor(dt, dt, relu_buf, ALU.add).then_inc(S.dt_made, 1)

                def times_x(k, i, s):
                    pool.wait_ge(S.dt_made, s + 1)
                    for h in range(2):
                        m = pool.tensor_tensor(shape(dx[:, h, :]), shape(dt[:, h, :]), px(xs[:, h, :], k, i), ALU.mult)
                    m.then_inc(S.dx_made, 1)

                def warm():
                    poly(0)
                    add_relu(0)
                    times_x(*place(0), 0)

                def body(k, i, s, prev, nxt):
                    for g in range(NG):
                        if g == 0:
                            pool.wait_ge(S.c_ready, s + 1)
                        pool.wait_ge(S.h_made, s * NG + g + 1)
                        if not (isinstance(s, int) and s == 0 and g < NHC):
                            pool.wait_ge(S.summed, s * NG + (g - NHC + 1))
                        pool.tensor_tensor(hc[:, g % NHC, :], hs[:, g, :], c_rep, ALU.mult).then_inc(S.hc_made, 1)
                        if nxt and g == POLY_AT:
                            poly(s + 1)
                        if nxt and g == ADD_AT:
                            add_relu(s + 1)
                        if nxt and g == ADD_AT + 1:
                            times_x(*nxt, s + 1)

                run(pool, body, warm, lambda: None)
        for q in range(NQ // 2):
            nc.gpsimd.sem_clear(stacked[q])
        end_phase(nc, S)


def layer0_after(nc, t, b):
    cv = Carver(t.arena)
    wt = cv.take(HC, L1_N)
    w = {n: wt[:, a:e] for n, (a, e) in L1_W.items()}
    ca1 = w["ca1"].rearrange("p (h m) -> p h m", h=2)
    ca2 = cv.take(12, C)
    cab = cv.take(HC, 3)
    xc, sq, yn, gate = (take_pair(cv, 2, QUAD) for _ in range(4))
    rstd = take_pair(cv, 1, QUAD)
    part, mean, hid, att = cv.take(HC, 2 * NCH), cv.take(HC, 2), cv.take(12, 1), cv.take(HC, 2)
    part = part.rearrange("p (h i) -> p h i", h=2)
    xs, ys, ps = halves(t.xs[0:HC, :], L), halves(t.ys[0:HC, :], L), t.ps
    mean_bank, var_bank = ([ps[0:HC, 2 * n + m, :] for n in range(QUAD)] for m in range(2))
    with ExitStack() as stack:
        G = semaphores(nc, stack, "weights image mean_done hid_made hid_done att_made att_done added")
        S = semaphore_pair(nc, stack, LN_SEMS + " gate_loaded gated part_done", ways=QUAD)
        with nc.Block() as block:
            @block.sync
            def _(sp):
                sp.dma_start(wt, t.inp["l1_w"]).then_inc(G.weights, 16)
                sp.dma_start(ca2, t.inp["ca2"]).then_inc(G.weights, 16)
                sp.dma_start(cab, t.inp["cab"]).then_inc(G.weights, 16)

                def load_gates(r):
                    for n in range(QUAD):
                        sp.wait_ge(S[n].gated, r)
                        sp.dma_start(gate[n], t.gate_scratch[:, :, bass.ds((QUAD * r + n) * T, T)])\
                          .then_inc(S[n].gate_loaded, 16)

                load_gates(0)
                sp.dma_start(xs, t.inp["x_in"][b].rearrange("(h p) l -> p h l", h=2)).then_inc(G.image, 16)
                with sp.Fori(1, NCH // QUAD) as r:
                    load_gates(r)

            @block.gpsimd
            def _(pool):
                with pool.Fori(0, NCH // QUAD) as r:
                    for n in range(QUAD):
                        pool.wait_ge(S[n].ln_out, r + 1)
                        pool.wait_ge(S[n].gate_loaded, 16 * (r + 1))
                        pool.tensor_tensor(chunk(ys, QUAD * r + n), yn[n], gate[n], ALU.mult).then_inc(S[n].gated, 1)

            @block.tensor
            def _(pe):
                pe.wait_ge(G.weights, 48)
                with pe.Fori(0, NCH // QUAD) as r:
                    for n in range(QUAD):
                        pe.wait_ge(S[n].ln_centered, r)
                        ln_mean(pe, S[n], mean_bank[n], w["mean"], chunk(ys, QUAD * r + n))
                    for n in range(QUAD):
                        pe.wait_ge(S[n].ln_std, r)
                        ln_variance(pe, S[n], r, var_bank[n], w["mean"], sq[n])
                pe.wait_ge(G.mean_done, 1)
                for h in range(2):
                    m = pe.matmul(ps[0:12, 2, 0:1], ca1[:, h, :], mean[:, h:h + 1], start=h == 0, stop=h == 1)
                m.then_inc(G.hid_made, 1)
                pe.wait_ge(G.hid_done, 1)
                for h in range(2):
                    m = pe.matmul(ps[0:HC, 2 + 4 * h, 1:2], ca2[:, h * HC:(h + 1) * HC], hid, start=True, stop=True)
                m.then_inc(G.att_made, 1)

            @block.scalar
            def _(act):
                act.wait_ge(G.weights, 48)
                with act.Fori(0, NCH // QUAD) as r:
                    for n in range(QUAD):
                        ln_square(act, S[n], r, xc[n], sq[n])
                    ln_root(act, S, r, var_bank, rstd, t.eps)
                    for n in range(QUAD):
                        act.wait_ge(S[n].gated, r)
                        ln_bias(act, S[n], r, xc[n], w["l0b"], yn[n])
                act.wait_ge(G.hid_made, 1)
                act.activation(hid, ps[0:12, 2, 0:1], ACT.Relu, bias=cab[0:12, 2:3], scale=1.0 / L).then_inc(G.hid_done, 1)
                act.wait_ge(G.att_made, 1)
                for h in range(2):
                    act.activation(att[:, h:h + 1], ps[0:HC, 2 + 4 * h, 1:2], ACT.Sigmoid, bias=cab[:, h:h + 1])\
                       .then_inc(G.att_done, 1)

            @block.vector
            def _(v):
                v.wait_ge(G.weights, 48)
                with v.Fori(0, NCH // QUAD) as r:
                    for n in range(QUAD):
                        v.wait_ge(S[n].ln_out, r)
                        ln_centre(v, S[n], r, mean_bank[n], chunk(ys, QUAD * r + n), xc[n])
                    for n in range(QUAD):
                        ln_scale(v, S[n], r, xc[n], rstd[n], w["l0g"])
                    for n in range(QUAD):
                        v.wait_ge(S[n].gated, r + 1)
                        v.tensor_reduce(part[:, :, bass.ds(QUAD * r + n, 1)], chunk(ys, QUAD * r + n), AX.X, ALU.add)\
                         .then_inc(S[n].part_done, 1)
                for n in range(QUAD):
                    v.wait_ge(S[n].part_done, NCH // QUAD)
                v.tensor_reduce(mean, part, AX.X, ALU.add).then_inc(G.mean_done, 1)
                v.wait_ge(G.image, 16)
                for h in range(2):
                    v.wait_ge(G.att_done, h + 1)
                    v.scalar_tensor_tensor(xs[:, h, :], ys[:, h, :], att[:, h:h + 1], xs[:, h, :], ALU.mult, ALU.add)\
                     .then_inc(G.added, 1)
        end_phase(nc, S[0] + S[1] + S[2] + S[3] + G)


def layer1(nc, t):
    cv = Carver(t.arena)
    wt = cv.take(HC, L1_N)
    w = {n: wt[:, a:e] for n, (a, e) in L1_W.items()}
    half2 = lambda n: w[n].rearrange("p (h o) -> p h o", h=2)
    win, ssmin, wx2, so, wo = (half2(n) for n in ("win", "ssmin", "wx2", "so", "wo"))
    xb, xcw, xd, dd = (half2(n) for n in ("xb", "xc", "xd", "D"))
    dtw = cv.take(K * DTR1 + 1, K * C).rearrange("p (k c) -> p k c", k=K)
    pick = cv.take(K * DS1, K * HC).rearrange("p (k c) -> p k c", k=K)
    wu = cv.take(HC, 4 * C).rearrange("p (h o) -> p h o", h=2)
    xc, sq, xn, xss, z, sx2, ez, rz, gain, term = (take_pair(cv, 2) for _ in range(10))
    rstd = take_pair(cv, 1)
    dsum, dsum2 = cv.take(HC, 2), cv.take(HC, 2)
    ddp = cv.take(HC, 2 * K)
    rows_b, bc = ([cv.take(K * DS1, T) for _ in range(2)] for _ in range(2))
    rows_dt = [cv.take(K * DTR1 + 1, T) for _ in range(2)]
    xs, ys, ps = halves(t.xs[0:HC, :], L), halves(t.ys[0:HC, :], L), t.ps
    mean_bank, var_bank = [ps[0:HC, 4 * n, :] for n in range(2)], [ps[0:HC, 4 * n + 1, :] for n in range(2)]
    low = [ps[0:HC, 4 * n:4 * n + 2, :] for n in range(2)]
    high = [ps[0:HC, 4 * n + 2:4 * n + 4, :] for n in range(2)]
    xc1, sq1, rstd1 = term, rz, [ez[n][:, 0, :] for n in range(2)]
    mean_bank1, var_bank1 = [ps[0:HC, 4 * n + 2, :] for n in range(2)], [ps[0:HC, 4 * n + 3, :] for n in range(2)]

    def pairs(eng, start, body):
        start()
        with eng.Fori(0, PAIRS - 1) as r:
            body(r, r + 1)
        body(PAIRS - 1, None)

    with ExitStack() as stack:
        G = semaphores(nc, stack, "weights ones_set wu_made wu_ready dsum_done dsum2_done init_done")
        S = semaphore_pair(nc, stack, LN_SEMS + " uss_made uz_made x2_made xss_done z_done sx2_done rows_made "
                           "dt_rows_made b_copied dt_copied bc_done dt_z bc_spread abs_done exp_done log_done relu_done "
                           "dt_done term_done gain_done y_done yz_done out_made s_done o_made x_done")
        M = semaphore_pair(nc, stack, LN_SEMS, "second_")
        with nc.Block() as block:
            @block.sync
            def _(sp):
                sp.dma_start(wt, t.inp["l1_w"]).then_inc(G.weights, 16)
                sp.dma_start(dtw, t.inp["l1_dtw"].rearrange("p (k c) -> p k c", k=K)).then_inc(G.weights, 16)
                sp.dma_start(pick, t.inp["pick"].rearrange("p (k c) -> p k c", k=K)).then_inc(G.weights, 16)
                sp.dma_start(ddp, t.inp["l2_d"]).then_inc(G.weights, 16)

            @block.tensor
            def _(pe):
                pe.wait_ge(G.weights, 64)
                for h in range(2):
                    for m in range(2):
                        mm = pe.matmul(ps[0:HC, h, 0:2 * C], win[:, m, h * HC:(h + 1) * HC], ssmin[:, m, :],
                                       start=m == 0, stop=m == 1)
                    mm.then_inc(G.wu_made, 1)
                pe.wait_ge(G.wu_ready, 2)

                def first_mean(r):
                    for n in range(2):
                        pe.wait_ge(S[n].relu_done, K * r)
                        ln_mean(pe, S[n], mean_bank1[n], w["mean"], chunk(xs, 2 * r + n))

                def first_variance(r):
                    for n in range(2):
                        ln_variance(pe, S[n], r, var_bank1[n], w["mean"], sq1[n])

                def start():
                    first_mean(0)
                    first_variance(0)

                def body(r, nxt):
                    for n in range(2):
                        pe.wait_ge(S[n].ln_out, r + 1)
                        pe.wait_ge(S[n].s_done, r)
                        conv192(pe, ps, (4 * n + 2, 4 * n + 3), wu, xn[n]).then_inc(S[n].uss_made, 1)
                        pe.wait_ge(S[n].x_done, r)
                        conv192(pe, ps, (4 * n, 4 * n + 1), wu[:, :, C:2 * C], xn[n]).then_inc(S[n].uz_made, 1)
                    for n in range(2):
                        pe.wait_ge(S[n].xss_done, r + 1)
                        conv192(pe, ps, (4 * n + 2, 4 * n + 3), wx2, xn[n]).then_inc(S[n].x2_made, 1)
                    for n in range(2):
                        pe.wait_ge(S[n].z_done, r + 1)
                        for bank, wm in ((0, xb), (1, xcw)):
                            for h in range(2):
                                m = pe.matmul(ps[0:K * DS1, 4 * n + bank, :], wm[:, h, :], xss[n][:, h, :],
                                              start=h == 0, stop=h == 1)
                        m.then_inc(S[n].rows_made, 1)
                        pe.wait_ge(S[n].sx2_done, r + 1)
                        for h in range(2):
                            m = pe.matmul(ps[0:K * DTR1, 4 * n + 2, :], xd[:, h, :], xss[n][:, h, :],
                                          start=h == 0, stop=h == 1)
                        m.then_inc(S[n].dt_rows_made, 1)
                    for k in range(K):
                        for n in range(2):
                            if k == 0:
                                pe.wait_ge(S[n].dt_copied, r + 1)
                            else:
                                pe.wait_ge(S[n].relu_done, K * r + k)
                                pe.wait_ge(S[n].abs_done, K * r + k)
                            for h in range(2):
                                m = pe.matmul(ps[0:HC, 4 * n + 2 + h, :], dtw[:, k, h * HC:(h + 1) * HC], rows_dt[n],
                                              start=True, stop=True)
                            m.then_inc(S[n].dt_z, 1)
                        for n in range(2):
                            if k == 0:
                                pe.wait_ge(S[n].bc_done, r + 1)
                            elif k >= 2:
                                pe.wait_ge(S[n].term_done, 2 * K * r + 2 * (k - 1))
                            pe.matmul(ps[0:HC, 4 * n + k % 2, :], pick[:, k, :], bc[n], start=True, stop=True)\
                              .then_inc(S[n].bc_spread, 1)
                    for n in range(2):
                        pe.wait_ge(S[n].y_done, r + 1)
                        ln_mean(pe, M[n], mean_bank[n], w["mean"], gain[n])
                    if nxt is not None:
                        first_mean(nxt)
                    for n in range(2):
                        ln_variance(pe, M[n], r, var_bank[n], w["mean"], sq[n])
                    if nxt is not None:
                        first_variance(nxt)
                    for n in range(2):
                        pe.wait_ge(S[n].yz_done, r + 1)
                        if nxt is not None:
                            pe.wait_ge(S[n].ln_centered, nxt + 1)
                            pe.wait_ge(S[n].ln_std, nxt + 1)
                        conv192(pe, ps, (4 * n + 2, 4 * n + 3), so, xc[n]).then_inc(S[n].out_made, 1)
                    for n in range(2):
                        pe.wait_ge(S[n].s_done, r + 1)
                        conv192(pe, ps, (4 * n, 4 * n + 1), wo, z[n]).then_inc(S[n].o_made, 1)

                pairs(pe, start, body)

            @block.gpsimd
            def _(pool):
                for n in range(2):
                    pool.memset(rows_dt[n], 1.0).then_inc(G.ones_set, 1)
                with pool.Fori(0, PAIRS) as r:
                    for k in range(1, K):
                        for n in range(2):
                            pool.wait_ge(S[n].term_done, 2 * K * r + 2 * (k + 1))
                            if k >= 2:
                                pool.wait_ge(S[n].gain_done, (K - 1) * r + k - 1)
                            pool.tensor_tensor(gain[n], gain[n], term[n], ALU.add).then_inc(S[n].gain_done, 1)

            @block.scalar
            def _(act):
                act.wait_ge(G.weights, 64)
                act.wait_ge(G.ones_set, 2)
                for h in range(2):
                    act.wait_ge(G.wu_made, h + 1)
                    act.activation(wu[:, h, :], ps[0:HC, h, 0:2 * C], ACT.Copy).then_inc(G.wu_ready, 1)
                act.preload_act_table_set("natural_log_exp_and_others")

                def first_square(r):
                    for n in range(2):
                        ln_square(act, S[n], r, xc1[n], sq1[n])

                def first_bias(r):
                    for n in range(2):
                        act.wait_ge(S[n].x2_made, r)
                        ln_bias(act, S[n], r, xc1[n], w["b"], xn[n])

                def start():
                    first_square(0)
                    ln_root(act, S, 0, var_bank1, rstd1, t.eps)
                    first_bias(0)

                def body(r, nxt):
                    for n in range(2):
                        act.wait_ge(S[n].uss_made, r + 1)
                        act.activation(xss[n], high[n], ACT.Silu).then_inc(S[n].xss_done, 1)
                        act.wait_ge(S[n].uz_made, r + 1)
                        act.wait_ge(S[n].o_made, r)
                        act.activation(z[n], low[n], ACT.Silu).then_inc(S[n].z_done, 1)
                    for n in range(2):
                        act.wait_ge(S[n].x2_made, r + 1)
                        act.activation(sx2[n], high[n], ACT.Silu).then_inc(S[n].sx2_done, 1)
                    act.preload_act_table_set("natural_log_exp_and_others")
                    for n in range(2):
                        act.wait_ge(S[n].rows_made, r + 1)
                        act.activation(rows_b[n], ps[0:K * DS1, 4 * n, :], ACT.Copy).then_inc(S[n].b_copied, 1)
                        act.wait_ge(S[n].dt_rows_made, r + 1)
                        act.activation(rows_dt[n][0:K * DTR1, :], ps[0:K * DTR1, 4 * n + 2, :], ACT.Copy).then_inc(S[n].dt_copied, 1)
                    for k in range(K):
                        for n in range(2):
                            act.wait_ge(S[n].dt_z, K * r + k + 1)
                            act.wait_ge(S[n].dt_done, K * r + k)
                            act.activation(ez[n], high[n], ACT.Abs).then_inc(S[n].abs_done, 1)
                        for n in range(2):
                            act.wait_ge(S[n].abs_done, K * r + k + 1)
                            act.activation(ez[n], ez[n], ACT.Exp, scale=-1.0).then_inc(S[n].exp_done, 1)
                        for n in range(2):
                            act.wait_ge(S[n].exp_done, K * r + k + 1)
                            act.activation(ez[n], ez[n], ACT.Ln, bias=1.0).then_inc(S[n].log_done, 1)
                    for n in range(2):
                        ln_square(act, M[n], r, xc[n], sq[n])
                    if nxt is not None:
                        first_square(nxt)
                    ln_root(act, M, r, var_bank, rstd, t.eps)
                    if nxt is not None:
                        ln_root(act, S, nxt, var_bank1, rstd1, t.eps)
                    for n in range(2):
                        ln_bias(act, M[n], r, xc[n], w["ob"], xc[n])
                    if nxt is not None:
                        first_bias(nxt)

                pairs(act, start, body)

            @block.vector
            def _(v):
                v.wait_ge(G.weights, 64)
                v.tensor_reduce(dsum, dd, AX.X, ALU.add).then_inc(G.dsum_done, 1)
                v.tensor_reduce(dsum2, ddp.rearrange("p (h k) -> p h k", h=2), AX.X, ALU.add).then_inc(G.dsum2_done, 1)
                v.wait_ge(G.dsum_done, 1)
                v.wait_ge(G.dsum2_done, 1)

                def first_centre(r):
                    for n in range(2):
                        ln_centre(v, S[n], r, mean_bank1[n], chunk(xs, 2 * r + n), xc1[n])

                def first_scale(r):
                    for n in range(2):
                        ln_scale(v, S[n], r, xc1[n], rstd1[n], w["g"])

                def start():
                    first_centre(0)
                    first_scale(0)

                def body(r, nxt):
                    for n in range(2):
                        v.wait_ge(S[n].b_copied, r + 1)
                        v.wait_ge(S[n].bc_spread, K * r)
                        v.tensor_tensor(bc[n], rows_b[n], ps[0:K * DS1, 4 * n + 1, :], ALU.mult).then_inc(S[n].bc_done, 1)
                    for k in range(K):
                        out = term if k else gain
                        for n in range(2):
                            v.wait_ge(S[n].abs_done, K * r + k + 1)
                            v.tensor_scalar(rz[n], high[n], 0.0, None, ALU.max).then_inc(S[n].relu_done, 1)
                        for n in range(2):
                            v.wait_ge(S[n].relu_done, K * r + k + 1)
                            v.wait_ge(S[n].log_done, K * r + k + 1)
                            if k >= 2:
                                v.wait_ge(S[n].gain_done, (K - 1) * r + k - 1)
                            v.tensor_tensor(out[n], rz[n], ez[n], ALU.add).then_inc(S[n].dt_done, 1)
                        for n in range(2):
                            v.wait_ge(S[n].dt_done, K * r + k + 1)
                            v.wait_ge(S[n].bc_spread, K * r + k + 1)
                            for h in range(2):
                                v.tensor_tensor(out[n][:, h, :], out[n][:, h, :], ps[0:HC, 4 * n + k % 2, :], ALU.mult)\
                                 .then_inc(S[n].term_done, 1)
                    for n in range(2):
                        v.wait_ge(S[n].gain_done, (K - 1) * (r + 1))
                        for h in range(2):
                            m = v.scalar_tensor_tensor(gain[n][:, h, :], gain[n][:, h, :], dsum[:, h:h + 1],
                                                       xss[n][:, h, :], ALU.add, ALU.mult)
                        m.then_inc(S[n].y_done, 1)
                    for n in range(2):
                        v.wait_ge(S[n].out_made, r)
                        ln_centre(v, M[n], r, mean_bank[n], gain[n], xc[n])
                    if nxt is not None:
                        first_centre(nxt)
                    for n in range(2):
                        ln_scale(v, M[n], r, xc[n], rstd[n], w["og"])
                    for n in range(2):
                        v.wait_ge(M[n].ln_out, r + 1)
                        v.tensor_tensor(xc[n], xc[n], z[n], ALU.mult).then_inc(S[n].yz_done, 1)
                    if nxt is not None:
                        first_scale(nxt)
                    for n in range(2):
                        v.wait_ge(S[n].out_made, r + 1)
                        v.wait_ge(S[n].yz_done, r + 1)
                        v.tensor_tensor(z[n], high[n], sx2[n], ALU.mult).then_inc(S[n].s_done, 1)
                    for n in range(2):
                        v.wait_ge(S[n].o_made, r + 1)
                        v.tensor_tensor(chunk(xs, 2 * r + n), chunk(xs, 2 * r + n), low[n], ALU.add).then_inc(S[n].x_done, 1)

                pairs(v, start, body)
                for n in range(2):
                    v.wait_ge(S[n].x_done, PAIRS)
                for h in range(2):
                    v.tensor_scalar(ys[:, h, :], xs[:, h, :], dsum2[:, h:h + 1], None, ALU.mult).then_inc(G.init_done, 1)
        end_phase(nc, S[0] + S[1] + M[0] + M[1] + G)


def layer3_first(nc, t):
    cv = Carver(t.arena)
    xc64 = cv.take(CB, L)
    wt, wt2 = cv.take(HC, L3_N), cv.take(128, L3B_N)
    w = {n: wt[:, a:e] for n, (a, e) in L3_W.items()}
    w1 = w["w1"].rearrange("p (h o) -> p h o", h=2)
    b1 = wt2[0:CB, slice(*L3B_W["b1"])]
    xc, sq, rstd = take_pair(cv, 2, QUAD), take_pair(cv, 2, QUAD), take_pair(cv, 1, QUAD)
    ys, ps = halves(t.ys[0:HC, :], L), t.ps
    mean_bank, var_bank = ([ps[0:HC, 2 * n + m, :] for n in range(QUAD)] for m in range(2))
    with ExitStack() as stack:
        G = semaphores(nc, stack, "weights")
        S = semaphore_pair(nc, stack, LN_SEMS + " conv_made conv_done", ways=QUAD)
        with nc.Block() as block:
            @block.sync
            def _(sp):
                sp.dma_start(wt, t.inp["l3_w"]).then_inc(G.weights, 16)
                sp.dma_start(wt2, t.inp["l3b_w"]).then_inc(G.weights, 16)

            @block.tensor
            def _(pe):
                pe.wait_ge(G.weights, 32)
                with pe.Fori(0, NCH // QUAD) as r:
                    for n in range(QUAD):
                        pe.wait_ge(S[n].conv_done, r)
                        ln_mean(pe, S[n], mean_bank[n], w["mean"], chunk(ys, QUAD * r + n))
                    for n in range(QUAD):
                        pe.wait_ge(S[n].ln_std, r)
                        ln_variance(pe, S[n], r, var_bank[n], w["mean"], sq[n])
                    for n in range(QUAD):
                        pe.wait_ge(S[n].ln_out, r + 1)
                        for h in range(2):
                            m = pe.matmul(ps[:, 2 * n, :], w1[:, h, :], ys[:, h, bass.ds((QUAD * r + n) * T, T)],
                                          start=h == 0, stop=h == 1)
                        m.then_inc(S[n].conv_made, 1)

            @block.scalar
            def _(act):
                act.wait_ge(G.weights, 32)
                with act.Fori(0, NCH // QUAD) as r:
                    for n in range(QUAD):
                        ln_square(act, S[n], r, xc[n], sq[n])
                    ln_root(act, S, r, var_bank, rstd, t.eps)
                    for n in range(QUAD):
                        ln_bias(act, S[n], r, xc[n], w["b"], chunk(ys, QUAD * r + n))
                    for n in range(QUAD):
                        act.wait_ge(S[n].conv_made, r + 1)
                        act.activation(xc64[:, bass.ds((QUAD * r + n) * T, T)], ps[0:CB, 2 * n, :], ACT.Identity, bias=b1)\
                           .then_inc(S[n].conv_done, 1)

            @block.vector
            def _(v):
                v.wait_ge(G.weights, 32)
                with v.Fori(0, NCH // QUAD) as r:
                    for n in range(QUAD):
                        v.wait_ge(S[n].ln_out, r)
                        ln_centre(v, S[n], r, mean_bank[n], chunk(ys, QUAD * r + n), xc[n])
                    for n in range(QUAD):
                        ln_scale(v, S[n], r, xc[n], rstd[n], w["g"])
        end_phase(nc, S[0] + S[1] + S[2] + S[3] + G)


def layer3_windows(nc, t, n_win):
    nw, step, k = WINS[n_win]
    kk, nn = k * k, nw * nw
    P2 = nn // 2
    KP = k + 2
    LU, LP = P2 * kk, P2 * KP * KP
    cv = Carver(t.arena)
    xc = cv.take(CB, L)
    fold12 = cv.take(CB, L)
    at = cv.at
    unf = cv.take(CB, kk * nn).rearrange("p (a b m n) -> p a b m n", a=k, b=k, m=nw)
    cv.at = at
    pad = cv.take(128, LP)
    acc = cv.take(128, LP)
    cv.at = at + 17424
    uc = cv.take(128, LU)
    wt2 = cv.take(128, L3B_N)
    se2 = cv.take(8, 128)
    icnt = xc if nw == 12 else None
    ysum, hid, att = cv.take(128, P2), cv.take(8, P2), cv.take(128, P2)
    w = {n: wt2[:, a:e] for n, (a, e) in L3B_W.items()}
    out = (t.xs[0:CB, 0:L], t.xs[0:CB, L:2 * L], fold12)[n_win]
    pad4 = pad.rearrange("p (n y x) -> p n y x", n=P2, y=KP)
    acc4 = acc.rearrange("p (n y x) -> p n y x", n=P2, y=KP)
    uc4 = uc.rearrange("p (n y x) -> p n y x", n=P2, y=k)
    uc3 = uc.rearrange("p (n r) -> p n r", n=P2)
    ps = t.ps
    total = CB * kk * nn
    flat = t.fold_scratch[0:total]
    as_unf = flat.rearrange("(c j) -> c j", c=CB)
    as_patch = flat.rearrange("(a n c r) -> a c n r", a=2, c=CB, r=kk)
    flat2 = t.fold_scratch2[0:total]
    as_unf2 = flat2.rearrange("(c j) -> c j", c=CB)
    as_patch2 = flat2.rearrange("(a n c r) -> a c n r", a=2, c=CB, r=kk)
    unf2 = unf.rearrange("p a b m n -> p (a b m n)")
    spans = [(a, min(a + T, LU)) for a in range(0, LU, T)]

    rows_of = ([a for a in range(k) if a % 5 < 2], [a for a in range(k) if 2 <= a % 5 < 4], [a for a in range(k) if a % 5 == 4])

    cuts = (0, P2 * 2 // 5, P2 * 4 // 5, P2)
    pads = [slice(cuts[n], cuts[n + 1]) for n in range(3)]

    def window_rows(a):
        rows = as_rows(xc)[:, a:a + step * (nw - 1) + 1:step, :]
        partition, lines, _ = rows.ap
        return bass.AP(tensor=rows.tensor, offset=rows.offset, ap=[partition, [1, k], lines, [step, nw]])

    with ExitStack() as stack:
        S = semaphores(nc, stack, "weights counts unfolded0 unfolded1 unfolded2 stored patches cleared padded0 padded1 padded2 conv_made conv_done summed hid_made hid_done "
                       "att_made att_done out_cleared scaled taps joined stored2 unf_loaded folded")
        with nc.Block() as block:
            @block.sync
            def _(sp):
                sp.dma_start(wt2, t.inp["l3b_w"]).then_inc(S.weights, 16)
                sp.dma_start(se2, t.inp["se2"]).then_inc(S.weights, 16)
                for n, done in enumerate((S.unfolded0, S.unfolded1, S.unfolded2)):
                    sp.wait_ge(done, len(rows_of[n]))
                if icnt is not None:
                    sp.dma_start(icnt, t.inp["inv_count"]).then_inc(S.counts, 16)
                sp.dma_start(as_unf, unf2).then_inc(S.stored, 16)
                sp.wait_ge(S.stored, 16)
                for a in range(2):
                    sp.dma_start(uc3[a * CB:(a + 1) * CB], as_patch[a]).then_inc(S.patches, 16)
                sp.wait_ge(S.joined, 1)
                for a in range(2):
                    sp.dma_start(as_patch2[a], uc3[a * CB:(a + 1) * CB]).then_inc(S.stored2, 16)
                sp.wait_ge(S.stored2, 32)
                sp.dma_start(unf2, as_unf2).then_inc(S.unf_loaded, 16)
                sp.wait_ge(S.unf_loaded, 16)

            @block.gpsimd
            def _(pool):
                for a in rows_of[2]:
                    pool.tensor_copy(unf[:, a], window_rows(a)).then_inc(S.unfolded2, 1)
                pool.wait_ge(S.stored, 16)
                pool.memset(pad, 0.0).then_inc(S.cleared, 1)
                pool.wait_ge(S.cleared, 1)
                pool.wait_ge(S.patches, 32)
                pool.tensor_copy(pad4[:, pads[2], 1:k + 1, 1:k + 1], uc4[:, pads[2]]).then_inc(S.padded2, 1)
                if step < k:
                    pool.memset(out, 0.0).then_inc(S.out_cleared, 1)
                pool.wait_ge(S.att_done, 1)
                pool.tensor_tensor(uc3, uc3, att.unsqueeze(2).broadcast_to([128, P2, kk]), ALU.mult).then_inc(S.scaled, 1)

            @block.tensor
            def _(pe):
                pe.wait_ge(S.weights, 32)
                pe.wait_ge(S.patches, 32)
                for n, (a, e) in enumerate(spans):
                    if n >= 4:
                        pe.wait_ge(S.conv_done, n - 3)
                    pe.matmul(ps[:, n % 4, 0:e - a], w["w2"], uc[:, a:e], start=True, stop=True).then_inc(S.conv_made, 1)
                pe.wait_ge(S.summed, 1)
                pe.matmul(ps[0:8, 4, 0:P2], w["se1"], ysum, start=True, stop=True).then_inc(S.hid_made, 1)
                pe.wait_ge(S.hid_done, 1)
                pe.matmul(ps[:, 5, 0:P2], se2, hid, start=True, stop=True).then_inc(S.att_made, 1)

            @block.scalar
            def _(act):
                for a in rows_of[1]:
                    act.activation(unf[:, a], window_rows(a), ACT.Copy).then_inc(S.unfolded1, 1)
                act.wait_ge(S.cleared, 1)
                act.wait_ge(S.patches, 32)
                act.activation(pad4[:, pads[1], 1:k + 1, 1:k + 1], uc4[:, pads[1]], ACT.Copy).then_inc(S.padded1, 1)
                for done in (S.padded0, S.padded1, S.padded2):
                    act.wait_ge(done, 1)
                for n, (a, e) in enumerate(spans):
                    act.wait_ge(S.conv_made, n + 1)
                    act.activation(uc[:, a:e], ps[:, n % 4, 0:e - a], ACT.Identity, bias=w["b2"]).then_inc(S.conv_done, 1)
                act.wait_ge(S.hid_made, 1)
                act.activation(hid, ps[0:8, 4, 0:P2], ACT.Relu, scale=1.0 / kk).then_inc(S.hid_done, 1)
                act.wait_ge(S.att_made, 1)
                act.activation(att, ps[:, 5, 0:P2], ACT.Sigmoid).then_inc(S.att_done, 1)

            @block.vector
            def _(v):
                for a in rows_of[0]:
                    v.tensor_copy(unf[:, a], window_rows(a)).then_inc(S.unfolded0, 1)
                v.wait_ge(S.weights, 32)
                v.wait_ge(S.cleared, 1)
                v.wait_ge(S.patches, 32)
                v.tensor_copy(pad4[:, pads[0], 1:k + 1, 1:k + 1], uc4[:, pads[0]]).then_inc(S.padded0, 1)
                for done in (S.padded0, S.padded1, S.padded2):
                    v.wait_ge(done, 1)
                lo, n = KP + 1, LP - 2 * KP - 2
                for j in range(9):
                    off = lo + (j // 3 - 1) * KP + j % 3 - 1
                    src, dst, tap = pad[:, off:off + n], acc[:, lo:lo + n], w["dw"][:, j:j + 1]
                    if j == 6:
                        v.wait_ge(S.conv_done, len(spans))
                        v.tensor_reduce(ysum, uc3, AX.X, ALU.add).then_inc(S.summed, 1)
                    if j == 0:
                        v.tensor_scalar(dst, src, tap, w["dwb"], ALU.mult, ALU.add).then_inc(S.taps, 1)
                    else:
                        v.wait_ge(S.taps, j)
                        v.scalar_tensor_tensor(dst, src, tap, dst, ALU.mult, ALU.add).then_inc(S.taps, 1)
                v.wait_ge(S.scaled, 1)
                v.wait_ge(S.taps, 9)
                v.tensor_tensor(uc4, uc4, acc4[:, :, 1:k + 1, 1:k + 1], ALU.add).then_inc(S.joined, 1)
                v.wait_ge(S.unf_loaded, 16)
                img = as_rows(out)
                done = 0
                if step == k:
                    for a in range(k):
                        v.tensor_copy(img[:, a::k, :].rearrange("p m (n c) -> p c m n", c=k), unf[:, a]).then_inc(S.folded, 1)
                else:
                    v.wait_ge(S.out_cleared, 1)
                    for a in range(k):
                        for c0, c1 in ((0, step), (step, k)):
                            dst = img[:, a:a + step * (nw - 1) + 1:step, c0 // step * step:]
                            x0 = c0 // step * step
                            rows = img[:, a:a + step * (nw - 1) + 1:step, x0:x0 + step * nw] if x0 + step * nw <= W else None
                            if rows is not None:
                                dst = rows.rearrange("p m (n c) -> p m n c", c=step)[:, :, :, 0:c1 - c0]
                                src = unf[:, a, c0:c1].rearrange("p c m n -> p m n c")
                                if done:
                                    v.wait_ge(S.folded, done)
                                v.tensor_tensor(dst, dst, src, ALU.add).then_inc(S.folded, 1)
                                done += 1
                            else:
                                dst = img[:, a:a + step * (nw - 1) + 1:step, x0:x0 + step * (nw - 1)]
                                dst = dst.rearrange("p m (n c) -> p m n c", c=step)[:, :, :, 0:c1 - c0]
                                src = unf[:, a, c0:c1, :, 0:nw - 1].rearrange("p c m n -> p m n c")
                                if done:
                                    v.wait_ge(S.folded, done)
                                v.tensor_tensor(dst, dst, src, ALU.add).then_inc(S.folded, 1)
                                x1 = x0 + step * (nw - 1)
                                dst = img[:, a:a + step * (nw - 1) + 1:step, x1:x1 + c1 - c0]
                                src = unf[:, a, c0:c1, :, nw - 1].rearrange("p c m -> p m c")
                                v.wait_ge(S.folded, done + 1)
                                v.tensor_tensor(dst, dst, src, ALU.add).then_inc(S.folded, 1)
                                done += 2
                    v.wait_ge(S.counts, 16)
                    v.wait_ge(S.folded, done)
                    v.tensor_tensor(out, out, icnt, ALU.mult).then_inc(S.folded, 1)
        end_phase(nc, S)


def layer3_last(nc, t, b):
    cv = Carver(t.arena)
    cv.take(CB, L)
    fold12 = cv.take(CB, L)
    wt, wt2 = cv.take(HC, L3_N), cv.take(128, L3B_N)
    b3 = wt[:, slice(*L3_W["b3"])]
    w3 = wt2[:, slice(*L3B_W["w3"])].rearrange("p (n o) -> p n o", n=3)
    res = cv.take(HC, 4 * T).rearrange("p (h n t) -> p h n t", h=2, n=2)
    ps = t.ps
    src = (t.ys[:, 0:L], t.ys[:, L:2 * L], t.xs[:, 0:L])
    out = t.out[b].rearrange("(h p) l -> p h l", h=2)
    with ExitStack() as stack:
        S = semaphores(nc, stack, "weights moved made0 made1 biased0 biased1 stored0 stored1")
        made, biased, stored = (S.made0, S.made1), (S.biased0, S.biased1), (S.stored0, S.stored1)
        with nc.Block() as block:
            @block.sync
            def _(sp):
                sp.dma_start(wt, t.inp["l3_w"]).then_inc(S.weights, 16)
                sp.dma_start(wt2, t.inp["l3b_w"]).then_inc(S.weights, 16)
                for h in range(2):
                    sp.dma_start(t.ys[HC:128, h * L:(h + 1) * L], fold12[32 * h:32 * h + 32, :]).then_inc(S.moved, 16)
                sp.dma_start(t.xs[CB:2 * CB, 0:L], t.xs[0:CB, L:2 * L]).then_inc(S.moved, 16)
                with sp.Fori(0, NCH // 2) as i:
                    for n in range(2):
                        sp.wait_ge(biased[n], i + 1)
                        sp.dma_start(out[:, :, bass.ds((2 * i + n) * T, T)], res[:, :, n, :]).then_inc(stored[n], 16)
                for n in range(2):
                    sp.wait_ge(stored[n], 16 * (NCH // 2))

            @block.tensor
            def _(pe):
                pe.wait_ge(S.weights, 32)
                pe.wait_ge(S.moved, 48)
                with pe.Fori(0, NCH // 2) as i:
                    for n in range(2):
                        at = bass.ds((2 * i + n) * T, T)
                        pe.wait_ge(biased[n], i)
                        for o in range(2):
                            bank = ps[0:HC, 2 * n + o, :]
                            cut = slice(o * HC, (o + 1) * HC)
                            for f in range(3):
                                m = pe.matmul(bank, w3[:, f, cut], src[f][:, at], start=f == 0, stop=f == 2)
                        m.then_inc(made[n], 1)

            @block.scalar
            def _(act):
                with act.Fori(0, NCH // 2) as i:
                    for n in range(2):
                        act.wait_ge(made[n], i + 1)
                        act.wait_ge(stored[n], 16 * i)
                        for o in range(2):
                            m = act.activation(res[:, o, n, :], ps[0:HC, 2 * n + o, :], ACT.Identity, bias=b3[:, o:o + 1])
                        m.then_inc(biased[n], 1)
        end_phase(nc, S)


class Tensors:
    pass


def build(nc, d, out):
    t = Tensors()
    t.inp, t.out = d, out
    with ExitStack() as stack:
        sb = lambda n, s, dt: stack.enter_context(nc.sbuf_tensor(n, s, dt))
        t.xs = sb("xs", [128, 2 * L], F32)
        t.ys = sb("ys", [128, 2 * L], F32)
        sel = sb("sel", [HC, 4, 128], BF16)
        gather = sb("gather", [128, (2 * NGH - 1) * CG], F32)
        t.arena = sb("arena", [128, 36350], F32)
        t.ps = stack.enter_context(nc.psum_tensor("ps", [128, 8, T], F32))
        t.gate_scratch = nc.dram_tensor("gate_scratch", (HC, 2, L), F32).ap()
        t.fold_scratch = nc.dram_tensor("fold_scratch", (CB * 81 * 144,), F32).ap()
        t.fold_scratch2 = nc.dram_tensor("fold_scratch2", (CB * 81 * 144,), F32).ap()
        t.sel, t.gather = sel, gather
        t.eps = sb("eps", [128, 1], F32)
        S = semaphores(nc, stack, "constants eps_set")
        with nc.Block() as block:
            @block.gpsimd
            def _(pool):
                pool.memset(t.eps[:, :], EPS).then_inc(S.eps_set, 1)

            @block.sync
            def _(sp):
                sp.dma_start(sel[:, :, :], t.inp["sel_c"]).then_inc(S.constants, 16)
                sp.dma_start(gather[:, :], t.inp["gather_c"]).then_inc(S.constants, 16)
                sp.wait_ge(S.constants, 32)
        with nc.Fori(0, NIMG) as b:
            layer0_before(nc, t, b)
            scan_layer(nc, t, 12, t.inp["s0_w"], t.inp["s0_r"], t.inp["s0_a"], (True, False, True, False))
            layer0_after(nc, t, b)
            layer1(nc, t)
            scan_layer(nc, t, 6, t.inp["s2_w"], t.inp["s2_r"], t.inp["s2_a"], (False, True, False, True))
            layer3_first(nc, t)
            for n in range(3):
                layer3_windows(nc, t, n)
            layer3_last(nc, t, b)


def by_half(w):
    w = np.asarray(w)
    return np.ascontiguousarray(w.reshape(2, HC, -1).transpose(1, 0, 2)).reshape(HC, -1)


def host_layouts(a):
    a = {k: np.asarray(v) for k, v in a.items()}
    f = np.float32
    mean = np.full((HC, HC), 1.0 / C, f)
    d = {"x_in": a["x"].reshape(NIMG, C, L)}

    def put(name, spec, parts):
        assert [n for n, _ in spec.items()] == list(parts), name
        d[name] = np.concatenate([p.reshape(p.shape[0], -1) for p in parts.values()], axis=1)
        assert all(p.size // p.shape[0] == spec[n][1] - spec[n][0] for n, p in parts.items())

    put("pre_w", PRE_W, {
        "p1": by_half(a["L0_conv_p1_w"].T), "p2": by_half(a["L0_conv_p2in_w"].T),
        "g": by_half(a["L0_conv_ln_g"]), "b": by_half(a["L0_conv_ln_b"]),
        "p1b": by_half(a["L0_conv_p1_b"]), "p2b": by_half(a["L0_conv_p2in_b"]),
        "dw": by_half(a["L0_conv_dw_w"].reshape(C, 9)), "dwb": by_half(a["L0_conv_dw_b"]),
        "D": by_half(a["L0_conv_Dp"].T), "mean": mean})
    for s, xp, dp, db, al, rank in (("s0", "L0_conv_x_proj_w", "L0_conv_dt_proj_w", "L0_conv_dt_proj_b", "L0_conv_A_log", 12),
                                    ("s2", "L2_conv_x_proj_weight", "L2_conv_dt_projs_weight", "L2_conv_dt_projs_bias",
                                     "L2_conv_A_logs", 6)):
        w = a[xp]
        rep = {}
        for name, at in (("wb", rank), ("wc", rank + NS)):
            rows = np.tile(w[:, at:at + NS], (1, CG, 1))
            rep[name] = rows.reshape(K, 128, 2, HC).transpose(3, 0, 2, 1)
        put(s + "_w", SCAN_W, {**rep, "dtb": by_half(a[db].T)})
        d[s + "_r"] = np.stack([w[:, :rank].transpose(1, 0, 2), a[dp].transpose(2, 0, 1)], axis=1).reshape(rank, -1)
        al = a[al].reshape(K, NG, CG * NS)
        d[s + "_a"] = np.ascontiguousarray(al.transpose(2, 0, 1)).reshape(128, -1)
    xp = a["L1_conv_x_proj_w"]
    win, ca1 = a["L1_conv_w_in"], a["L0_conv_ca_w1"]
    rows = lambda w: by_half(w.reshape(-1, C).T)
    put("l1_w", L1_W, {
        "win": by_half(win[:C]), "ssmin": by_half(a["L1_conv_ssm_in_w"].T), "wx2": by_half(win[C:].T),
        "xb": rows(xp[:, DTR1:DTR1 + DS1]), "xc": rows(xp[:, DTR1 + DS1:]), "xd": rows(xp[:, :DTR1]),
        "D": by_half(a["L1_conv_Ds"].reshape(K, C).T),
        "g": by_half(a["L1_conv_norm_w"]), "b": by_half(a["L1_conv_norm_b"]),
        "og": by_half(a["L1_conv_out_norm_w"]), "ob": by_half(a["L1_conv_out_norm_b"]),
        "so": by_half(a["L1_conv_ssm_out_w"].T), "wo": by_half(a["L1_conv_w_out"].T), "mean": mean,
        "l0g": by_half(a["L0_conv_on_g"]), "l0b": by_half(a["L0_conv_on_b"]), "ca1": by_half(ca1.T)})
    dtw = np.zeros((K * DTR1 + 1, K, C), f)
    dtw[-1] = a["L1_conv_dt_b"]
    pick = np.zeros((K, DS1, K, HC), f)
    for k in range(K):
        dtw[k * DTR1:(k + 1) * DTR1, k] = a["L1_conv_dt_w"][k].T
        pick[k, :, k] = 1.0
    d["l1_dtw"], d["pick"] = dtw.reshape(K * DTR1 + 1, -1), pick.reshape(K * DS1, -1)
    d["l2_d"] = by_half(a["L2_conv_Ds"].reshape(K, C).T)
    d["ca2"] = np.ascontiguousarray(a["L0_conv_ca_w2"].T)
    cab = np.zeros((HC, 3), f)
    cab[:, 0:2] = by_half(a["L0_conv_ca_b2"])
    cab[0:12, 2] = a["L0_conv_ca_b1"]
    d["cab"] = cab
    w3 = a["L3_conv_w3"]
    put("l3_w", L3_W, {"w1": by_half(np.concatenate([a["L3_conv_w1"].T] * 2, axis=1)), "b3": by_half(a["L3_conv_b3"]),
                       "g": by_half(a["L2_conv_ln_g"].reshape(C)), "b": by_half(a["L2_conv_ln_b"].reshape(C)), "mean": mean})
    w2 = np.zeros((2, CB, 2, CB), f)
    se1 = np.zeros((2, CB, 2, 4), f)
    se2 = np.zeros((2, 4, 2, CB), f)
    for h in range(2):
        w2[h, :, h] = a["L3_conv_w2"].T
        se1[h, :, h] = a["L3_conv_wse1"].T
        se2[h, :, h] = a["L3_conv_wse2"].T
    with_x = [np.concatenate([w3.T[h * HC:(h + 1) * HC], w3.T[2 * CB + 32 * h:2 * CB + 32 * (h + 1)]]) for h in range(2)]
    two = lambda v: np.concatenate([v.reshape(CB, -1)] * 2, axis=0)
    put("l3b_w", L3B_W, {"w2": w2.reshape(128, 128), "se1": se1.reshape(128, 8), "b2": two(a["L3_conv_b2"]),
                         "dw": two(a["L3_conv_wpos"]), "dwb": two(a["L3_conv_bpos"]),
                         "w3": np.stack([*with_x, w3.T[0:2 * CB]], axis=1),
                         "b1": two(a["L3_conv_b1"])})
    d["se2"] = se2.reshape(8, 128)
    bf = mybir.dt.np(BF16)
    sel = np.zeros((3, 4, CG, 4, CG, NS), f)
    for g in range(4):
        for c in range(CG):
            sel[:, g, c, g, c] = 1.0
    d["sel_c"] = sel.reshape(HC, 4, 128).astype(bf)
    gather = np.zeros((CG, NS, (2 * NGH - 1) * CG), f)
    for c in range(CG):
        gather[c, :, (NGH - 1) * CG + c] = 1.0
    d["gather_c"] = gather.reshape(128, -1)
    nw, step, k = WINS[2]
    n = np.zeros(H, f)
    for m in range(nw):
        n[m * step:m * step + k] += 1.0
    d["inv_count"] = np.broadcast_to((1.0 / np.outer(n, n)).reshape(1, L), (CB, L)).astype(f)
    return {n: np.ascontiguousarray(v) for n, v in d.items()}


def kernel(**inputs):
    import concourse.bacc as bacc
    from concourse.bass_utils import run_bass_kernel_spmd

    nc = bacc.Bacc("TRN2", target_bir_lowering=False, num_devices=1)
    arrays = host_layouts(inputs)
    aps = {n: nc.dram_tensor(n, v.shape, mybir.dt.from_np(v.dtype), kind="ExternalInput").ap()
           for n, v in arrays.items()}
    out = nc.dram_tensor("out", (NIMG, C, L), F32, kind="ExternalOutput").ap()
    build(nc, aps, out)
    r = run_bass_kernel_spmd(nc, [arrays], core_ids=[0])
    return r.results[0]["out"].reshape(NIMG, C, H, W)
```
